# Optimizing a Trainium2 kernel written in Bass

```python
import numpy as np
import jax
import jax.numpy as jnp

def _softmax(x, axis=-1):
    return jax.nn.softmax(x, axis=axis)

def _gelu(x):
    return jax.nn.gelu(x, approximate=True)

def _silu(x):
    return jax.nn.silu(x)

def _sigmoid(x):
    return jax.nn.sigmoid(x)

def _layernorm(x, axis=-1, eps=1e-05):
    m = jnp.mean(x, axis=axis, keepdims=True)
    v = jnp.var(x, axis=axis, keepdims=True)
    return (x - m) / jnp.sqrt(v + eps)

def _scatter_add(tgt, idx, src, axis=0):
    return tgt.at[idx].add(src)

def _segment_sum(src, seg, n):
    return jax.ops.segment_sum(src, seg, n)
kernel_name = 'mk_gnn_resnorm_d4_gnn_r8_24876e'

def setup_inputs(seed: int=0):
    np.random.seed(seed)
    _w = jnp.asarray

    def _rec_inputs():
        import jax
        import jax.numpy as jnp
        _gk = jax.random.key(seed)
        x = -0.0009044 + 1 * jax.random.normal(jax.random.fold_in(_gk, 1), (12500, 32), jnp.float32)
        src = jax.random.randint(jax.random.fold_in(_gk, 2), (200000,), 0, 12500, jnp.int32)
        dst = jax.random.randint(jax.random.fold_in(_gk, 3), (200000,), 0, 12500, jnp.int32)
        _o = jnp.argsort(dst, stable=True)
        src = src[_o]
        dst = dst[_o]
        edge_attr_16 = 0.000312547 + 1.00004 * jax.random.normal(jax.random.fold_in(_gk, 12), (200000, 16), jnp.float32)
        edge_attr_32 = 0.000189758 + 1.00013 * jax.random.normal(jax.random.fold_in(_gk, 13), (200000, 32), jnp.float32)
        return (x, src, dst, edge_attr_16, edge_attr_32)
    x, src, dst, edge_attr_16, edge_attr_32 = _rec_inputs()

    def _L0_gnn_setup():
        import jax, jax.numpy as jnp
        import numpy as np
        N_NODES = 6250
        DEG = 16
        N_HEAD = 4
        F_IN = 32
        F_OUT = 32
        key = jax.random.key(seed)
        k_h, k_w, k_fw, k_fb = jax.random.split(key, 4)
        h = jax.random.normal(k_h, (N_NODES, F_IN), dtype=jnp.float32)
        src = jnp.repeat(jnp.arange(N_NODES, dtype=jnp.int64), DEG)
        offs = (jnp.arange(DEG, dtype=jnp.int64) + 1) * 97
        dst = (src.reshape(N_NODES, DEG) + offs[None, :]).reshape(-1) % N_NODES
        edge_index = jnp.stack([src, dst], axis=0)
        gain = 1.414
        bound_w = gain * np.sqrt(6.0 / (F_IN + F_OUT))
        w = jax.random.uniform(k_w, (N_HEAD, F_IN, F_OUT), jnp.float32, -bound_w, bound_w)
        bound_fc = np.sqrt(1.0 / (2 * F_OUT))
        fc_w = jax.random.uniform(k_fw, (1, 2 * F_OUT), jnp.float32, -bound_fc, bound_fc)
        fc_b = jax.random.uniform(k_fb, (1,), jnp.float32, -bound_fc, bound_fc)
        bias = jnp.zeros((F_OUT,), jnp.float32)
        return {'h': h, 'edge_index': edge_index, 'w': w, 'fc_w': fc_w, 'fc_b': fc_b, 'bias': bias}
    _L0_gnn_all = _L0_gnn_setup()
    _L0_gnn_in = {k: v for k, v in _L0_gnn_all.items() if k in ('w', 'fc_w', 'fc_b', 'bias')}
    del _L0_gnn_all

    def _L1_gnn_setup():
        import jax, jax.numpy as jnp
        import numpy as np
        N_NODES = 12500
        N_EDGES = 312500
        IN_CH = 32
        HID = 16
        OUT_CH = 32

        def _gin_conv(x, src, dst, W_a, b_a, W_b, b_b):
            agg = jax.ops.segment_sum(x[src], dst, num_segments=x.shape[0])
            h = x + agg
            h = jnp.maximum(h @ W_a + b_a, 0.0)
            return h @ W_b + b_b
        key = jax.random.key(seed)
        ks = jax.random.split(key, 10)
        x = jax.random.normal(ks[0], (N_NODES, IN_CH), dtype=jnp.float32)
        edge_index = jax.random.randint(ks[1], (2, N_EDGES), 0, N_NODES, dtype=jnp.int64)
        W1 = jax.random.normal(ks[2], (IN_CH, HID), dtype=jnp.float32) / np.sqrt(IN_CH)
        b1 = jnp.zeros((HID,), dtype=jnp.float32)
        W2 = jax.random.normal(ks[3], (HID, OUT_CH), dtype=jnp.float32) / np.sqrt(HID)
        b2 = jnp.zeros((OUT_CH,), dtype=jnp.float32)
        W3 = jax.random.normal(ks[4], (OUT_CH, HID), dtype=jnp.float32) / np.sqrt(OUT_CH)
        b3 = jnp.zeros((HID,), dtype=jnp.float32)
        W4 = jax.random.normal(ks[5], (HID, OUT_CH), dtype=jnp.float32) / np.sqrt(HID)
        b4 = jnp.zeros((OUT_CH,), dtype=jnp.float32)
        return {'x': x, 'edge_index': edge_index, 'W1': W1, 'b1': b1, 'W2': W2, 'b2': b2, 'W3': W3, 'b3': b3, 'W4': W4, 'b4': b4}
    _L1_gnn_all = _L1_gnn_setup()
    _L1_gnn_in = {k: v for k, v in _L1_gnn_all.items() if k in ('W1', 'b1', 'W2', 'b2', 'W3', 'b3', 'W4', 'b4')}
    del _L1_gnn_all

    def _L2_gnn_setup():
        import jax, jax.numpy as jnp
        import numpy as np
        N_NODES = 12500
        N_EDGES = 125000
        IN_CH = 32
        EDGE_CH = 16
        OUT_CH = 32
        D_CAT = 2 * IN_CH + EDGE_CH
        D_MID = 56
        key = jax.random.key(seed)
        ks = jax.random.split(key, 8)
        x = jax.random.normal(ks[0], (N_NODES, IN_CH), dtype=jnp.float32)
        edge_index = jax.random.randint(ks[1], (2, N_EDGES), 0, N_NODES, dtype=jnp.int64)
        edge_attr = jax.random.normal(ks[2], (N_EDGES, EDGE_CH), dtype=jnp.float32)
        W1 = jax.random.normal(ks[3], (D_CAT, D_MID), dtype=jnp.float32) / np.sqrt(D_CAT).astype(np.float32)
        b1 = jnp.zeros((D_MID,), dtype=jnp.float32)
        W2 = jax.random.normal(ks[4], (D_MID, OUT_CH), dtype=jnp.float32) / np.sqrt(D_MID).astype(np.float32)
        b2 = jnp.zeros((OUT_CH,), dtype=jnp.float32)
        return {'x': x, 'edge_index': edge_index, 'edge_attr': edge_attr, 'W1': W1, 'b1': b1, 'W2': W2, 'b2': b2}
    _L2_gnn_all = _L2_gnn_setup()
    _L2_gnn_in = {k: v for k, v in _L2_gnn_all.items() if k in ('W1', 'b1', 'W2', 'b2')}
    del _L2_gnn_all

    def _L3_gnn_setup():
        import jax, jax.numpy as jnp
        import numpy as np
        N_VERTICES = 6250
        N_EDGES = 200000
        D_FEAT = 32
        key = jax.random.key(seed)
        k1, k2, k3, k4 = jax.random.split(key, 4)
        vertex_attr = jax.random.normal(k1, (N_VERTICES, D_FEAT), dtype=jnp.float32)
        edgeij_pair = jax.random.randint(k2, (2, N_EDGES), 0, N_VERTICES, dtype=jnp.int64)
        edge_attr = jax.random.normal(k3, (N_EDGES, D_FEAT), dtype=jnp.float32)
        g = jax.random.normal(k4, (1, D_FEAT), dtype=jnp.float32)
        batch = jnp.zeros((N_VERTICES,), dtype=jnp.int64)
        return {'vertex_attr': vertex_attr, 'edgeij_pair': edgeij_pair, 'edge_attr': edge_attr, 'g': g, 'batch': batch}
    _L3_gnn_all = _L3_gnn_setup()
    _L3_gnn_in = {k: v for k, v in _L3_gnn_all.items() if k in ('g',)}
    del _L3_gnn_all
    return {'x': x, 'src': src, 'dst': dst, 'edge_attr_16': edge_attr_16, 'edge_attr_32': edge_attr_32, 'L0_gnn_w': _L0_gnn_in['w'], 'L0_gnn_fc_w': _L0_gnn_in['fc_w'], 'L0_gnn_fc_b': _L0_gnn_in['fc_b'], 'L0_gnn_bias': _L0_gnn_in['bias'], 'L1_gnn_W1': _L1_gnn_in['W1'], 'L1_gnn_b1': _L1_gnn_in['b1'], 'L1_gnn_W2': _L1_gnn_in['W2'], 'L1_gnn_b2': _L1_gnn_in['b2'], 'L1_gnn_W3': _L1_gnn_in['W3'], 'L1_gnn_b3': _L1_gnn_in['b3'], 'L1_gnn_W4': _L1_gnn_in['W4'], 'L1_gnn_b4': _L1_gnn_in['b4'], 'L2_gnn_W1': _L2_gnn_in['W1'], 'L2_gnn_b1': _L2_gnn_in['b1'], 'L2_gnn_W2': _L2_gnn_in['W2'], 'L2_gnn_b2': _L2_gnn_in['b2'], 'L3_gnn_g': _L3_gnn_in['g']}

def reference(x, src, dst, edge_attr_16, edge_attr_32, L0_gnn_w, L0_gnn_fc_w, L0_gnn_fc_b, L0_gnn_bias, L1_gnn_W1, L1_gnn_b1, L1_gnn_W2, L1_gnn_b2, L1_gnn_W3, L1_gnn_b3, L1_gnn_W4, L1_gnn_b4, L2_gnn_W1, L2_gnn_b1, L2_gnn_W2, L2_gnn_b2, L3_gnn_g):
    import jax
    import jax.numpy as jnp

    def _L0_gnn_ref(h, edge_index, w, fc_w, fc_b, bias):
        import jax, jax.numpy as jnp
        import numpy as np
        N_NODES = 6250
        DEG = 16
        N_HEAD = 4
        F_IN = 32
        F_OUT = 32
        n_head, f_in, f_out = w.shape
        n = h.shape[0]
        src, dst = (edge_index[0], edge_index[1])
        hp = jnp.einsum('nf,hfo->hno', h, w)
        w_src = fc_w[0, :f_out]
        w_dst = fc_w[0, f_out:]
        a_src = jnp.einsum('hnf,f->hn', hp, w_src)
        a_dst = jnp.einsum('hnf,f->hn', hp, w_dst)
        e = a_src[:, src] + a_dst[:, dst] + fc_b[0]
        e = jax.nn.leaky_relu(e, negative_slope=0.2)
        seg_max = jax.ops.segment_max(e.T, src, num_segments=n)
        e = jnp.exp(e - seg_max.T[:, src])
        seg_sum = jax.ops.segment_sum(e.T, src, num_segments=n)
        att = e / seg_sum.T[:, src]
        msg = att[:, :, None] * hp[:, dst, :]
        agg = jax.vmap(lambda m: jax.ops.segment_sum(m, src, num_segments=n))(msg)
        out = agg.mean(axis=0) + bias
        return out

    def _L1_gnn_ref(x, edge_index, W1, b1, W2, b2, W3, b3, W4, b4):
        import jax, jax.numpy as jnp
        import numpy as np
        N_NODES = 12500
        N_EDGES = 312500
        IN_CH = 32
        HID = 16
        OUT_CH = 32

        def _gin_conv(x, src, dst, W_a, b_a, W_b, b_b):
            agg = jax.ops.segment_sum(x[src], dst, num_segments=x.shape[0])
            h = x + agg
            h = jnp.maximum(h @ W_a + b_a, 0.0)
            return h @ W_b + b_b
        src, dst = (edge_index[0], edge_index[1])
        h = _gin_conv(x, src, dst, W1, b1, W2, b2)
        h = jnp.maximum(h, 0.0)
        out = _gin_conv(h, src, dst, W3, b3, W4, b4)
        return out

    def _L2_gnn_ref(x, edge_index, edge_attr, W1, b1, W2, b2):
        import jax, jax.numpy as jnp
        import numpy as np
        N_NODES = 12500
        N_EDGES = 125000
        IN_CH = 32
        EDGE_CH = 16
        OUT_CH = 32
        D_CAT = 2 * IN_CH + EDGE_CH
        D_MID = 56
        num_nodes = x.shape[0]
        rol, col = (edge_index[0], edge_index[1])
        e = jnp.concatenate([x[rol], x[col], edge_attr], axis=-1)
        h = jax.nn.leaky_relu(e @ W1 + b1)
        v = jax.nn.leaky_relu(h @ W2 + b2)
        agg = jax.ops.segment_max(v, col, num_segments=num_nodes)
        agg = jnp.where(jnp.isneginf(agg), jnp.zeros((), dtype=agg.dtype), agg)
        out = jnp.maximum(agg, x[:, -v.shape[-1]:])
        return out

    def _L3_gnn_ref(vertex_attr, edgeij_pair, edge_attr, g, batch):
        import jax, jax.numpy as jnp
        import numpy as np
        N_VERTICES = 6250
        N_EDGES = 200000
        D_FEAT = 32
        n_vertices = vertex_attr.shape[0]
        cbar_i = jax.ops.segment_sum(edge_attr, edgeij_pair[0], num_segments=n_vertices)
        return cbar_i
    edge_index = jnp.stack([src, dst])
    batch0 = jnp.zeros((12500,), jnp.int32)
    x = _layernorm(x + _L0_gnn_ref(x, edge_index, L0_gnn_w, L0_gnn_fc_w, L0_gnn_fc_b, L0_gnn_bias), axis=-1)
    x = _layernorm(x + _L1_gnn_ref(x, edge_index, L1_gnn_W1, L1_gnn_b1, L1_gnn_W2, L1_gnn_b2, L1_gnn_W3, L1_gnn_b3, L1_gnn_W4, L1_gnn_b4), axis=-1)
    x = _layernorm(x + _L2_gnn_ref(x, edge_index, edge_attr_16, L2_gnn_W1, L2_gnn_b1, L2_gnn_W2, L2_gnn_b2), axis=-1)
    x = _layernorm(x + _L3_gnn_ref(x, edge_index, edge_attr_32, L3_gnn_g, batch0), axis=-1)
    return x

_drawn_inputs = setup_inputs


def setup_inputs(seed=0):
    import zlib

    import numpy as np

    out = dict(_drawn_inputs(seed))
    spreads = {'L0_gnn_bias': (0.0, 0.1),
     'L1_gnn_b1': (0.0, 0.765),
     'L1_gnn_b2': (0.0, 0.7),
     'L1_gnn_b3': (0.0, 2.0),
     'L1_gnn_b4': (0.0, 2.0),
     'L2_gnn_b1': (0.0, 0.8),
     'L2_gnn_b2': (0.0, 0.659)}
    factors = {'edge_attr_16': 2.742}
    for name, (base, spread) in spreads.items():
        noise = np.random.default_rng([zlib.crc32(name.encode()), seed]).standard_normal(out[name].shape)
        drawn = base * np.exp(spread * noise) if base else spread * noise
        out[name] = jnp.asarray(drawn.astype(out[name].dtype))
    for name, factor in factors.items():
        out[name] = (out[name] * factor).astype(out[name].dtype)
    return out
```

```python
import concourse.bass as bass
from concourse import mybir
from contextlib import ExitStack

f32 = mybir.dt.float32
bf16 = mybir.dt.bfloat16
i32 = mybir.dt.int32
ALU = mybir.AluOpType
ACT = mybir.ActivationFunctionType
AX = mybir.AxisListType

P = 128
N, E, F, HEADS, HID = 12500, 200000, 32, 4, 16
ATTR, MID = 16, 56
NJ = 100
NP_REAL = N // NJ
T = 1600
EP_REAL = E // T
N_PAD, E_PAD = P * NJ, P * T
TB = 32
NIT = T // (2 * TB)
CH = 8
STEPS = TB // CH
BIG = 3.4e38
MAGIC = 12582912.0
W_DS = 2 + ATTR + F
W_XA = HEADS + F
W_SS = 1 + W_XA + F
W_V = HEADS * F + HEADS + F
SPLITS = ((0, 112), (112, 125))


def hold(eng, sem, value, tick):
    eng.wait_ge(sem, value)
    eng.sem_inc(tick, 1)


class Build:
    def __init__(self, nc, a, out):
        self.nc, self.a, self.out, self.n, self.owned = nc, a, out, 0, {}

    def sb(self, ctx, name, shape, dt=f32):
        self.n += 1
        return ctx.enter_context(self.nc.sbuf_tensor(f"{name}_{self.n}", shape, dt))

    def ps(self, ctx, name, shape, dt=f32):
        self.n += 1
        return ctx.enter_context(self.nc.psum_tensor(f"{name}_{self.n}", shape, dt))

    def sem(self, ctx, name):
        self.n += 1
        s = self.nc.alloc_semaphore(f"{name}_{self.n}")
        if id(ctx) not in self.owned:
            self.owned[id(ctx)] = []
            ctx.callback(self.release, id(ctx))
        self.owned[id(ctx)].append(s)
        return s

    def release(self, key):
        self.nc.clear_and_free_semaphores(self.owned.pop(key))
        self.nc.all_engine_barrier()

    def dram(self, name, shape, dt=f32):
        return self.nc.dram_tensor(name, shape, dt, kind="Internal").ap()

    def setup(self, ctx):
        nc, a = self.nc, self.a
        sb = lambda name, shape, dt=f32: self.sb(ctx, name, shape, dt)
        self.irow = sb("irow", [P, P])
        self.ipart = sb("ipart", [P, 1])
        self.inode = sb("inode", [P, NJ])
        self.irow_b = sb("irow_b", [P, P], bf16)
        self.ident = sb("ident", [P, P])
        self.ident_b = sb("ident_b", [P, P], bf16)
        self.tri = sb("tri", [P, P])
        self.tri_b = sb("tri_b", [P, P], bf16)
        self.ones = sb("ones", [P, P])
        self.x = sb("x", [P, NJ, F])
        self.zero = sb("zero", [P, 1600])
        self.edge = sb("edge", [P, T + CH, 2])
        self.z_x = self.dram("z_x", (E_PAD + N_PAD, W_XA))
        self.z_e = self.dram("z_e", (E_PAD + N_PAD, 2 * HEADS))
        self.z_2 = self.dram("z_2", (E_PAD + N_PAD, F))
        self.s_v = self.dram("s_v", (E_PAD + 1, W_V))
        self.s_m = self.dram("s_m", (E_PAD + 1, HEADS))
        self.s_1 = self.dram("s_1", (E_PAD + 1, HID))
        self.s_1b = self.dram("s_1b", (E_PAD + 1, HID))
        self.s_2 = self.dram("s_2", (E_PAD + 1, F))
        with ExitStack() as c:
            ki = self.sb(c, "ki", [P, T, 2], i32)
            s_in, s_z, s_io, s_ms = (self.sem(c, n) for n in ("s_in", "s_z", "s_io", "s_ms"))
            block = c.enter_context(nc.Block())

            @block.gpsimd
            def _(pool):
                nc.gpsimd.iota(self.irow[:], [[1, P]], base=0, channel_multiplier=0,
                               allow_small_or_imprecise_dtypes=True)
                nc.gpsimd.iota(self.ipart[:], [[1, 1]], base=0, channel_multiplier=1,
                               allow_small_or_imprecise_dtypes=True)
                nc.gpsimd.iota(self.inode[:], [[1, NJ]], base=0, channel_multiplier=NJ,
                               allow_small_or_imprecise_dtypes=True)
                pool.drain().then_inc(s_io, 1)

            @block.vector
            def _(v):
                nc.vector.memset(self.zero[:], 0.0)
                nc.vector.memset(self.x[:], 0.0)
                nc.vector.memset(self.ones[:], 1.0)
                nc.vector.memset(ki[:], N)
                nc.vector.memset(self.edge[:], float(N))
                v.drain().then_inc(s_ms, 1)
                v.wait_ge(s_io, 1)
                nc.vector.tensor_scalar(self.ident[:], self.irow[:], self.ipart[:, 0:1], None, ALU.is_equal)
                nc.vector.tensor_scalar(self.tri[:], self.irow[:], self.ipart[:, 0:1], None, ALU.is_gt)
                nc.vector.tensor_scalar(self.ident_b[:], self.irow[:], self.ipart[:, 0:1], None, ALU.is_equal)
                nc.vector.tensor_scalar(self.tri_b[:], self.irow[:], self.ipart[:, 0:1], None, ALU.is_gt)
                nc.vector.tensor_copy(self.irow_b[:], self.irow[:])
                v.wait_ge(s_in, 16 * 6)
                nc.vector.tensor_copy(self.edge[:, 0:T, :], ki[:])

            @block.sync
            def _(sp):
                sp.wait_ge(s_ms, 1)
                for lo, hi in SPLITS:
                    sp.dma_start(self.x[lo:hi], a["x"].rearrange("(p j) f -> p j f", j=NJ)[lo:hi]).then_inc(s_in, 16)
                    with nc.allow_non_contiguous_dma(reason="keys interleaved"):
                        for k, name in ((0, "dst"), (1, "src")):
                            sp.dma_start(ki[lo:hi, :, k], a[name].rearrange("(p t) -> p t", t=T)[lo:hi]).then_inc(s_in, 16)
                n = 0
                for z in (self.z_x, self.z_e, self.z_2):
                    w = z.shape[1]
                    rows = z[0:E_PAD].rearrange("(p t) w -> p (t w)", p=P)
                    for k in range(w):
                        sp.dma_start(rows[:, k * T:(k + 1) * T], self.zero[:]).then_inc(s_z, 16)
                        n += 1
                for s in (self.s_v, self.s_m, self.s_1, self.s_1b, self.s_2):
                    sp.dma_start(s[E_PAD:E_PAD + 1, :], self.zero[0:1, 0:s.shape[1]]).then_inc(s_z, 16)
                    n += 1
                sp.wait_ge(s_z, 16 * n)
                sp.wait_ge(s_in, 16 * 6)

    def csr(self, ctx, which, first=None, last=None):
        nc = self.nc
        kp = self.sb(ctx, "kp", [P, T + CH])
        kj = self.sb(ctx, "kj", [P, T + CH])
        C = self.sb(ctx, "C", [P, CH, NJ])
        first = first or self.sb(ctx, "first", [P, NJ], i32)
        last = last or self.sb(ctx, "last", [P, NJ], i32)
        with ExitStack() as c:
            H = self.sb(c, "H", [P, CH, NJ])
            cnt, incl, start, full, t1, t2 = (self.sb(c, n, [P, NJ]) for n in ("cnt", "incl", "start", "full", "t1", "t2"))
            kb = self.sb(c, "kb", [P, 2, 2 * TB])
            ohp = self.sb(c, "ohp", [P, 2, CH, P], bf16)
            ohj = self.sb(c, "ohj", [P, 2, CH, P], bf16)
            Hp = self.ps(c, "Hp", [P, 2, CH, P])
            pre = self.ps(c, "pre", [P, 1])
            s_oh, s_h, s_rs, s_pre, tick = (self.sem(c, n) for n in ("s_oh", "s_h", "s_rs", "s_pre", "tick"))
            block = c.enter_context(nc.Block())
            NS = 2 * STEPS

            @block.vector
            def _(v):
                key = self.edge[:, :, which]
                nc.vector.memset(H[:], 0.0)
                nc.vector.tensor_scalar(kp[:], key, 1.0 / NJ, -0.495, ALU.mult, ALU.add)
                v.drain()
                nc.vector.tensor_scalar(kp[:], kp[:], MAGIC, MAGIC, ALU.add, ALU.subtract)
                v.drain()
                nc.vector.scalar_tensor_tensor(kj[:], kp[:], -float(NJ), key, ALU.mult, ALU.add)
                v.drain()
                v.sem_inc(s_h, 1)
                with v.Fori(0, NIT) as i:
                    nc.vector.tensor_copy(kb[:, 0, :], kp[:, bass.ds(i * 2 * TB, 2 * TB)])
                    nc.vector.tensor_copy(kb[:, 1, :], kj[:, bass.ds(i * 2 * TB, 2 * TB)])
                    v.drain()
                    for s in range(NS):
                        for k in range(CH):
                            t = s * CH + k
                            nc.vector.tensor_scalar(ohp[:, s % 2, k, :], self.irow_b[:], kb[:, 0, t:t + 1], None, ALU.is_equal)
                            nc.vector.tensor_scalar(ohj[:, s % 2, k, 0:NJ], self.irow_b[:, 0:NJ], kb[:, 1, t:t + 1], None, ALU.is_equal)
                        v.drain().then_inc(s_oh, 1)
                        hold(v, s_h, i * NS + s + 1, tick)
                        if s > 0:
                            nc.vector.tensor_tensor(H[:], H[:], Hp[:, (s - 1) % 2, :, 0:NJ], ALU.add)
                            v.drain()
                    hold(v, s_h, i * NS + NS + 1, tick)
                    nc.vector.tensor_tensor(H[:], H[:], Hp[:, (NS - 1) % 2, :, 0:NJ], ALU.add)
                    v.drain()
                nc.vector.tensor_tensor(cnt[:], H[:, 0, :], H[:, 1, :], ALU.add)
                for k in range(2, CH):
                    v.drain()
                    nc.vector.tensor_tensor(cnt[:], cnt[:], H[:, k, :], ALU.add)
                v.drain()
                nc.vector.tensor_tensor_scan(incl[:], self.ones[:, 0:NJ], cnt[:], 0.0, ALU.mult, ALU.add)
                v.drain().then_inc(s_rs, 1)
                v.wait_ge(s_pre, 1)
                nc.vector.tensor_tensor(start[:], incl[:], cnt[:], ALU.subtract)
                v.drain()
                nc.vector.tensor_scalar(start[:], start[:], pre[:, 0:1], None, ALU.add)
                nc.vector.tensor_scalar(full[:], cnt[:], 0.0, None, ALU.is_gt)
                v.drain()
                nc.vector.tensor_copy(C[:, 0, :], start[:])
                for k in range(1, CH):
                    v.drain()
                    nc.vector.tensor_tensor(C[:, k, :], C[:, k - 1, :], H[:, k - 1, :], ALU.add)
                nc.vector.tensor_scalar(t1[:], self.inode[:], float(E_PAD), None, ALU.add)
                nc.vector.scalar_tensor_tensor(t2[:], start[:], -1.0 - E_PAD, cnt[:], ALU.add, ALU.add)
                v.drain()
                nc.vector.tensor_tensor(start[:], start[:], t1[:], ALU.subtract)
                nc.vector.tensor_tensor(t2[:], t2[:], full[:], ALU.mult)
                v.drain()
                nc.vector.tensor_tensor(start[:], start[:], full[:], ALU.mult)
                nc.vector.tensor_scalar(last[:], t2[:], float(E_PAD), None, ALU.add)
                v.drain()
                nc.vector.tensor_tensor(first[:], start[:], t1[:], ALU.add)

            @block.tensor
            def _(pe):
                with pe.Fori(0, NIT) as i:
                    for s in range(NS):
                        hold(pe, s_oh, i * NS + s + 1, tick)
                        for k in range(CH):
                            mm = nc.tensor.matmul(Hp[:, s % 2, k, 0:NJ], ohp[:, s % 2, k, :], ohj[:, s % 2, k, 0:NJ],
                                                  start=True, stop=True)
                        mm.then_inc(s_h, 1)
                pe.wait_ge(s_rs, 1)
                nc.tensor.matmul(pre[:], self.tri[:], incl[:, NJ - 1:NJ], start=True, stop=True).then_inc(s_pre, 1)
        return kp, kj, C, first, last

    def sort(self, digits, C, W, rows, prepare, loads, fill):
        nc = self.nc
        kp, kj = digits
        with ExitStack() as c:
            pay = self.sb(c, "pay", [P, 2, TB, W])
            pos = self.sb(c, "pos", [P, 2, TB], i32)
            kb = self.sb(c, "kb", [P, 2, 2 * TB + CH])
            ohp = self.sb(c, "ohp", [P, 2, CH, P], bf16)
            ohj = self.sb(c, "ohj", [P, 2, CH, P], bf16)
            ohT = self.sb(c, "ohT", [P, CH, P])
            ohTb = self.sb(c, "ohTb", [P, CH, P], bf16)
            Lm = self.sb(c, "Lm", [P, CH, P], bf16)
            g = self.sb(c, "g", [P, CH, NJ])
            posf = self.sb(c, "posf", [P, CH])
            pT = self.ps(c, "pT", [P, CH, P], bf16)
            pS = self.ps(c, "pS", [P, CH, P])
            pD = self.ps(c, "pD", [P, CH, P])
            pG = self.ps(c, "pG", [P, CH, P])
            names = ("s_oh", "s_T", "s_cp", "s_S", "s_L", "s_G", "s_C", "s_pos", "tick", "s_pre")
            s_oh, s_T, s_cp, s_S, s_L, s_G, s_C, s_pos, tick, s_prep = (self.sem(c, n) for n in names)
            s_ld = [self.sem(c, "s_ld") for _ in range(2)]
            s_sc = [self.sem(c, "s_sc") for _ in range(2)]
            s_free = [self.sem(c, "s_free") for _ in range(2)]
            s_pay = self.sem(c, "s_pay")
            extra = prepare(c)
            nload = loads(None, None, None, None, extra)
            block = c.enter_context(nc.Block())
            NS = 2 * STEPS
            target = rows

            @block.vector
            def _(v):
                def onehots(s, buf):
                    for k in range(CH):
                        t = s * CH + k
                        nc.vector.tensor_scalar(ohp[:, buf, k, :], self.irow_b[:], kb[:, 0, t:t + 1], None, ALU.is_equal)
                        nc.vector.tensor_scalar(ohj[:, buf, k, 0:NJ], self.irow_b[:, 0:NJ], kb[:, 1, t:t + 1], None, ALU.is_equal)
                    v.drain().then_inc(s_oh, 1)

                nc.vector.memset(pay[:], 0.0)
                nc.vector.tensor_copy(kb[:, 0, 0:CH], kp[:, 0:CH])
                nc.vector.tensor_copy(kb[:, 1, 0:CH], kj[:, 0:CH])
                v.drain().then_inc(s_prep, 1)
                onehots(0, 0)
                with v.Fori(0, NIT) as i:
                    nc.vector.tensor_copy(kb[:, 0, :], kp[:, bass.ds(i * 2 * TB, 2 * TB + CH)])
                    nc.vector.tensor_copy(kb[:, 1, :], kj[:, bass.ds(i * 2 * TB, 2 * TB + CH)])
                    v.drain()
                    for s in range(NS):
                        h = s // STEPS
                        if s % STEPS == 0:
                            hold(v, s_ld[h], (i + 1) * (16 * nload), tick)
                            fill(v, i, h, pay, extra)
                            v.drain().then_inc(s_pay, 1)
                        hold(v, s_S, i * NS + s + 1, tick)
                        nc.vector.tensor_tensor(Lm[:], pS[:], self.tri_b[:].unsqueeze(1).to_broadcast([P, CH, P]), ALU.mult)
                        v.drain().then_inc(s_L, 1)
                        onehots(s + 1, (s + 1) % 2)
                        hold(v, s_G, i * NS + s + 1, tick)
                        nc.vector.tensor_tensor(g[:], pG[:, :, 0:NJ], ohj[:, s % 2, :, 0:NJ], ALU.mult)
                        nc.vector.tensor_tensor(C[:], C[:], pD[:, :, 0:NJ], ALU.add)
                        v.drain().then_inc(s_C, 1)
                        nc.vector.tensor_reduce(posf[:], g[:], AX.X, ALU.add)
                        v.drain()
                        o = (s % STEPS) * CH
                        nc.vector.tensor_copy(pos[:, h, o:o + CH], posf[:]).then_inc(s_pos, 1)

            @block.scalar
            def _(act):
                def copies():
                    nc.scalar.copy(ohT[:], pT[:])
                    nc.scalar.copy(ohTb[:], pT[:]).then_inc(s_cp, 1)
                act.wait_ge(s_T, 1)
                copies()
                with act.Fori(0, NIT) as i:
                    for s in range(NS):
                        hold(act, s_T, i * NS + s + 2, tick)
                        copies()

            @block.tensor
            def _(pe):
                def turn(buf):
                    for k in range(CH):
                        mm = nc.tensor.transpose(pT[:, k, :], ohp[:, buf, k, :], self.ident_b[:])
                    mm.then_inc(s_T, 1)

                def pairs(buf):
                    for k in range(CH):
                        nc.tensor.matmul(pS[:, k, :], ohTb[:, k, :], ohTb[:, k, :], start=True, stop=True)

                def counts(buf):
                    for k in range(CH):
                        mm = nc.tensor.matmul(pD[:, k, 0:NJ], ohp[:, buf, k, :], ohj[:, buf, k, 0:NJ], start=True, stop=True)
                    mm.then_inc(s_S, 1)

                pe.wait_ge(s_oh, 1)
                turn(0)
                pe.wait_ge(s_cp, 1)
                pairs(0)
                counts(0)
                with pe.Fori(0, NIT) as i:
                    for s in range(NS):
                        hold(pe, s_L, i * NS + s + 1, tick)
                        for k in range(CH):
                            nc.tensor.matmul(pG[:, k, 0:NJ], ohT[:, k, :], C[:, k, :], start=True, stop=False)
                            mm = nc.tensor.matmul(pG[:, k, 0:NJ], Lm[:, k, :], ohj[:, s % 2, k, 0:NJ], start=False, stop=True)
                        mm.then_inc(s_G, 1)
                        hold(pe, s_oh, i * NS + s + 2, tick)
                        turn((s + 1) % 2)
                        hold(pe, s_cp, i * NS + s + 2, tick)
                        pairs((s + 1) % 2)
                        hold(pe, s_C, i * NS + s + 1, tick)
                        counts((s + 1) % 2)

            @block.gpsimd
            def _(pool):
                with pool.Fori(0, NIT) as i:
                    for s in range(NS):
                        h = s // STEPS
                        if s % STEPS == 0:
                            hold(pool, s_pay, i * 2 + h + 1, tick)
                        hold(pool, s_pos, i * NS + s + 1, tick)
                        for k in range(CH):
                            t = (s % STEPS) * CH + k
                            nc.gpsimd.indirect_dma_start(target[:, :], bass.IndirectOffsetOnAxis(pos[:, h, t:t + 1], 0),
                                                         pay[:, h, t, :], None).then_inc(s_sc[h], 16)
                for h in range(2):
                    pool.wait_ge(s_sc[h], NIT * TB * 16)

            @block.sync
            def _(sp):
                sp.wait_ge(s_prep, 1)
                for h in range(2):
                    loads(sp, 0, h, (pay, s_ld[h]), extra)
                with sp.Fori(0, NIT - 1) as i:
                    for h in range(2):
                        hold(sp, s_sc[h], (i + 1) * (TB * 16), tick)
                        loads(sp, i + 1, h, (pay, s_ld[h]), extra)

    def sort_by_dst(self, first_d, last_d):
        nc, a = self.nc, self.a
        with ExitStack() as c:
            kp, kj, C, _, _ = self.csr(c, 0, first_d, last_d)
            self.ds = self.dram("ds", (E_PAD, W_DS))
            a16 = a["edge_attr_16"].rearrange("(p t) f -> p t f", t=T)
            a32 = a["edge_attr_32"].rearrange("(p t) f -> p t f", t=T)

            def loads(sp, i, h, to, extra):
                if sp is not None:
                    pay, done = to
                    at = bass.ds((i * 2 + h) * TB, TB)
                    for lo, hi in SPLITS:
                        sp.dma_start(pay[lo:hi, h, :, 2:2 + ATTR], a16[lo:hi, at, :]).then_inc(done, 16)
                        sp.dma_start(pay[lo:hi, h, :, 2 + ATTR:W_DS], a32[lo:hi, at, :]).then_inc(done, 16)
                return 4

            def fill(v, i, h, pay, extra):
                nc.vector.tensor_copy(pay[:, h, :, 0:2], self.edge[:, bass.ds((i * 2 + h) * TB, TB), :])

            self.sort((kp, kj), C, W_DS, self.ds, lambda c: None, loads, fill)

    def order_tiles(self, ctx):
        return {
            "cont": self.sb(ctx, "cont", [P, T]),
            "contm": self.sb(ctx, "contm", [P, T]),
            "fix": self.sb(ctx, "fix", [P, 1], i32),
            "w": self.sb(ctx, "w", [P, P]),
            "wm": self.sb(ctx, "wm", [P, P]),
        }

    def order(self, ctx, key, o=None):
        nc = self.nc
        o = o or self.order_tiles(ctx)
        with ExitStack() as c:
            prev = self.sb(c, "prev", [P, 1])
            last = self.sb(c, "lastk", [P, 1])
            n, whole = self.sb(c, "n", [P, 1]), self.sb(c, "whole", [P, 1])
            eq = self.sb(c, "eq", [P, T])
            wb = self.sb(c, "wb", [P, P])
            pw = self.ps(c, "pw", [P, P])
            s_a, s_b, s_w, s_m = (self.sem(c, n_) for n_ in ("s_a", "s_b", "s_w", "s_m"))
            block = c.enter_context(nc.Block())

            @block.sync
            def _(sp):
                sp.wait_ge(s_a, 1)
                sp.dma_start(prev[1:P, :], last[0:P - 1, :]).then_inc(s_b, 16)
                sp.wait_ge(s_b, 16)

            @block.tensor
            def _(pe):
                pe.wait_ge(s_w, 1)
                nc.tensor.matmul(pw[:], wb[:], self.ident[:], start=True, stop=True).then_inc(s_m, 1)

            @block.vector
            def _(v):
                nc.vector.memset(prev[:], -1.0)
                nc.vector.tensor_copy(last[:], key[:, T - 1:T])
                v.drain().then_inc(s_a, 1)
                nc.vector.tensor_copy(eq[:], key)
                v.drain()
                nc.vector.tensor_tensor(o["cont"][:, 1:T], eq[:, 1:T], eq[:, 0:T - 1], ALU.is_equal)
                v.wait_ge(s_b, 16)
                nc.vector.tensor_tensor(o["cont"][:, 0:1], eq[:, 0:1], prev[:], ALU.is_equal)
                v.drain()
                nc.vector.tensor_scalar(o["contm"][:], o["cont"][:], 2.0, -1.0, ALU.mult, ALU.add)
                nc.vector.tensor_scalar(wb[:, 0:1], eq[:, 0:1], 1.0, None, ALU.mult)
                v.drain()
                nc.vector.tensor_scalar(o["contm"][:], o["contm"][:], BIG, None, ALU.mult)
                nc.vector.tensor_scalar(eq[:], eq[:], wb[:, 0:1], None, ALU.is_equal)
                v.drain()
                nc.vector.reduce_sum(n[:], eq[:], AX.X)
                v.drain()
                nc.vector.tensor_scalar(whole[:], n[:], float(T), None, ALU.is_equal)
                nc.vector.scalar_tensor_tensor(n[:], self.ipart[:], float(T), n[:], ALU.mult, ALU.add)
                v.drain()
                nc.vector.tensor_scalar(o["fix"][:], n[:], 1.0, None, ALU.subtract)
                nc.vector.tensor_tensor(whole[:], whole[:], o["cont"][:, 0:1], ALU.mult)
                v.drain()
                nc.vector.tensor_scalar(wb[:], self.ones[:], whole[:, 0:1], None, ALU.mult)
                v.drain().then_inc(s_w, 1)
                v.wait_ge(s_m, 1)
                nc.vector.tensor_copy(o["w"][:], pw[:])
                v.drain()
                nc.vector.tensor_scalar(o["wm"][:], o["w"][:], 2.0, -1.0, ALU.mult, ALU.add)
                v.drain()
                nc.vector.tensor_scalar(o["wm"][:], o["wm"][:], BIG, None, ALU.mult)
        return o

    def join(self, o, tail, W, s, is_max):
        nc = self.nc
        neutral = -BIG if is_max else 0.0
        ops = (ALU.min, ALU.max) if is_max else (ALU.mult, ALU.add)
        groups = [(lo, min(lo + P, W)) for lo in range(0, W, P)]
        with ExitStack() as c:
            tT = self.sb(c, "tT", [P, P])
            sT = self.sb(c, "sT", [P, P + 1])
            carry = self.sb(c, "carry", [P, W])
            row = self.sb(c, "row", [P, W])
            pt = self.ps(c, "pt", [P, P])
            pb = self.ps(c, "pb", [P, P])
            s_t, s_s, s_b, s_g, s_r, s_o, s_d = (self.sem(c, n) for n in ("s_t", "s_s", "s_b", "s_g", "s_r", "s_o", "s_d"))
            block = c.enter_context(nc.Block())

            @block.tensor
            def _(pe):
                for k, (lo, hi) in enumerate(groups):
                    if k:
                        pe.wait_ge(s_d, k)
                    nc.tensor.transpose(pt[0:hi - lo, :], tail[:, lo:hi], self.ident[:]).then_inc(s_t, 1)
                    pe.wait_ge(s_s, k + 1)
                    nc.tensor.transpose(pb[:, 0:hi - lo], sT[0:hi - lo, 0:P], self.ident[0:hi - lo, 0:hi - lo]).then_inc(s_b, 1)

            @block.vector
            def _(v):
                nc.vector.memset(sT[:], neutral)
                v.drain()
                for k, (lo, hi) in enumerate(groups):
                    n = hi - lo
                    v.wait_ge(s_t, k + 1)
                    nc.vector.tensor_copy(tT[0:n, :], pt[0:n, :])
                    v.drain()
                    nc.vector.tensor_tensor_scan(sT[0:n, 1:P + 1], o["wm" if is_max else "w"][0:n, :], tT[0:n, :], neutral, *ops)
                    v.drain().then_inc(s_s, 1)
                    v.wait_ge(s_b, k + 1)
                    nc.vector.tensor_scalar(carry[:, lo:hi], pb[:, 0:n], o["contm" if is_max else "cont"][:, 0:1], None, ops[0])
                    v.drain().then_inc(s_d, 1)
                v.wait_ge(s_g, 16)
                nc.vector.tensor_tensor(row[:], row[:], carry[:], ops[1])
                v.drain().then_inc(s_r, 1)

            @block.gpsimd
            def _(pool):
                nc.gpsimd.indirect_dma_start(row[:], None, s[:, :], bass.IndirectOffsetOnAxis(o["fix"][:, 0:1], 0)).then_inc(s_g, 16)
                pool.wait_ge(s_r, 1)
                nc.gpsimd.indirect_dma_start(s[:, :], bass.IndirectOffsetOnAxis(o["fix"][:, 0:1], 0), row[:], None).then_inc(s_o, 16)
                pool.wait_ge(s_o, 16)

    def fetch(self, s, idx, out):
        nc = self.nc
        with ExitStack() as c:
            s_g = self.sem(c, "s_g")
            block = c.enter_context(nc.Block())

            @block.gpsimd
            def _(pool):
                for j in range(NJ):
                    nc.gpsimd.indirect_dma_start(out[:, j, :], None, s[:, :], bass.IndirectOffsetOnAxis(idx[:, j:j + 1], 0)).then_inc(s_g, 16)
                pool.wait_ge(s_g, 16 * NJ)

    def spread(self, z, idx, rows, table=None):
        nc = self.nc
        with ExitStack() as c:
            s_g, s_t = self.sem(c, "s_g"), self.sem(c, "s_t")
            block = c.enter_context(nc.Block())

            @block.gpsimd
            def _(pool):
                for j in range(NJ if z is not None else 0):
                    nc.gpsimd.indirect_dma_start(z[:, :], bass.IndirectOffsetOnAxis(idx[:, j:j + 1], 0), rows[:, j, :], None).then_inc(s_g, 16)
                if z is not None:
                    pool.wait_ge(s_g, 16 * NJ)

            @block.sync
            def _(sp):
                if table is not None:
                    sp.dma_start(table.rearrange("(p j) f -> p j f", j=NJ), rows[:]).then_inc(s_t, 16)
                    sp.wait_ge(s_t, 16)

    def first_rows(self, table, idx, out):
        nc = self.nc
        with ExitStack() as c:
            s_g = self.sem(c, "s_g")
            block = c.enter_context(nc.Block())

            @block.gpsimd
            def _(pool):
                nc.gpsimd.indirect_dma_start(out[:], None, table[:, :], bass.IndirectOffsetOnAxis(idx, 0)).then_inc(s_g, 16)
                pool.wait_ge(s_g, 16)

    def dense(self, src, J, K, M, weights, post):
        nc = self.nc
        G = NJ // J
        with ExitStack() as c:
            xT = self.sb(c, "xT", [P, 2, P])
            pt = [self.ps(c, "pt", [P, P]) for _ in range(2)]
            po = [self.ps(c, "po", [P, J * M]) for _ in range(2)]
            s_t, s_c, s_m, s_p = (self.sem(c, n) for n in ("s_t", "s_c", "s_m", "s_p"))
            block = c.enter_context(nc.Block())

            @block.tensor
            def _(pe):
                for g in range(G + 1):
                    if g < G:
                        if g >= 2:
                            pe.wait_ge(s_c, g - 1)
                        nc.tensor.transpose(pt[g % 2][0:J * K, :], src[:, g * J:(g + 1) * J, :].rearrange("p j k -> p (j k)"),
                                            self.ident[:]).then_inc(s_t, 1)
                    if g >= 1:
                        pe.wait_ge(s_c, g)
                        if g >= 3:
                            pe.wait_ge(s_p, g - 2)
                        nc.tensor.matmul(po[(g - 1) % 2][:], xT[0:J * K, (g - 1) % 2, :], weights, start=True, stop=True).then_inc(s_m, 1)

            @block.scalar
            def _(act):
                for g in range(G):
                    act.wait_ge(s_t, g + 1)
                    if g >= 2:
                        act.wait_ge(s_m, g - 1)
                    nc.scalar.copy(xT[0:J * K, g % 2, :], pt[g % 2][0:J * K, :]).then_inc(s_c, 1)

            @block.vector
            def _(v):
                for g in range(G):
                    v.wait_ge(s_m, g + 1)
                    post(v, g, po[g % 2])
                    v.drain().then_inc(s_p, 1)

    def block_diagonal(self, ctx, w, K, M, J=4, transform=None):
        nc = self.nc
        wd = self.sb(ctx, "wd", [P, J * M])
        with ExitStack() as c:
            s_z, s_l = self.sem(c, "s_z"), self.sem(c, "s_l")
            block = c.enter_context(nc.Block())

            @block.vector
            def _(v):
                nc.vector.memset(wd[:], 0.0)
                v.drain().then_inc(s_z, 1)

            @block.sync
            def _(sp):
                sp.wait_ge(s_z, 1)
                for j in range(J):
                    sp.dma_start(wd[j * K:(j + 1) * K, j * M:(j + 1) * M], w).then_inc(s_l, 16)
                sp.wait_ge(s_l, 16 * J)
        return wd[0:J * K, :]

    def row_of(self, ctx, b, n, J=1):
        nc = self.nc
        t = self.sb(ctx, "bias", [P, J, n])
        with ExitStack() as c:
            s_l = self.sem(c, "s_l")
            block = c.enter_context(nc.Block())

            @block.sync
            def _(sp):
                for j in range(J):
                    sp.dma_start(t[:, j, :], b.rearrange("(o n) -> o n", o=1).to_broadcast([P, n])).then_inc(s_l, 16)
                sp.wait_ge(s_l, 16 * J)
        return t

    def norm(self, y):
        nc = self.nc
        with ExitStack() as c:
            m, q = self.sb(c, "m", [P, NJ]), self.sb(c, "q", [P, NJ])
            sq = self.sb(c, "sq", [P, NJ, F])
            s_v, s_q = self.sem(c, "s_v"), self.sem(c, "s_q")
            block = c.enter_context(nc.Block())
            wide = lambda t: t[:].unsqueeze(2).to_broadcast([P, NJ, F])

            @block.vector
            def _(v):
                nc.vector.reduce_sum(m[:], y[:], AX.X)
                v.drain()
                nc.vector.tensor_scalar(m[:], m[:], 1.0 / F, None, ALU.mult)
                v.drain()
                nc.vector.tensor_tensor(y[:], y[:], wide(m), ALU.subtract)
                v.drain()
                nc.vector.tensor_tensor(sq[:], y[:], y[:], ALU.mult)
                v.drain()
                nc.vector.reduce_sum(q[:], sq[:], AX.X)
                v.drain()
                nc.vector.tensor_scalar(q[:], q[:], 1.0 / F, 1e-5, ALU.mult, ALU.add)
                v.drain().then_inc(s_v, 1)
                v.wait_ge(s_q, 1)
                nc.vector.reciprocal(q[:], q[:])
                v.drain()
                nc.vector.tensor_tensor(self.x[:], y[:], wide(q), ALU.mult)

            @block.scalar
            def _(act):
                act.wait_ge(s_v, 1)
                nc.scalar.activation(q[:], q[:], ACT.Sqrt).then_inc(s_q, 1)

    def dst_order(self, ctx):
        nc = self.nc
        self.src_i = self.sb(ctx, "src_i", [P, T], i32)
        self.key0_i = self.sb(ctx, "key0_i", [P, 1], i32)
        with ExitStack() as c:
            s_l = self.sem(c, "s_l")
            block = c.enter_context(nc.Block())

            @block.sync
            def _(sp):
                with nc.allow_non_contiguous_dma(reason="key columns of the sorted rows"):
                    sp.dma_start(self.edge[:, 0:T, :], self.ds.rearrange("(p t) w -> p t w", t=T)[:, :, 0:2]).then_inc(s_l, 16)
                sp.wait_ge(s_l, 16)

            @block.vector
            def _(v):
                v.wait_ge(s_l, 16)
                nc.vector.tensor_copy(self.src_i[:], self.edge[:, 0:T, 1])
                nc.vector.tensor_copy(self.key0_i[:], self.edge[:, 0:1, 0])
        return self.order(ctx, self.edge[:, 0:T, 0])

    def attention(self, d, first_d):
        nc, a = self.nc, self.a
        with ExitStack() as top:
            ab = self.sb(top, "ab", [P, NJ, 2 * HEADS])
            kp, kj, C, first_s, last_s = self.csr(top, 1)
            self.ss = self.dram("ss", (E_PAD, W_SS))
            xa_d = self.dram("xa_d", (N_PAD, W_XA))
            with ExitStack() as c:
                xa = self.sb(c, "xa", [P, NJ, W_XA])
                w_s = self.sb(c, "w_s", [F, HEADS, F])
                fc = self.sb(c, "fc", [F, 2 * F])
                fcb = self.sb(c, "fcb", [P, 1])
                pr = self.sb(c, "pr", [F, 2, HEADS, F])
                u = self.sb(c, "u", [F, 2 * HEADS])
                ud = self.sb(c, "ud", [P, 4 * 2 * HEADS])
                with ExitStack() as cc:
                    s_l, s_u, s_d = (self.sem(cc, n) for n in ("s_l", "s_u", "s_d"))
                    block = cc.enter_context(nc.Block())

                    @block.sync
                    def _(sp):
                        sp.dma_start(w_s[:], a["L0_gnn_w"].rearrange("h f o -> f h o")).then_inc(s_l, 16)
                        sp.dma_start(fc[:], a["L0_gnn_fc_w"].to_broadcast([F, 2 * F])).then_inc(s_l, 16)
                        sp.dma_start(fcb[:], a["L0_gnn_fc_b"].rearrange("(o n) -> o n", o=1).to_broadcast([P, 1])).then_inc(s_l, 16)
                        sp.wait_ge(s_u, 1)
                        for j in range(4):
                            sp.dma_start(ud[j * F:(j + 1) * F, j * 8:(j + 1) * 8], u[:]).then_inc(s_d, 16)
                        sp.wait_ge(s_d, 64)

                    @block.vector
                    def _(v):
                        nc.vector.memset(ud[:], 0.0)
                        v.wait_ge(s_l, 48)
                        for k in range(2):
                            nc.vector.tensor_tensor(pr[:, k], w_s[:], fc[:, k * F:(k + 1) * F].unsqueeze(1).to_broadcast([F, HEADS, F]), ALU.mult)
                            v.drain()
                            nc.vector.reduce_sum(u[:, k * HEADS:(k + 1) * HEADS], pr[:, k], AX.X)
                        nc.vector.tensor_copy(xa[:, :, HEADS:W_XA], self.x[:])
                        v.drain().then_inc(s_u, 1)

                def post(v, g, po):
                    o = po[:].rearrange("p (j m) -> p j m", j=4)
                    nc.vector.tensor_scalar(ab[:, 4 * g:4 * g + 4, 0:HEADS], o[:, :, 0:HEADS], fcb[:, 0:1], None, ALU.add)
                    nc.vector.tensor_copy(xa[:, 4 * g:4 * g + 4, 0:HEADS], o[:, :, HEADS:2 * HEADS])
                self.dense(self.x, 4, F, 2 * HEADS, ud[:], post)
                self.spread(self.z_x, first_d, xa, xa_d)

            z = self.z_x[0:E_PAD].rearrange("(p t) w -> p t w", t=T)
            dsv = self.ds.rearrange("(p t) w -> p t w", t=T)

            def prepare(c):
                zt = self.sb(c, "zt", [P, 2, TB, W_XA])
                carry = self.sb(c, "carry", [P, W_XA])
                cb = self.sb(c, "cb", [P, TB])
                self.first_rows(xa_d, self.key0_i[:, 0:1], carry)
                return zt, carry, cb

            def loads(sp, i, h, to, extra):
                if sp is not None:
                    pay, done = to
                    at = bass.ds((i * 2 + h) * TB, TB)
                    sp.dma_start(extra[0][:, h], z[:, at, :]).then_inc(done, 16)
                    sp.dma_start(pay[:, h, :, 1 + W_XA:W_SS], dsv[:, at, 2 + ATTR:W_DS]).then_inc(done, 16)
                return 2

            def fill(v, i, h, pay, extra):
                zt, carry, cb = extra
                at = bass.ds((i * 2 + h) * TB, TB)
                nc.vector.tensor_copy(cb[:], d["cont"][:, at])
                nc.vector.tensor_copy(pay[:, h, :, 0], self.edge[:, at, 1])
                v.drain()
                for f in range(W_XA):
                    nc.vector.tensor_tensor_scan(pay[:, h, :, 1 + f], cb[:], zt[:, h, :, f], carry[:, f:f + 1], ALU.mult, ALU.add)
                v.drain()
                nc.vector.tensor_copy(carry[:], pay[:, h, TB - 1, 1:1 + W_XA])
            self.sort((kp, kj), C, W_SS, self.ss, prepare, loads, fill)

            o_ctx = top.enter_context(ExitStack())
            ssv = self.ss.rearrange("(p t) w -> p t w", t=T)
            key0 = self.sb(o_ctx, "key0", [P, 1], i32)
            s = self.order_tiles(o_ctx)
            with ExitStack() as c:
                ka = self.sb(c, "ka", [P, T, 1 + HEADS])
                s_l = self.sem(c, "s_l")
                with ExitStack() as cc:
                    block = cc.enter_context(nc.Block())

                    @block.sync
                    def _(sp):
                        sp.dma_start(ka[:], ssv[:, :, 0:1 + HEADS]).then_inc(s_l, 16)
                        sp.wait_ge(s_l, 16)

                    @block.vector
                    def _(v):
                        v.wait_ge(s_l, 16)
                        nc.vector.tensor_copy(key0[:], ka[:, 0:1, 0])
                self.order(None, ka[:, :, 0], s)
                with ExitStack() as cc:
                    s_v, s_o = self.sem(cc, "s_v"), self.sem(cc, "s_o")
                    block = cc.enter_context(nc.Block())

                    @block.vector
                    def _(v):
                        for k in range(HEADS):
                            nc.vector.tensor_tensor_scan(ka[:, :, 1 + k], s["contm"][:], ka[:, :, 1 + k], -BIG, ALU.min, ALU.max)
                        v.drain().then_inc(s_v, 1)

                    @block.sync
                    def _(sp):
                        sp.wait_ge(s_v, 1)
                        sp.dma_start(self.s_m[0:E_PAD].rearrange("(p t) w -> p t w", t=T), ka[:, :, 1:1 + HEADS]).then_inc(s_o, 16)
                        sp.wait_ge(s_o, 16)
                self.join(s, ka[:, T - 1, 1:1 + HEADS], HEADS, self.s_m, True)
            e_d = self.dram("e_d", (N_PAD, 2 * HEADS))
            with ExitStack() as c:
                mx = self.sb(c, "mx", [P, NJ, HEADS])
                self.fetch(self.s_m, last_s, mx)
                with ExitStack() as cc:
                    block = cc.enter_context(nc.Block())

                    @block.vector
                    def _(v):
                        nc.vector.tensor_tensor(mx[:], mx[:], ab[:, :, 0:HEADS], ALU.add)
                        v.drain()
                        nc.vector.scalar_tensor_tensor(ab[:, :, HEADS:], mx[:], 0.2, mx[:], ALU.mult, ALU.max)
                self.spread(self.z_e, first_s, ab, e_d)
            tail = self.sb(o_ctx, "tail", [P, W_V])
            self.attention_edges(s, tail, key0, e_d, ssv)
            self.join(s, tail, W_V, self.s_v, False)
            with ExitStack() as c:
                r = self.sb(c, "r", [P, NJ, W_V])
                self.fetch(self.s_v, last_s, r)
                self.attention_nodes(r)

    def attention_edges(self, s, tail, key0, e_d, ssv):
        nc = self.nc
        ze = self.z_e[0:E_PAD].rearrange("(p t) w -> p t w", t=T)
        sv = self.s_v[0:E_PAD].rearrange("(p t) w -> p t w", t=T)
        with ExitStack() as c:
            row = self.sb(c, "row", [P, 2, TB, W_SS])
            ex = self.sb(c, "ex", [P, 2, TB, 2 * HEADS])
            ecar = self.sb(c, "ecar", [P, 2 * HEADS])
            V = self.sb(c, "V", [P, 2, TB, W_V])
            e = self.sb(c, "e", [P, 2, TB, HEADS])
            p = self.sb(c, "p", [P, 2, TB, HEADS])
            cb = self.sb(c, "cb", [P, 2, TB])
            self.first_rows(e_d, key0[:, 0:1], ecar)
            s_ld = [self.sem(c, "s_ld") for _ in range(2)]
            s_st = [self.sem(c, "s_st") for _ in range(2)]
            s_e, s_p, s_r, s_v, tick = (self.sem(c, n) for n in ("s_e", "s_p", "s_r", "s_v", "tick"))
            block = c.enter_context(nc.Block())

            @block.vector
            def _(v):
                nc.vector.memset(tail[:], 0.0)
                with v.Fori(0, NIT) as i:
                    for h in range(2):
                        nc.vector.tensor_copy(cb[:, h, :], s["cont"][:, bass.ds((i * 2 + h) * TB, TB)])
                        hold(v, s_ld[h], (i + 1) * 32, tick)
                        v.drain()
                        for k in range(2 * HEADS):
                            nc.vector.tensor_tensor_scan(ex[:, h, :, k], cb[:, h, :], ex[:, h, :, k], ecar[:, k:k + 1], ALU.mult, ALU.add)
                        v.drain()
                        nc.vector.tensor_copy(ecar[:], ex[:, h, TB - 1, :])
                        nc.vector.tensor_tensor(e[:, h], ex[:, h, :, 0:HEADS], row[:, h, :, 1:1 + HEADS], ALU.add)
                        v.drain()
                        nc.vector.scalar_tensor_tensor(p[:, h], e[:, h], 0.2, e[:, h], ALU.mult, ALU.max)
                        v.drain()
                        nc.vector.tensor_tensor(e[:, h], p[:, h], ex[:, h, :, HEADS:], ALU.subtract)
                        v.drain().then_inc(s_e, 1)
                        hold(v, s_p, i * 2 + h + 1, tick)
                        for k in range(HEADS):
                            nc.vector.tensor_tensor(V[:, h, :, k * F:(k + 1) * F], row[:, h, :, 1 + HEADS:1 + W_XA],
                                                    p[:, h, :, k:k + 1].to_broadcast([P, TB, F]), ALU.mult)
                        nc.vector.tensor_copy(V[:, h, :, HEADS * F:HEADS * F + HEADS], p[:, h])
                        nc.vector.tensor_copy(V[:, h, :, HEADS * F + HEADS:], row[:, h, :, 1 + W_XA:])
                        v.drain().then_inc(s_r, 1)
                        for k in range(W_V):
                            nc.vector.tensor_tensor_scan(V[:, h, :, k], cb[:, h, :], V[:, h, :, k], tail[:, k:k + 1], ALU.mult, ALU.add)
                        v.drain().then_inc(s_v, 1)
                        nc.vector.tensor_copy(tail[:], V[:, h, TB - 1, :])

            @block.scalar
            def _(act):
                with act.Fori(0, NIT) as i:
                    for h in range(2):
                        hold(act, s_e, i * 2 + h + 1, tick)
                        nc.scalar.activation(p[:, h], e[:, h], ACT.Exp).then_inc(s_p, 1)

            @block.sync
            def _(sp):
                def load(i, h):
                    at = bass.ds((i * 2 + h) * TB, TB)
                    sp.dma_start(row[:, h], ssv[:, at, :]).then_inc(s_ld[h], 16)
                    sp.dma_start(ex[:, h], ze[:, at, :]).then_inc(s_ld[h], 16)

                def store(i, h):
                    sp.dma_start(sv[:, bass.ds((i * 2 + h) * TB, TB), :], V[:, h]).then_inc(s_st[h], 16)
                for h in range(2):
                    load(0, h)
                with sp.Fori(0, NIT - 1) as i:
                    for h in range(2):
                        hold(sp, s_v, i * 2 + h + 1, tick)
                        store(i, h)
                        hold(sp, s_st[h], i * 16 + 16, tick)
                        load(i + 1, h)
                for h in range(2):
                    sp.wait_ge(s_v, 2 * (NIT - 1) + h + 1)
                    store(NIT - 1, h)
                for h in range(2):
                    sp.wait_ge(s_st[h], 16 * NIT)

    def attention_nodes(self, r):
        nc, a = self.nc, self.a
        HF = HEADS * F
        with ExitStack() as c:
            w = self.sb(c, "w0", [HF, F])
            y = self.sb(c, "y", [P, NJ, F])
            bias = self.row_of(c, a["L0_gnn_bias"], F)
            d0 = self.sb(c, "d0", [P, NJ, HEADS])
            with ExitStack() as cc:
                s_l = self.sem(cc, "s_l")
                block = cc.enter_context(nc.Block())

                @block.sync
                def _(sp):
                    sp.dma_start(w[:], a["L0_gnn_w"].rearrange("h f o -> (h f) o")).then_inc(s_l, 16)

                @block.vector
                def _(v):
                    den = r[:, :, HF:HF + HEADS]
                    nc.vector.tensor_copy(self.edge_sum[:], r[:, :, HF + HEADS:])
                    nc.vector.tensor_scalar(d0[:], den, 0.0, None, ALU.is_equal)
                    v.drain()
                    nc.vector.tensor_tensor(d0[:], d0[:], den, ALU.add)
                    v.drain()
                    nc.vector.tensor_scalar(d0[:], d0[:], float(HEADS), None, ALU.mult)
                    v.drain()
                    nc.vector.reciprocal(d0[:], d0[:])
                    v.drain()
                    for k in range(HEADS):
                        at = r[:, :, k * F:(k + 1) * F]
                        nc.vector.tensor_tensor(at, at, d0[:, :, k:k + 1].to_broadcast([P, NJ, F]), ALU.mult)
                    v.wait_ge(s_l, 16)

            def post(v, g, po):
                nc.vector.tensor_tensor(y[:, g, :], po[:], self.x[:, g, :], ALU.add)
                v.drain()
                nc.vector.tensor_tensor(y[:, g, :], y[:, g, :], bias[:, 0, :], ALU.add)
            self.dense(r[:, :, 0:HF], 1, HF, F, w[:], post)
            self.norm(y)

    def gather_sum(self, d, y_d, s_dram, tail):
        nc = self.nc
        sv = s_dram[0:E_PAD].rearrange("(p t) w -> p t w", t=T)
        with ExitStack() as c:
            buf = self.sb(c, "buf", [P, 2, TB, HID])
            idx = self.sb(c, "idx", [P, 2, TB], i32)
            cb = self.sb(c, "cb", [P, 2, TB])
            s_g = [self.sem(c, "s_g") for _ in range(2)]
            s_st = [self.sem(c, "s_st") for _ in range(2)]
            s_free = [self.sem(c, "s_free") for _ in range(2)]
            s_i, s_v, tick = (self.sem(c, n) for n in ("s_i", "s_v", "tick"))
            block = c.enter_context(nc.Block())

            @block.scalar
            def _(act):
                with act.Fori(0, NIT) as i:
                    for h in range(2):
                        hold(act, s_free[h], i + 1, tick)
                        nc.scalar.copy(idx[:, h, :], self.src_i[:, bass.ds((i * 2 + h) * TB, TB)]).then_inc(s_i, 1)

            @block.gpsimd
            def _(pool):
                with pool.Fori(0, NIT) as i:
                    for h in range(2):
                        hold(pool, s_i, i * 2 + h + 1, tick)
                        for t in range(TB):
                            nc.gpsimd.indirect_dma_start(buf[:, h, t, :], None, y_d[:, :],
                                                         bass.IndirectOffsetOnAxis(idx[:, h, t:t + 1], 0)).then_inc(s_g[h], 16)

            @block.vector
            def _(v):
                nc.vector.memset(tail[:], 0.0)
                with v.Fori(0, NIT) as i:
                    for h in range(2):
                        nc.vector.tensor_copy(cb[:, h, :], d["cont"][:, bass.ds((i * 2 + h) * TB, TB)])
                        v.drain()
                        hold(v, s_g[h], (i + 1) * (16 * TB), tick)
                        for k in range(HID):
                            nc.vector.tensor_tensor_scan(buf[:, h, :, k], cb[:, h, :], buf[:, h, :, k], tail[:, k:k + 1], ALU.mult, ALU.add)
                        v.drain()
                        nc.vector.tensor_copy(tail[:], buf[:, h, TB - 1, :])
                        v.drain().then_inc(s_v, 1)

            @block.sync
            def _(sp):
                for h in range(2):
                    sp.sem_inc(s_free[h], 1)
                with sp.Fori(0, NIT) as i:
                    for h in range(2):
                        hold(sp, s_v, i * 2 + h + 1, tick)
                        sp.dma_start(sv[:, bass.ds((i * 2 + h) * TB, TB), :], buf[:, h]).then_inc(s_st[h], 16)
                        hold(sp, s_st[h], i * 16 + 16, s_free[h])

    def gin(self, d, last_d):
        nc, a = self.nc, self.a
        with ExitStack() as c:
            y = self.sb(c, "y", [P, NJ, HID])
            h = self.sb(c, "h", [P, NJ, HID])
            r = self.sb(c, "r", [P, NJ, F])
            tail = self.sb(c, "tail", [P, HID])
            w1 = self.block_diagonal(c, a["L1_gnn_W1"], F, HID)
            w2 = self.block_diagonal(c, a["L1_gnn_W2"], HID, F)
            w3 = self.block_diagonal(c, a["L1_gnn_W3"], F, HID)
            w4 = self.block_diagonal(c, a["L1_gnn_W4"], HID, F)
            b1 = self.row_of(c, a["L1_gnn_b1"], HID)
            b2 = self.row_of(c, a["L1_gnn_b2"], F, 4)
            b3 = self.row_of(c, a["L1_gnn_b3"], HID)
            b4 = self.row_of(c, a["L1_gnn_b4"], F, 4)

            def conv(x, w_in, b_in, w_out, post, y_d, s_dram):
                def keep(v, g, po):
                    nc.vector.tensor_copy(y[:, 4 * g:4 * g + 4, :], po[:].rearrange("p (j m) -> p j m", j=4))
                self.dense(x, 4, F, HID, w_in, keep)
                self.spread(None, None, y, y_d)
                self.gather_sum(d, y_d, s_dram, tail)
                self.join(d, tail, HID, s_dram, False)
                self.fetch(s_dram, last_d, h)
                with ExitStack() as cc:
                    block = cc.enter_context(nc.Block())

                    @block.vector
                    def _(v):
                        nc.vector.tensor_tensor(h[:], h[:], y[:], ALU.add)
                        v.drain()
                        nc.vector.tensor_tensor(h[:], h[:], b_in[:].to_broadcast([P, NJ, HID]), ALU.add)
                        v.drain()
                        nc.vector.tensor_scalar(h[:], h[:], 0.0, None, ALU.max)
                self.dense(h, 4, HID, F, w_out, post)

            def post_a(v, g, po):
                at = r[:, 4 * g:4 * g + 4, :]
                nc.vector.tensor_tensor(at, po[:].rearrange("p (j m) -> p j m", j=4), b2[:], ALU.add)
                v.drain()
                nc.vector.tensor_scalar(at, at, 0.0, None, ALU.max)

            def post_b(v, g, po):
                at = r[:, 4 * g:4 * g + 4, :]
                nc.vector.tensor_tensor(at, po[:].rearrange("p (j m) -> p j m", j=4), b4[:], ALU.add)
                v.drain()
                nc.vector.tensor_tensor(at, at, self.x[:, 4 * g:4 * g + 4, :], ALU.add)
            conv(self.x, w1, b1, w2, post_a, self.dram("y1", (N_PAD, HID)), self.s_1)
            conv(r, w3, b3, w4, post_b, self.dram("y2", (N_PAD, HID)), self.s_1b)
            self.norm(r)

    def edge_mlp(self, d, first_d, last_d):
        nc, a = self.nc, self.a
        D = 2 * F + ATTR
        with ExitStack() as top:
            x_d = self.dram("x_d", (N_PAD, F))
            self.spread(self.z_2, first_d, self.x, x_d)
            tail = self.sb(top, "tail", [P, F])
            z = self.z_2[0:E_PAD].rearrange("(p t) w -> p t w", t=T)
            dsv = self.ds.rearrange("(p t) w -> p t w", t=T)
            sv = self.s_2[0:E_PAD].rearrange("(p t) w -> p t w", t=T)
            with ExitStack() as c:
                w1 = self.sb(c, "w1", [D, MID + 1])
                b1 = self.sb(c, "b1", [64, 1])
                w2 = self.sb(c, "w2", [MID + 1, F])
                car = self.sb(c, "car", [P, F])
                et = self.sb(c, "et", [P, 2, TB, D])
                V = self.sb(c, "V", [P, 2, TB, F])
                idx = self.sb(c, "idx", [P, 2, TB], i32)
                cb = self.sb(c, "cb", [P, 2, 2, TB])
                eT = self.sb(c, "eT", [D, 2, 4 * P])
                zT = self.sb(c, "zT", [MID + 1, 2, 4 * P])
                hT = self.sb(c, "hT", [MID + 1, 2, 4 * P])
                pT = [self.ps(c, "pT", [D, 4 * P]) for _ in range(2)]
                p1 = [self.ps(c, "p1", [MID + 1, 4 * P]) for _ in range(2)]
                p2 = self.ps(c, "p2", [P, TB, F])
                self.first_rows(x_d, self.key0_i[:, 0:1], car)
                with ExitStack() as cc:
                    s_m, s_l = self.sem(cc, "s_m"), self.sem(cc, "s_l")
                    block = cc.enter_context(nc.Block())

                    @block.vector
                    def _(v):
                        nc.vector.memset(w1[:], 0.0)
                        nc.vector.memset(b1[:], 1.0)
                        nc.vector.memset(tail[:], -BIG)
                        v.drain().then_inc(s_m, 1)

                    @block.sync
                    def _(sp):
                        sp.wait_ge(s_m, 1)
                        sp.dma_start(w1[:, 0:MID], a["L2_gnn_W1"]).then_inc(s_l, 16)
                        with nc.allow_non_contiguous_dma(reason="one value per partition"):
                            sp.dma_start(b1[0:MID, :], a["L2_gnn_b1"].rearrange("(n o) -> n o", o=1)).then_inc(s_l, 16)
                        sp.dma_start(w2[0:MID, :], a["L2_gnn_W2"]).then_inc(s_l, 16)
                        sp.dma_start(w2[MID:MID + 1, :], a["L2_gnn_b2"].rearrange("(o n) -> o n", o=1)).then_inc(s_l, 16)
                        sp.wait_ge(s_l, 64)
                s_g = [self.sem(c, "s_g") for _ in range(2)]
                s_ld = [self.sem(c, "s_ld") for _ in range(2)]
                s_st = [self.sem(c, "s_st") for _ in range(2)]
                names = ("s_i", "s_f", "s_T", "s_c", "s_1", "s_h", "s_2", "s_y", "s_v", "s_free", "s_z", "tick")
                s_i, s_f, s_T, s_c, s_1, s_h, s_2, s_y, s_v, s_free, s_z, tick = (self.sem(c, n) for n in names)
                block = c.enter_context(nc.Block())
                NQ = TB // 4

                @block.sync
                def _(sp):
                    def load(i, h):
                        at = bass.ds((i * 2 + h) * TB, TB)
                        sp.dma_start(et[:, h, :, F:2 * F], z[:, at, :]).then_inc(s_ld[h], 16)
                        sp.dma_start(et[:, h, :, 2 * F:D], dsv[:, at, 2:2 + ATTR]).then_inc(s_ld[h], 16)

                    def store(i, h):
                        sp.dma_start(sv[:, bass.ds((i * 2 + h) * TB, TB), :], V[:, h]).then_inc(s_st[h], 16)
                    sp.sem_inc(s_free, 1)
                    load(0, 0)
                    sp.sem_inc(s_free, 1)
                    load(0, 1)
                    with sp.Fori(0, NIT - 1) as i:
                        for h in range(2):
                            hold(sp, s_v, i * 2 + h + 1, tick)
                            store(i, h)
                            hold(sp, s_st[h], i * 16 + 16, s_free)
                            load(i + 1, h)
                    for h in range(2):
                        sp.wait_ge(s_v, 2 * (NIT - 1) + h + 1)
                        store(NIT - 1, h)
                    for h in range(2):
                        sp.wait_ge(s_st[h], 16 * NIT)

                @block.gpsimd
                def _(pool):
                    with pool.Fori(0, NIT) as i:
                        for h in range(2):
                            hold(pool, s_i, i * 2 + h + 1, tick)
                            for t in range(TB):
                                nc.gpsimd.indirect_dma_start(et[:, h, t, 0:F], None, x_d[:, :],
                                                             bass.IndirectOffsetOnAxis(idx[:, h, t:t + 1], 0)).then_inc(s_g[h], 16)

                @block.vector
                def _(v):
                    def carry_on(i, h):
                        nc.vector.tensor_copy(cb[:, h, 0, :], d["cont"][:, bass.ds((i * 2 + h) * TB, TB)])
                        nc.vector.tensor_copy(cb[:, h, 1, :], d["contm"][:, bass.ds((i * 2 + h) * TB, TB)])
                        v.drain()
                        for k in range(F):
                            nc.vector.tensor_tensor_scan(et[:, h, :, F + k], cb[:, h, 0, :], et[:, h, :, F + k], car[:, k:k + 1], ALU.mult, ALU.add)
                        v.drain()
                        nc.vector.tensor_copy(car[:], et[:, h, TB - 1, F:2 * F])
                        v.drain().then_inc(s_f, 1)

                    with v.Fori(0, NIT) as i:
                        for h in range(2):
                            hold(v, s_free, i * 2 + h + 1, tick)
                            nc.vector.tensor_copy(idx[:, h, :], self.src_i[:, bass.ds((i * 2 + h) * TB, TB)])
                            v.drain().then_inc(s_i, 1)
                        for h in range(2):
                            hold(v, s_ld[h], (i + 1) * 32, tick)
                            carry_on(i, h)
                        for h in range(2):
                            for q in range(NQ):
                                hold(v, s_z, (i * 2 + h) * NQ + q + 1, tick)
                                nc.vector.scalar_tensor_tensor(hT[:, q % 2, :], zT[:, q % 2, :], 0.01, zT[:, q % 2, :],
                                                               ALU.mult, ALU.max).then_inc(s_h, 1)
                            hold(v, s_y, i * 2 + h + 1, tick)
                            nc.vector.scalar_tensor_tensor(V[:, h], V[:, h], 0.01, V[:, h], ALU.mult, ALU.max)
                            v.drain()
                            for k in range(F):
                                nc.vector.tensor_tensor_scan(V[:, h, :, k], cb[:, h, 1, :], V[:, h, :, k], tail[:, k:k + 1], ALU.min, ALU.max)
                            v.drain()
                            nc.vector.tensor_copy(tail[:], V[:, h, TB - 1, :])
                            v.drain().then_inc(s_v, 1)

                @block.tensor
                def _(pe):
                    with pe.Fori(0, NIT) as i:
                        for h in range(2):
                            hold(pe, s_g[h], (i + 1) * (16 * TB), tick)
                            hold(pe, s_f, i * 2 + h + 1, tick)
                            for q in range(NQ + 2):
                                n = (i * 2 + h) * NQ
                                if q < NQ:
                                    for k in range(4):
                                        mm = nc.tensor.transpose(pT[q % 2][:, k * P:(k + 1) * P], et[:, h, 4 * q + k, :], self.ident[:])
                                    mm.then_inc(s_T, 1)
                                if 1 <= q <= NQ:
                                    hold(pe, s_c, n + q, tick)
                                    nc.tensor.matmul(p1[(q - 1) % 2][:], w1[:], eT[:, (q - 1) % 2, :], start=True, stop=True).then_inc(s_1, 1)
                                if q >= 2:
                                    hold(pe, s_h, n + q - 1, tick)
                                    if q == 2:
                                        hold(pe, s_free, i * 2 + h + 1, tick)
                                    for k in range(4):
                                        mm = nc.tensor.matmul(p2[:, 4 * (q - 2) + k, :], hT[:, (q - 2) % 2, k * P:(k + 1) * P], w2[:],
                                                              start=True, stop=True)
                            mm.then_inc(s_2, 1)
                            hold(pe, s_y, i * 2 + h + 1, tick)

                @block.scalar
                def _(act):
                    with act.Fori(0, NIT) as i:
                        for h in range(2):
                            n = (i * 2 + h) * NQ
                            for q in range(NQ + 1):
                                if q < NQ:
                                    hold(act, s_T, n + q + 1, tick)
                                    nc.scalar.copy(eT[:, q % 2, :], pT[q % 2][:]).then_inc(s_c, 1)
                                if q >= 1:
                                    hold(act, s_1, n + q, tick)
                                    nc.scalar.activation(zT[:, (q - 1) % 2, :], p1[(q - 1) % 2][:], ACT.Identity,
                                                         bias=b1[0:MID + 1, 0:1]).then_inc(s_z, 1)
                            hold(act, s_2, i * 2 + h + 1, tick)
                            for k in range(2):
                                o = slice(k * TB // 2, (k + 1) * TB // 2)
                                last = nc.scalar.copy(V[:, h, o, :], p2[:, o, :])
                            last.then_inc(s_y, 1)
            self.join(d, tail, F, self.s_2, True)
            with ExitStack() as c:
                y = self.sb(c, "y", [P, NJ, F])
                self.fetch(self.s_2, last_d, y)
                with ExitStack() as cc:
                    block = cc.enter_context(nc.Block())

                    @block.vector
                    def _(v):
                        nc.vector.tensor_tensor(y[:], y[:], self.x[:], ALU.max)
                        v.drain()
                        nc.vector.tensor_tensor(y[:], y[:], self.x[:], ALU.add)
                self.norm(y)

    def finish(self):
        nc = self.nc
        with ExitStack() as c:
            y = self.sb(c, "y", [P, NJ, F])
            with ExitStack() as cc:
                block = cc.enter_context(nc.Block())

                @block.vector
                def _(v):
                    nc.vector.tensor_tensor(y[:], self.x[:], self.edge_sum[:], ALU.add)
            self.norm(y)
            s_o = self.sem(c, "s_o")
            block = c.enter_context(nc.Block())

            @block.sync
            def _(sp):
                for lo, hi in SPLITS:
                    sp.dma_start(self.out.rearrange("(p j) f -> p j f", j=NJ)[lo:hi], self.x[lo:hi]).then_inc(s_o, 16)
                sp.wait_ge(s_o, 32)

    def program(self):
        with ExitStack() as top:
            self.setup(top)
            self.edge_sum = self.sb(top, "edge_sum", [P, NJ, F])
            first_d, last_d = self.sb(top, "first_d", [P, NJ], i32), self.sb(top, "last_d", [P, NJ], i32)
            self.sort_by_dst(first_d, last_d)
            d = self.dst_order(top)
            self.attention(d, first_d)
            self.gin(d, last_d)
            self.edge_mlp(d, first_d, last_d)
            self.finish()


_INS = ["x", "src", "dst", "edge_attr_16", "edge_attr_32", "L0_gnn_w", "L0_gnn_fc_w", "L0_gnn_fc_b", "L0_gnn_bias",
        "L1_gnn_W1", "L1_gnn_b1", "L1_gnn_W2", "L1_gnn_b2", "L1_gnn_W3", "L1_gnn_b3", "L1_gnn_W4", "L1_gnn_b4",
        "L2_gnn_W1", "L2_gnn_b1", "L2_gnn_W2", "L2_gnn_b2"]


def kernel(**inputs):
    import numpy as _np
    import concourse.bacc as _bacc
    from concourse.bass_utils import run_bass_kernel_spmd as _run

    nc = _bacc.Bacc("TRN2", target_bir_lowering=False, num_devices=1)
    arrays, args = {}, {}
    for name in _INS:
        a = _np.ascontiguousarray(inputs[name])
        arrays[f"in_{name}_dram"] = a
        args[name] = nc.dram_tensor(f"in_{name}_dram", a.shape, mybir.dt.from_np(a.dtype), kind="ExternalInput").ap()
    out = nc.dram_tensor("out_0_dram", (N, F), f32, kind="ExternalOutput").ap()
    Build(nc, args, out).program()
    r = _run(nc, [arrays], core_ids=[0])
    return r.results[0]["out_0_dram"]
```

```python
import concourse.bass as bass
from concourse import mybir
from contextlib import ExitStack

f32 = mybir.dt.float32
bf16 = mybir.dt.bfloat16
i32 = mybir.dt.int32
ALU = mybir.AluOpType
ACT = mybir.ActivationFunctionType
AX = mybir.AxisListType

P = 128
N, E, F, HEADS, HID = 12500, 200000, 32, 4, 16
ATTR, MID = 16, 56
NJ = 100
NP_REAL = N // NJ
T = 1600
EP_REAL = E // T
N_PAD, E_PAD = P * NJ, P * T
TB = 32
NIT = T // (2 * TB)
LAST = NIT - 1
CH = 8
STEPS = TB // CH
BIG = 3.4e38
MAGIC = 12582912.0
W_DS = 2 + ATTR + F
W_XA = HEADS + F
W_SS = 1 + W_XA + F
W_V = HEADS * F + HEADS + F
BY_POOL, BY_ACT = 2, 3
POOL_HEADS = 4
TBA = 50
SPLITS = ((0, 112), (112, 125))


def hold(eng, sem, value, tick):
    eng.wait_ge(sem, value)
    if not isinstance(value, int):
        eng.sem_inc(tick, 1)


class SpreadFill:

    def __init__(self, b, c, d, z, table):
        self.b, self.d, self.z = b, d, z
        self.zt = b.sb(c, "zt", [P, 2, TB, W_XA])
        self.carry = b.sb(c, "carry", [P, W_XA])
        self.cb = b.sb(c, "cb", [P, TB])
        b.first_rows(table, b.key0_i[:, 0:1], self.carry)
        self.s_z = [b.sem(c, "s_zl") for _ in range(2)]
        self.s_f, self.s_d, self.tick = (b.sem(c, n) for n in ("s_f", "s_d", "tick"))

    def load(self, sp, i, h):
        sp.dma_start(self.zt[:, h], self.z[:, bass.ds((i * 2 + h) * TB, TB), :]).then_inc(self.s_z[h], 16)

    def free(self, sp, i, h):
        hold(sp, self.s_d, i * 2 + h + 1, self.tick)

    def columns(self, v, i, h, lo, hi):
        nc = self.b.nc
        if lo == 0:
            hold(v, self.s_z[h], (i + 1) * 16, self.tick)
            v.drain()
            nc.vector.tensor_copy(self.cb[:], self.d["cont"][:, bass.ds((i * 2 + h) * TB, TB)])
            v.drain()
        for f in range(lo, hi):
            nc.vector.tensor_tensor_scan(self.zt[:, h, :, f], self.cb[:], self.zt[:, h, :, f], self.carry[:, f:f + 1], ALU.mult, ALU.add)
        if hi == W_XA:
            v.drain()
            nc.vector.tensor_copy(self.carry[:], self.zt[:, h, TB - 1, :]).then_inc(self.s_f, 1)

    def first(self, v):
        self.columns(v, 0, 0, 0, W_XA)

    def scan(self, v, i, s):
        n = W_XA // STEPS
        h, k = s // STEPS, s % STEPS
        if h == 0:
            self.columns(v, i, 1, k * n, (k + 1) * n)
        else:
            self.columns(v, i + 1, 0, k * n, (k + 1) * n)

    def deliver(self, act, i, h, pay):
        hold(act, self.s_f, i * 2 + h + 1, self.tick)
        self.b.nc.scalar.copy(pay[:, h, :, 1:1 + W_XA], self.zt[:, h]).then_inc(self.s_d, 1)


class Build:
    def __init__(self, nc, a, out):
        self.nc, self.a, self.out, self.n, self.owned = nc, a, out, 0, {}

    def sb(self, ctx, name, shape, dt=f32):
        self.n += 1
        return ctx.enter_context(self.nc.sbuf_tensor(f"{name}_{self.n}", shape, dt))

    def ps(self, ctx, name, shape, dt=f32):
        self.n += 1
        return ctx.enter_context(self.nc.psum_tensor(f"{name}_{self.n}", shape, dt))

    def sem(self, ctx, name):
        self.n += 1
        s = self.nc.alloc_semaphore(f"{name}_{self.n}")
        if id(ctx) not in self.owned:
            self.owned[id(ctx)] = []
            ctx.callback(self.release, id(ctx))
        self.owned[id(ctx)].append(s)
        return s

    def release(self, key):
        self.nc.clear_and_free_semaphores(self.owned.pop(key))
        self.nc.all_engine_barrier()

    def dram(self, name, shape, dt=f32):
        return self.nc.dram_tensor(name, shape, dt, kind="Internal").ap()

    def setup(self, ctx):
        nc, a = self.nc, self.a
        sb = lambda name, shape, dt=f32: self.sb(ctx, name, shape, dt)
        self.irow = sb("irow", [P, P])
        self.ipart = sb("ipart", [P, 1])
        self.inode = sb("inode", [P, NJ])
        self.irow_b = sb("irow_b", [P, P], bf16)
        self.ident = sb("ident", [P, P])
        self.ident_b = sb("ident_b", [P, P], bf16)
        self.tri = sb("tri", [P, P])
        self.tri_b = sb("tri_b", [P, P], bf16)
        self.ones = sb("ones", [P, P])
        self.x = sb("x", [P, NJ, F])
        self.zero = sb("zero", [P, T // 2])
        self.edge = sb("edge", [P, T + 2 * CH, 2])
        self.z_x = self.dram("z_x", (E_PAD + N_PAD, W_XA))
        self.z_e = self.dram("z_e", (E_PAD + N_PAD, 2 * HEADS))
        self.z_2 = self.dram("z_2", (E_PAD + N_PAD, F))
        self.s_v = self.dram("s_v", (E_PAD + 1, W_V))
        self.s_m = self.dram("s_m", (E_PAD + 1, HEADS))
        self.s_1 = self.dram("s_1", (E_PAD + 1, HID))
        self.s_1b = self.dram("s_1b", (E_PAD + 1, HID))
        self.s_2 = self.dram("s_2", (E_PAD + 1, F))
        with ExitStack() as c:
            ki = self.sb(c, "ki", [P, 2, T], i32)
            s_in, s_io, s_ms = (self.sem(c, n) for n in ("s_in", "s_io", "s_ms"))
            self.s_z = self.sem(ctx, "s_z")
            block = c.enter_context(nc.Block())

            @block.gpsimd
            def _(pool):
                nc.gpsimd.iota(self.irow[:], [[1, P]], base=0, channel_multiplier=0,
                               allow_small_or_imprecise_dtypes=True)
                nc.gpsimd.iota(self.ipart[:], [[1, 1]], base=0, channel_multiplier=1,
                               allow_small_or_imprecise_dtypes=True)
                nc.gpsimd.iota(self.inode[:], [[1, NJ]], base=0, channel_multiplier=NJ,
                               allow_small_or_imprecise_dtypes=True)
                pool.drain().then_inc(s_io, 1)

            @block.vector
            def _(v):
                nc.vector.memset(self.zero[:], 0.0)
                nc.vector.memset(self.x[:], 0.0)
                nc.vector.memset(self.ones[:], 1.0)
                nc.vector.memset(ki[:], N)
                nc.vector.memset(self.edge[:], float(N))
                v.drain().then_inc(s_ms, 1)
                v.wait_ge(s_io, 1)
                nc.vector.tensor_scalar(self.ident[:], self.irow[:], self.ipart[:, 0:1], None, ALU.is_equal)
                nc.vector.tensor_scalar(self.tri[:], self.irow[:], self.ipart[:, 0:1], None, ALU.is_gt)
                nc.vector.tensor_scalar(self.ident_b[:], self.irow[:], self.ipart[:, 0:1], None, ALU.is_equal)
                nc.vector.tensor_scalar(self.tri_b[:], self.irow[:], self.ipart[:, 0:1], None, ALU.is_gt)
                nc.vector.tensor_copy(self.irow_b[:], self.irow[:])
                v.wait_ge(s_in, 16 * 6)
                nc.vector.tensor_copy(self.edge[:, 0:T, 0], ki[:, 0, :])
                nc.vector.tensor_copy(self.edge[:, 0:T, 1], ki[:, 1, :])

            @block.sync
            def _(sp):
                sp.wait_ge(s_ms, 1)
                for lo, hi in SPLITS:
                    sp.dma_start(self.x[lo:hi], a["x"].rearrange("(p j) f -> p j f", j=NJ)[lo:hi]).then_inc(s_in, 16)
                    for k, name in ((0, "dst"), (1, "src")):
                        sp.dma_start(ki[lo:hi, k, :], a[name].rearrange("(p t) -> p t", t=T)[lo:hi]).then_inc(s_in, 16)

    def csr(self, ctx, digits, which, C, first, last):
        nc = self.nc
        kp, kj = digits
        with ExitStack() as c:
            H = self.sb(c, "H", [P, CH, NJ])
            cnt, incl, start, full, t1, t2 = (self.sb(c, n, [P, NJ]) for n in ("cnt", "incl", "start", "full", "t1", "t2"))
            kbp = self.sb(c, "kbp", [P, 2 * TB])
            kbj = self.sb(c, "kbj", [P, 2 * TB])
            kbv = self.sb(c, "kbv", [P, 2 * TB])
            nkb = self.sb(c, "nkb", [P, 2 * TB])
            sq = self.sb(c, "sq", [P, BY_ACT, P])
            ohp = self.sb(c, "ohp", [P, 2, CH, P], bf16)
            ohj = self.sb(c, "ohj", [P, 2, CH, P], bf16)
            Hp = self.ps(c, "Hp", [P, 2, CH, P])
            pre = self.ps(c, "pre", [P, 1])
            names = ("s_dig", "s_kp", "s_oa", "s_oj", "s_op", "s_mm", "s_add", "s_rs", "s_pre", "tick")
            s_dig, s_kp, s_oa, s_oj, s_op, s_mm, s_add, s_rs, s_pre, tick = (self.sem(c, n) for n in names)
            block = c.enter_context(nc.Block())
            NS = 2 * STEPS
            GS = NS // 2

            @block.vector
            def _(v):
                key = self.edge[:, :, which]
                nc.vector.memset(H[:], 0.0)
                nc.vector.memset(Hp[:, 1], 0.0)
                nc.vector.tensor_scalar(kp[:], key, 1.0 / NJ, -0.495, ALU.mult, ALU.add)
                v.drain()
                nc.vector.tensor_scalar(kp[:], kp[:], MAGIC, MAGIC, ALU.add, ALU.subtract)
                v.drain().then_inc(s_dig, 1)
                nc.vector.scalar_tensor_tensor(kj[:], kp[:], -float(NJ), key, ALU.mult, ALU.add)
                v.drain()
                with v.Fori(0, NIT) as i:
                    nc.vector.tensor_copy(kbj[:], kj[:, bass.ds(i * 2 * TB, 2 * TB)])
                    nc.vector.tensor_copy(kbv[:], kp[:, bass.ds(i * 2 * TB, 2 * TB)])
                    v.drain()
                    for s in range(NS):
                        hold(v, s_mm, i * NS + s + 1, tick)
                        for k in range(CH):
                            oh = nc.vector.tensor_scalar(ohj[:, s % 2, k, 0:NJ], self.irow_b[:, 0:NJ],
                                                         kbj[:, s * CH + k:s * CH + k + 1], None, ALU.is_equal)
                        for k in range(BY_POOL + BY_ACT, CH):
                            oh = nc.vector.tensor_scalar(ohp[:, s % 2, k, :], self.irow_b[:], kbv[:, s * CH + k:s * CH + k + 1], None, ALU.is_equal)
                        oh.then_inc(s_oj, 1)
                        if s % GS == 1:
                            nc.vector.tensor_tensor(H[:], H[:], Hp[:, (s // GS + 1) % 2, :, 0:NJ], ALU.add)
                            v.drain().then_inc(s_add, 1)
                    v.drain()
                v.wait_ge(s_mm, NIT * NS + 2)
                nc.vector.tensor_tensor(H[:], H[:], Hp[:, 1, :, 0:NJ], ALU.add)
                v.drain()
                nc.vector.tensor_tensor(cnt[:], H[:, 0, :], H[:, 1, :], ALU.add)
                for k in range(2, CH):
                    v.drain()
                    nc.vector.tensor_tensor(cnt[:], cnt[:], H[:, k, :], ALU.add)
                v.drain()
                nc.vector.tensor_tensor_scan(incl[:], self.ones[:, 0:NJ], cnt[:], 0.0, ALU.mult, ALU.add)
                v.drain().then_inc(s_rs, 1)
                v.wait_ge(s_pre, 1)
                nc.vector.tensor_tensor(start[:], incl[:], cnt[:], ALU.subtract)
                v.drain()
                nc.vector.tensor_scalar(start[:], start[:], pre[:, 0:1], None, ALU.add)
                nc.vector.tensor_scalar(full[:], cnt[:], 0.0, None, ALU.is_gt)
                v.drain()
                nc.vector.tensor_copy(C[:, 0, :], start[:])
                for k in range(1, CH):
                    v.drain()
                    nc.vector.tensor_tensor(C[:, k, :], C[:, k - 1, :], H[:, k - 1, :], ALU.add)
                nc.vector.tensor_scalar(t1[:], self.inode[:], float(E_PAD), None, ALU.add)
                nc.vector.scalar_tensor_tensor(t2[:], start[:], -1.0 - E_PAD, cnt[:], ALU.add, ALU.add)
                v.drain()
                nc.vector.tensor_tensor(start[:], start[:], t1[:], ALU.subtract)
                nc.vector.tensor_tensor(t2[:], t2[:], full[:], ALU.mult)
                v.drain()
                nc.vector.tensor_tensor(start[:], start[:], full[:], ALU.mult)
                nc.vector.tensor_scalar(last[:], t2[:], float(E_PAD), None, ALU.add)
                v.drain()
                nc.vector.tensor_tensor(first[:], start[:], t1[:], ALU.add)

            @block.gpsimd
            def _(pool):
                pool.wait_ge(s_dig, 1)
                with pool.Fori(0, NIT) as i:
                    hold(pool, s_mm, i * NS + 2, tick)
                    nc.gpsimd.tensor_copy(kbp[:], kp[:, bass.ds(i * 2 * TB, 2 * TB)]).then_inc(s_kp, 1)
                    hold(pool, s_kp, i + 1, tick)
                    for s in range(NS):
                        hold(pool, s_mm, i * NS + s + 1, tick)
                        for k in range(BY_POOL):
                            oh = nc.gpsimd.tensor_scalar(ohp[:, s % 2, k, :], self.irow_b[:], kbp[:, s * CH + k:s * CH + k + 1], None, ALU.is_equal)
                        oh.then_inc(s_op, 1)

            @block.scalar
            def _(act):
                act.wait_ge(s_dig, 1)
                with act.Fori(0, NIT) as i:
                    nc.scalar.activation(nkb[:], kp[:, bass.ds(i * 2 * TB, 2 * TB)], ACT.Copy, scale=-1.0)
                    for s in range(NS):
                        act.drain()
                        for k in range(BY_ACT):
                            t = s * CH + BY_POOL + k
                            nc.scalar.activation(sq[:, k, :], self.irow[:], ACT.Square, bias=nkb[:, t:t + 1])
                        act.drain()
                        hold(act, s_mm, i * NS + s + 1, tick)
                        nc.scalar.activation(ohp[:, s % 2, BY_POOL:BY_POOL + BY_ACT, :], sq[:], ACT.Relu, bias=1.0, scale=-1.0).then_inc(s_oa, 1)
                    act.drain()

            @block.tensor
            def _(pe):
                pe.sem_inc(s_mm, 1)
                pe.sem_inc(s_mm, 1)
                pe.sem_inc(s_add, 1)
                with pe.Fori(0, NIT) as i:
                    for s in range(NS):
                        hold(pe, s_oj, i * NS + s + 1, tick)
                        hold(pe, s_op, i * NS + s + 1, tick)
                        hold(pe, s_oa, i * NS + s + 1, tick)
                        if s % GS == 0:
                            hold(pe, s_add, i * 2 + s // GS + 1, tick)
                        for k in range(CH):
                            mm = nc.tensor.matmul(Hp[:, s // GS, k, 0:NJ], ohp[:, s % 2, k, :], ohj[:, s % 2, k, 0:NJ],
                                                  start=(s % GS == 0 and k % 4 == 0), stop=(s % GS == GS - 1),
                                                  skip_group_check=True)
                        mm.then_inc(s_mm, 1)
                pe.wait_ge(s_rs, 1)
                nc.tensor.matmul(pre[:], self.tri[:], incl[:, NJ - 1:NJ], start=True, stop=True).then_inc(s_pre, 1)

    def sort(self, digits, C, W, rows, prepare, loads):
        nc = self.nc
        kp, kj = digits
        with ExitStack() as c:
            pay = self.sb(c, "pay", [P, 2, TB, W])
            pos = self.sb(c, "pos", [P, 2, TB], i32)
            kb = self.sb(c, "kb", [P, 2, 2 * TB + 2 * CH])
            ohp = self.sb(c, "ohp", [P, 4, CH, P], bf16)
            ohj = self.sb(c, "ohj", [P, 4, CH, P], bf16)
            ohT = self.sb(c, "ohT", [P, 2, CH, P])
            ohTb = self.sb(c, "ohTb", [P, 2, CH, P], bf16)
            Lm = self.sb(c, "Lm", [P, CH, P], bf16)
            g = self.sb(c, "g", [P, 2, CH, NJ])
            posf = self.sb(c, "posf", [P, CH])
            pT = self.ps(c, "pT", [P, CH, P], bf16)
            pS = self.ps(c, "pS", [P, CH, P])
            pD = self.ps(c, "pD", [P, CH, P])
            pG = self.ps(c, "pG", [P, CH, P])
            names = ("s_oh", "s_T", "s_cp", "s_S", "s_L", "s_G", "s_C", "s_D", "s_pos", "tick", "s_pre")
            s_oh, s_T, s_cp, s_S, s_L, s_G, s_C, s_D, s_pos, tick, s_prep = (self.sem(c, n) for n in names)
            s_ld = [self.sem(c, "s_ld") for _ in range(2)]
            s_sc = [self.sem(c, "s_sc") for _ in range(2)]
            s_free = [self.sem(c, "s_free") for _ in range(2)]
            s_pay = self.sem(c, "s_pay")
            fill = prepare(c)
            nload = loads(None, None, None, None)
            nkey = 1 if fill else 2
            block = c.enter_context(nc.Block())
            NS = 2 * STEPS
            target = rows

            @block.vector
            def _(v):
                def onehots(s, buf):
                    for k in range(CH):
                        t = s * CH + k
                        nc.vector.tensor_scalar(ohp[:, buf, k, :], self.irow_b[:], kb[:, 0, t:t + 1], None, ALU.is_equal)
                        nc.vector.tensor_scalar(ohj[:, buf, k, 0:NJ], self.irow_b[:, 0:NJ], kb[:, 1, t:t + 1], None, ALU.is_equal)
                    v.drain().then_inc(s_oh, 1)

                def place(i, s):
                    h, o = s // STEPS, (s % STEPS) * CH
                    if s % STEPS == 0:
                        hold(v, s_ld[h], (i + 1) * (16 * nload), tick)
                    v.drain()
                    nc.vector.tensor_reduce(posf[:], g[:, s % 2], AX.X, ALU.add)
                    v.drain()
                    nc.vector.tensor_copy(pos[:, h, o:o + CH], posf[:]).then_inc(s_pos, 1)

                nc.vector.memset(pay[:], 0.0)
                nc.vector.tensor_copy(kb[:, 0, 0:2 * CH], kp[:, 0:2 * CH])
                nc.vector.tensor_copy(kb[:, 1, 0:2 * CH], kj[:, 0:2 * CH])
                v.drain().then_inc(s_prep, 1)
                onehots(0, 0)
                onehots(1, 1)
                v.drain()
                if fill:
                    fill.first(v)
                def round_(i):
                    nc.vector.tensor_copy(kb[:, 0, :], kp[:, bass.ds(i * 2 * TB, 2 * TB + 2 * CH)])
                    nc.vector.tensor_copy(kb[:, 1, :], kj[:, bass.ds(i * 2 * TB, 2 * TB + 2 * CH)])
                    for s in range(NS):
                        h = s // STEPS
                        hold(v, s_S, i * NS + s + 1, tick)
                        nc.vector.tensor_tensor(Lm[:], pS[:], self.tri_b[:].unsqueeze(1).to_broadcast([P, CH, P]), ALU.mult).then_inc(s_L, 1)
                        if s > 0:
                            place(i, s - 1)
                        else:
                            v.drain()
                        onehots(s + 2, (s + 2) % 4)
                        if fill and not (isinstance(i, int) and s >= STEPS):
                            fill.scan(v, i, s)
                        hold(v, s_G, i * NS + s + 1, tick)
                        hold(v, s_D, i * NS + s + 1, tick)
                        nc.vector.tensor_tensor(C[:], C[:], pD[:, :, 0:NJ], ALU.add).then_inc(s_C, 1)
                        nc.vector.tensor_tensor(g[:, s % 2], pG[:, :, 0:NJ], ohj[:, s % 4, :, 0:NJ], ALU.mult)
                    v.drain()
                    place(i, NS - 1)
                    v.drain()

                with v.Fori(0, LAST) as i:
                    round_(i)
                round_(LAST)

            @block.scalar
            def _(act):
                def copies(buf):
                    nc.scalar.copy(ohTb[:, buf], pT[:])
                    nc.scalar.copy(ohT[:, buf], pT[:]).then_inc(s_cp, 1)
                for n in range(2):
                    act.wait_ge(s_T, n + 1)
                    copies(n)
                with act.Fori(0, NIT) as i:
                    for s in range(NS):
                        h = s // STEPS
                        if s % STEPS == 0:
                            hold(act, s_ld[h], (i + 1) * (16 * nload), tick)
                            at = bass.ds((i * 2 + h) * TB, TB)
                            if fill:
                                fill.deliver(act, i, h, pay)
                            nc.scalar.copy(pay[:, h, :, 0:nkey], self.edge[:, at, 2 - nkey:2]).then_inc(s_pay, 1)
                        hold(act, s_T, i * NS + s + 3, tick)
                        copies(s % 2)

            @block.tensor
            def _(pe):
                def turn(buf):
                    for k in range(CH):
                        mm = nc.tensor.transpose(pT[:, k, :], ohp[:, buf, k, :], self.ident_b[:])
                    mm.then_inc(s_T, 1)

                def pairs(buf):
                    for k in range(CH):
                        mm = nc.tensor.matmul(pS[:, k, :], ohTb[:, buf, k, :], ohTb[:, buf, k, :], start=True, stop=True)
                    mm.then_inc(s_S, 1)

                def counts(buf):
                    for k in range(CH):
                        mm = nc.tensor.matmul(pD[:, k, 0:NJ], ohp[:, buf, k, :], ohj[:, buf, k, 0:NJ], start=True, stop=True)
                    mm.then_inc(s_D, 1)

                pe.wait_ge(s_oh, 1)
                turn(0)
                pe.wait_ge(s_cp, 1)
                pairs(0)
                counts(0)
                pe.wait_ge(s_oh, 2)
                turn(1)
                with pe.Fori(0, NIT) as i:
                    for s in range(NS):
                        hold(pe, s_L, i * NS + s + 1, tick)
                        for k in range(CH):
                            nc.tensor.matmul(pG[:, k, 0:NJ], ohT[:, s % 2, k, :], C[:, k, :], start=True, stop=False)
                            mm = nc.tensor.matmul(pG[:, k, 0:NJ], Lm[:, k, :], ohj[:, s % 4, k, 0:NJ], start=False, stop=True)
                        mm.then_inc(s_G, 1)
                        hold(pe, s_cp, i * NS + s + 2, tick)
                        pairs((s + 1) % 2)
                        hold(pe, s_C, i * NS + s + 1, tick)
                        counts((s + 1) % 4)
                        hold(pe, s_oh, i * NS + s + 3, tick)
                        turn((s + 2) % 4)

            @block.gpsimd
            def _(pool):
                with pool.Fori(0, NIT) as i:
                    for s in range(NS):
                        h = s // STEPS
                        if s % STEPS == 0:
                            hold(pool, s_pay, i * 2 + h + 1, tick)
                        hold(pool, s_pos, i * NS + s + 1, tick)
                        for k in range(CH):
                            t = (s % STEPS) * CH + k
                            nc.gpsimd.indirect_dma_start(target[:, :], bass.IndirectOffsetOnAxis(pos[:, h, t:t + 1], 0),
                                                         pay[:, h, t, :], None).then_inc(s_sc[h], 16)
                for h in range(2):
                    pool.wait_ge(s_sc[h], NIT * TB * 16)

            @block.sync
            def _(sp):
                sp.wait_ge(s_prep, 1)
                for h in range(2):
                    loads(sp, 0, h, (pay, s_ld[h]))
                    if fill:
                        fill.load(sp, 0, h)
                with sp.Fori(0, NIT - 1) as i:
                    for h in range(2):
                        if fill:
                            fill.free(sp, i, h)
                            fill.load(sp, i + 1, h)
                        hold(sp, s_sc[h], (i + 1) * (TB * 16), tick)
                        loads(sp, i + 1, h, (pay, s_ld[h]))

    def sort_by_dst(self, first_d, last_d):
        nc, a = self.nc, self.a
        self.ds = self.dram("ds", (E_PAD, W_DS))
        a16 = a["edge_attr_16"].rearrange("(p t) f -> p t f", t=T)
        a32 = a["edge_attr_32"].rearrange("(p t) f -> p t f", t=T)
        dsv = self.ds.rearrange("(p t) w -> p t w", t=T)
        with ExitStack() as c:
            digits = [self.sb(c, n, [P, T + 2 * CH]) for n in ("kp", "kj")]
            C = self.sb(c, "C", [P, CH, NJ])
            falls = self.sb(c, "falls", [P, 1], i32)
            self.lay_down(falls, dsv, a16, a32)
            self.csr(c, digits, 0, C, first_d, last_d)

            def loads(sp, i, h, to):
                if sp is not None:
                    pay, done = to
                    at = bass.ds((i * 2 + h) * TB, TB)
                    for lo, hi in SPLITS:
                        sp.dma_start(pay[lo:hi, h, :, 2:2 + ATTR], a16[lo:hi, at, :]).then_inc(done, 16)
                        sp.dma_start(pay[lo:hi, h, :, 2 + ATTR:W_DS], a32[lo:hi, at, :]).then_inc(done, 16)
                return 4

            self.laid_down()
            unsorted = nc.values_load(falls[0:1, 0:1], min_val=0, max_val=E_PAD)
            with nc.If(unsorted > 0):
                self.sort(digits, C, W_DS, self.ds, lambda c: None, loads)
                self.reload_keys()

    def reload_keys(self):
        nc = self.nc
        with ExitStack() as c:
            s_l = self.sem(c, "s_l")
            block = c.enter_context(nc.Block())

            @block.sync
            def _(sp):
                with nc.allow_non_contiguous_dma(reason="key columns of the sorted rows"):
                    sp.dma_start(self.edge[:, 0:T, :], self.ds.rearrange("(p t) w -> p t w", t=T)[:, :, 0:2]).then_inc(s_l, 16)
                sp.wait_ge(s_l, 16)

    def lay_down(self, falls, dsv, a16, a32):
        nc = self.nc
        self.s_lay = self.sem(self.top, "s_lay")
        with ExitStack() as c:
            prev, last, n = (self.sb(c, k, [P, 1]) for k in ("prev", "lastk", "n"))
            lt = self.sb(c, "lt", [P, T])
            pn = self.ps(c, "pn", [P, 1])
            s_a, s_b, s_n, s_m = (self.sem(c, k) for k in ("s_a", "s_b", "s_n", "s_m"))
            block = c.enter_context(nc.Block())

            @block.vector
            def _(v):
                key = self.edge[:, 0:T, 0]
                nc.vector.memset(prev[:], -1.0)
                nc.vector.tensor_copy(last[:], key[:, T - 1:T])
                v.drain().then_inc(s_a, 1)
                nc.vector.tensor_tensor(lt[:, 1:T], key[:, 1:T], key[:, 0:T - 1], ALU.is_lt)
                v.wait_ge(s_b, 16)
                nc.vector.tensor_tensor(lt[:, 0:1], key[:, 0:1], prev[:], ALU.is_lt)
                v.drain()
                nc.vector.reduce_sum(n[:], lt[:], AX.X)
                v.drain().then_inc(s_n, 1)
                v.wait_ge(s_m, 1)
                nc.vector.tensor_copy(falls[:], pn[:])

            @block.tensor
            def _(pe):
                pe.wait_ge(s_n, 1)
                nc.tensor.matmul(pn[:], self.ones[:], n[:], start=True, stop=True).then_inc(s_m, 1)

            @block.sync
            def _(sp):
                sp.wait_ge(s_a, 1)
                sp.dma_start(prev[1:P, :], last[0:P - 1, :]).then_inc(s_b, 16)
                sp.wait_ge(s_b, 16)
                n = 0
                for z in (self.z_x, self.z_e, self.z_2):
                    w = z.shape[1]
                    rows = z[0:E_PAD].rearrange("(p t) w -> p (t w)", p=P)
                    for k in range(2 * w):
                        sp.dma_start(rows[:, k * T // 2:(k + 1) * T // 2], self.zero[:]).then_inc(self.s_z, 16)
                        n += 1
                for s in (self.s_v, self.s_m, self.s_1, self.s_1b, self.s_2):
                    sp.dma_start(s[E_PAD:E_PAD + 1, :], self.zero[0:1, 0:s.shape[1]]).then_inc(self.s_z, 16)
                    n += 1
                self.zeroed = 16 * n

            @block.scalar
            def _(act):
                act.wait_ge(s_b, 16)
                pads = self.ds[E:E_PAD].rearrange("a w -> (a w)").rearrange("(p c) -> p c", p=P)
                piece = pads.shape[1] // 3
                for k in range(3):
                    act.dma_start(pads[:, k * piece:(k + 1) * piece], self.zero[:, 0:piece]).then_inc(self.s_lay, 16)
                act.wait_ge(self.s_lay, 48)
                with nc.allow_non_contiguous_dma(reason="key columns"):
                    act.dma_start(dsv[:, :, 0:2], self.edge[:, 0:T, :]).then_inc(self.s_lay, 16)
                for lo, hi in SPLITS:
                    act.dma_start(dsv[lo:hi, :, 2:2 + ATTR], a16[lo:hi]).then_inc(self.s_lay, 16)
                    act.dma_start(dsv[lo:hi, :, 2 + ATTR:W_DS], a32[lo:hi]).then_inc(self.s_lay, 16)

    def laid_down(self):
        nc = self.nc
        with nc.Block() as block:
            @block.sync
            def _(sp):
                sp.wait_ge(self.s_lay, 16 * 8)

    def order_tiles(self, ctx):
        return {
            "cont": self.sb(ctx, "cont", [P, T]),
            "contm": self.sb(ctx, "contm", [P, T]),
            "fix": self.sb(ctx, "fix", [P, 1], i32),
            "w": self.sb(ctx, "w", [P, P]),
            "wm": self.sb(ctx, "wm", [P, P]),
        }

    def order(self, ctx, key, o=None):
        nc = self.nc
        o = o or self.order_tiles(ctx)
        with ExitStack() as c:
            prev = self.sb(c, "prev", [P, 1])
            last = self.sb(c, "lastk", [P, 1])
            n, whole = self.sb(c, "n", [P, 1]), self.sb(c, "whole", [P, 1])
            eq = self.sb(c, "eq", [P, T])
            wb = self.sb(c, "wb", [P, P])
            pw = self.ps(c, "pw", [P, P])
            s_a, s_b, s_w, s_m = (self.sem(c, n_) for n_ in ("s_a", "s_b", "s_w", "s_m"))
            block = c.enter_context(nc.Block())

            @block.sync
            def _(sp):
                sp.wait_ge(s_a, 1)
                sp.dma_start(prev[1:P, :], last[0:P - 1, :]).then_inc(s_b, 16)
                sp.wait_ge(s_b, 16)

            @block.tensor
            def _(pe):
                pe.wait_ge(s_w, 1)
                nc.tensor.matmul(pw[:], wb[:], self.ident[:], start=True, stop=True).then_inc(s_m, 1)

            @block.vector
            def _(v):
                nc.vector.memset(prev[:], -1.0)
                nc.vector.tensor_copy(last[:], key[:, T - 1:T])
                v.drain().then_inc(s_a, 1)
                nc.vector.tensor_copy(eq[:], key)
                v.drain()
                nc.vector.tensor_tensor(o["cont"][:, 1:T], eq[:, 1:T], eq[:, 0:T - 1], ALU.is_equal)
                v.wait_ge(s_b, 16)
                nc.vector.tensor_tensor(o["cont"][:, 0:1], eq[:, 0:1], prev[:], ALU.is_equal)
                v.drain()
                nc.vector.tensor_scalar(o["contm"][:], o["cont"][:], 2.0, -1.0, ALU.mult, ALU.add)
                nc.vector.tensor_scalar(wb[:, 0:1], eq[:, 0:1], 1.0, None, ALU.mult)
                v.drain()
                nc.vector.tensor_scalar(o["contm"][:], o["contm"][:], BIG, None, ALU.mult)
                nc.vector.tensor_scalar(eq[:], eq[:], wb[:, 0:1], None, ALU.is_equal)
                v.drain()
                nc.vector.reduce_sum(n[:], eq[:], AX.X)
                v.drain()
                nc.vector.tensor_scalar(whole[:], n[:], float(T), None, ALU.is_equal)
                nc.vector.scalar_tensor_tensor(n[:], self.ipart[:], float(T), n[:], ALU.mult, ALU.add)
                v.drain()
                nc.vector.tensor_scalar(o["fix"][:], n[:], 1.0, None, ALU.subtract)
                nc.vector.tensor_tensor(whole[:], whole[:], o["cont"][:, 0:1], ALU.mult)
                v.drain()
                nc.vector.tensor_scalar(wb[:], self.ones[:], whole[:, 0:1], None, ALU.mult)
                v.drain().then_inc(s_w, 1)
                v.wait_ge(s_m, 1)
                nc.vector.tensor_copy(o["w"][:], pw[:])
                v.drain()
                nc.vector.tensor_scalar(o["wm"][:], o["w"][:], 2.0, -1.0, ALU.mult, ALU.add)
                v.drain()
                nc.vector.tensor_scalar(o["wm"][:], o["wm"][:], BIG, None, ALU.mult)
        return o

    def join(self, o, tail, W, s, is_max):
        nc = self.nc
        neutral = -BIG if is_max else 0.0
        ops = (ALU.min, ALU.max) if is_max else (ALU.mult, ALU.add)
        groups = [(lo, min(lo + P, W)) for lo in range(0, W, P)]
        with ExitStack() as c:
            tT = self.sb(c, "tT", [P, P])
            sT = self.sb(c, "sT", [P, P + 1])
            carry = self.sb(c, "carry", [P, W])
            row = self.sb(c, "row", [P, W])
            pt = self.ps(c, "pt", [P, P])
            pb = self.ps(c, "pb", [P, P])
            s_t, s_s, s_b, s_g, s_r, s_o, s_d = (self.sem(c, n) for n in ("s_t", "s_s", "s_b", "s_g", "s_r", "s_o", "s_d"))
            block = c.enter_context(nc.Block())

            @block.tensor
            def _(pe):
                for k, (lo, hi) in enumerate(groups):
                    if k:
                        pe.wait_ge(s_d, k)
                    nc.tensor.transpose(pt[0:hi - lo, :], tail[:, lo:hi], self.ident[:]).then_inc(s_t, 1)
                    pe.wait_ge(s_s, k + 1)
                    nc.tensor.transpose(pb[:, 0:hi - lo], sT[0:hi - lo, 0:P], self.ident[0:hi - lo, 0:hi - lo]).then_inc(s_b, 1)

            @block.vector
            def _(v):
                nc.vector.memset(sT[:], neutral)
                v.drain()
                for k, (lo, hi) in enumerate(groups):
                    n = hi - lo
                    v.wait_ge(s_t, k + 1)
                    nc.vector.tensor_copy(tT[0:n, :], pt[0:n, :])
                    v.drain()
                    nc.vector.tensor_tensor_scan(sT[0:n, 1:P + 1], o["wm" if is_max else "w"][0:n, :], tT[0:n, :], neutral, *ops)
                    v.drain().then_inc(s_s, 1)
                    v.wait_ge(s_b, k + 1)
                    nc.vector.tensor_scalar(carry[:, lo:hi], pb[:, 0:n], o["contm" if is_max else "cont"][:, 0:1], None, ops[0])
                    v.drain().then_inc(s_d, 1)
                v.wait_ge(s_g, 16)
                nc.vector.tensor_tensor(row[:], row[:], carry[:], ops[1])
                v.drain().then_inc(s_r, 1)

            @block.gpsimd
            def _(pool):
                nc.gpsimd.indirect_dma_start(row[:], None, s[:, :], bass.IndirectOffsetOnAxis(o["fix"][:, 0:1], 0)).then_inc(s_g, 16)
                pool.wait_ge(s_r, 1)
                nc.gpsimd.indirect_dma_start(s[:, :], bass.IndirectOffsetOnAxis(o["fix"][:, 0:1], 0), row[:], None).then_inc(s_o, 16)
                pool.wait_ge(s_o, 16)

    def fetch(self, s, idx, out):
        nc = self.nc
        with ExitStack() as c:
            s_g = self.sem(c, "s_g")
            block = c.enter_context(nc.Block())

            @block.gpsimd
            def _(pool):
                for j in range(NJ):
                    nc.gpsimd.indirect_dma_start(out[:, j, :], None, s[:, :], bass.IndirectOffsetOnAxis(idx[:, j:j + 1], 0)).then_inc(s_g, 16)
                pool.wait_ge(s_g, 16 * NJ)

    def spread(self, z, idx, rows, table=None):
        nc = self.nc
        with ExitStack() as c:
            s_g, s_t = self.sem(c, "s_g"), self.sem(c, "s_t")
            block = c.enter_context(nc.Block())

            @block.gpsimd
            def _(pool):
                if z is not None:
                    pool.wait_ge(self.s_z, self.zeroed)
                for j in range(NJ if z is not None else 0):
                    nc.gpsimd.indirect_dma_start(z[:, :], bass.IndirectOffsetOnAxis(idx[:, j:j + 1], 0), rows[:, j, :], None).then_inc(s_g, 16)
                if z is not None:
                    pool.wait_ge(s_g, 16 * NJ)

            @block.sync
            def _(sp):
                if table is not None:
                    sp.dma_start(table.rearrange("(p j) f -> p j f", j=NJ), rows[:]).then_inc(s_t, 16)
                    sp.wait_ge(s_t, 16)

    def first_rows(self, table, idx, out):
        nc = self.nc
        with ExitStack() as c:
            s_g = self.sem(c, "s_g")
            block = c.enter_context(nc.Block())

            @block.gpsimd
            def _(pool):
                nc.gpsimd.indirect_dma_start(out[:], None, table[:, :], bass.IndirectOffsetOnAxis(idx, 0)).then_inc(s_g, 16)
                pool.wait_ge(s_g, 16)

    def dense(self, src, J, K, M, weights, post):
        nc = self.nc
        G = NJ // J
        with ExitStack() as c:
            xT = self.sb(c, "xT", [P, 2, P])
            pt = [self.ps(c, "pt", [P, P]) for _ in range(2)]
            po = [self.ps(c, "po", [P, J * M]) for _ in range(2)]
            s_t, s_c, s_m, s_p = (self.sem(c, n) for n in ("s_t", "s_c", "s_m", "s_p"))
            block = c.enter_context(nc.Block())

            @block.tensor
            def _(pe):
                for g in range(G + 1):
                    if g < G:
                        if g >= 2:
                            pe.wait_ge(s_c, g - 1)
                        nc.tensor.transpose(pt[g % 2][0:J * K, :], src[:, g * J:(g + 1) * J, :].rearrange("p j k -> p (j k)"),
                                            self.ident[:]).then_inc(s_t, 1)
                    if g >= 1:
                        pe.wait_ge(s_c, g)
                        if g >= 3:
                            pe.wait_ge(s_p, g - 2)
                        nc.tensor.matmul(po[(g - 1) % 2][:], xT[0:J * K, (g - 1) % 2, :], weights, start=True, stop=True).then_inc(s_m, 1)

            @block.scalar
            def _(act):
                for g in range(G):
                    act.wait_ge(s_t, g + 1)
                    if g >= 2:
                        act.wait_ge(s_m, g - 1)
                    nc.scalar.copy(xT[0:J * K, g % 2, :], pt[g % 2][0:J * K, :]).then_inc(s_c, 1)

            @block.vector
            def _(v):
                for g in range(G):
                    v.wait_ge(s_m, g + 1)
                    post(v, g, po[g % 2])
                    v.drain().then_inc(s_p, 1)

    def block_diagonal(self, ctx, w, K, M, J=4, transform=None):
        nc = self.nc
        wd = self.sb(ctx, "wd", [P, J * M])
        with ExitStack() as c:
            s_z, s_l = self.sem(c, "s_z"), self.sem(c, "s_l")
            block = c.enter_context(nc.Block())

            @block.vector
            def _(v):
                nc.vector.memset(wd[:], 0.0)
                v.drain().then_inc(s_z, 1)

            @block.sync
            def _(sp):
                sp.wait_ge(s_z, 1)
                for j in range(J):
                    sp.dma_start(wd[j * K:(j + 1) * K, j * M:(j + 1) * M], w).then_inc(s_l, 16)
                sp.wait_ge(s_l, 16 * J)
        return wd[0:J * K, :]

    def row_of(self, ctx, b, n, J=1):
        nc = self.nc
        t = self.sb(ctx, "bias", [P, J, n])
        with ExitStack() as c:
            s_l = self.sem(c, "s_l")
            block = c.enter_context(nc.Block())

            @block.sync
            def _(sp):
                for j in range(J):
                    sp.dma_start(t[:, j, :], b.rearrange("(o n) -> o n", o=1).to_broadcast([P, n])).then_inc(s_l, 16)
                sp.wait_ge(s_l, 16 * J)
        return t

    def norm(self, y):
        nc = self.nc
        with ExitStack() as c:
            m, q = self.sb(c, "m", [P, NJ]), self.sb(c, "q", [P, NJ])
            sq = self.sb(c, "sq", [P, NJ, F])
            s_v, s_q = self.sem(c, "s_v"), self.sem(c, "s_q")
            block = c.enter_context(nc.Block())
            wide = lambda t: t[:].unsqueeze(2).to_broadcast([P, NJ, F])

            @block.vector
            def _(v):
                nc.vector.reduce_sum(m[:], y[:], AX.X)
                v.drain()
                nc.vector.tensor_scalar(m[:], m[:], 1.0 / F, None, ALU.mult)
                v.drain()
                nc.vector.tensor_tensor(y[:], y[:], wide(m), ALU.subtract)
                v.drain()
                nc.vector.tensor_tensor(sq[:], y[:], y[:], ALU.mult)
                v.drain()
                nc.vector.reduce_sum(q[:], sq[:], AX.X)
                v.drain()
                nc.vector.tensor_scalar(q[:], q[:], 1.0 / F, 1e-5, ALU.mult, ALU.add)
                v.drain().then_inc(s_v, 1)
                v.wait_ge(s_q, 1)
                nc.vector.reciprocal(q[:], q[:])
                v.drain()
                nc.vector.tensor_tensor(self.x[:], y[:], wide(q), ALU.mult)

            @block.scalar
            def _(act):
                act.wait_ge(s_v, 1)
                nc.scalar.activation(q[:], q[:], ACT.Sqrt).then_inc(s_q, 1)

    def dst_order(self, ctx):
        nc = self.nc
        self.src_i = self.sb(ctx, "src_i", [P, T], i32)
        self.key0_i = self.sb(ctx, "key0_i", [P, 1], i32)
        with nc.Block() as block:
            @block.vector
            def _(v):
                nc.vector.tensor_copy(self.src_i[:], self.edge[:, 0:T, 1])
                nc.vector.tensor_copy(self.key0_i[:], self.edge[:, 0:1, 0])
        return self.order(ctx, self.edge[:, 0:T, 0])

    def attention(self, d, first_d):
        nc, a = self.nc, self.a
        with ExitStack() as top:
            ab = self.sb(top, "ab", [P, NJ, 2 * HEADS])
            first_s, last_s = (self.sb(top, n, [P, NJ], i32) for n in ("first_s", "last_s"))
            sorting = top.enter_context(ExitStack())
            digits = [self.sb(sorting, n, [P, T + 2 * CH]) for n in ("kp", "kj")]
            C = self.sb(sorting, "C", [P, CH, NJ])
            self.csr(sorting, digits, 1, C, first_s, last_s)
            self.ss = self.dram("ss", (E_PAD, W_SS))
            xa_d = self.dram("xa_d", (N_PAD, W_XA))
            with ExitStack() as c:
                xa = self.sb(c, "xa", [P, NJ, W_XA])
                w_s = self.sb(c, "w_s", [F, HEADS, F])
                fc = self.sb(c, "fc", [F, 2 * F])
                fcb = self.sb(c, "fcb", [P, 1])
                pr = self.sb(c, "pr", [F, 2, HEADS, F])
                u = self.sb(c, "u", [F, 2 * HEADS])
                ud = self.sb(c, "ud", [P, 4 * 2 * HEADS])
                with ExitStack() as cc:
                    s_l, s_u, s_d = (self.sem(cc, n) for n in ("s_l", "s_u", "s_d"))
                    block = cc.enter_context(nc.Block())

                    @block.sync
                    def _(sp):
                        sp.dma_start(w_s[:], a["L0_gnn_w"].rearrange("h f o -> f h o")).then_inc(s_l, 16)
                        sp.dma_start(fc[:], a["L0_gnn_fc_w"].to_broadcast([F, 2 * F])).then_inc(s_l, 16)
                        sp.dma_start(fcb[:], a["L0_gnn_fc_b"].rearrange("(o n) -> o n", o=1).to_broadcast([P, 1])).then_inc(s_l, 16)
                        sp.wait_ge(s_u, 1)
                        for j in range(4):
                            sp.dma_start(ud[j * F:(j + 1) * F, j * 8:(j + 1) * 8], u[:]).then_inc(s_d, 16)
                        sp.wait_ge(s_d, 64)

                    @block.vector
                    def _(v):
                        nc.vector.memset(ud[:], 0.0)
                        v.wait_ge(s_l, 48)
                        for k in range(2):
                            nc.vector.tensor_tensor(pr[:, k], w_s[:], fc[:, k * F:(k + 1) * F].unsqueeze(1).to_broadcast([F, HEADS, F]), ALU.mult)
                            v.drain()
                            nc.vector.reduce_sum(u[:, k * HEADS:(k + 1) * HEADS], pr[:, k], AX.X)
                        nc.vector.tensor_copy(xa[:, :, HEADS:W_XA], self.x[:])
                        v.drain().then_inc(s_u, 1)

                def post(v, g, po):
                    o = po[:].rearrange("p (j m) -> p j m", j=4)
                    nc.vector.tensor_scalar(ab[:, 4 * g:4 * g + 4, 0:HEADS], o[:, :, 0:HEADS], fcb[:, 0:1], None, ALU.add)
                    nc.vector.tensor_copy(xa[:, 4 * g:4 * g + 4, 0:HEADS], o[:, :, HEADS:2 * HEADS])
                self.dense(self.x, 4, F, 2 * HEADS, ud[:], post)
                self.spread(self.z_x, first_d, xa, xa_d)

            z = self.z_x[0:E_PAD].rearrange("(p t) w -> p t w", t=T)
            dsv = self.ds.rearrange("(p t) w -> p t w", t=T)

            def loads(sp, i, h, to):
                if sp is not None:
                    pay, done = to
                    at = bass.ds((i * 2 + h) * TB, TB)
                    sp.dma_start(pay[:, h, :, 1 + W_XA:W_SS], dsv[:, at, 2 + ATTR:W_DS]).then_inc(done, 16)
                return 1
            self.sort(digits, C, W_SS, self.ss, lambda c: SpreadFill(self, c, d, z, xa_d), loads)
            sorting.close()

            o_ctx = top.enter_context(ExitStack())
            ssv = self.ss.rearrange("(p t) w -> p t w", t=T)
            key0 = self.sb(o_ctx, "key0", [P, 1], i32)
            s = self.order_tiles(o_ctx)
            with ExitStack() as c:
                ka = self.sb(c, "ka", [P, T, 1 + HEADS])
                s_l = self.sem(c, "s_l")
                with ExitStack() as cc:
                    block = cc.enter_context(nc.Block())

                    @block.sync
                    def _(sp):
                        sp.dma_start(ka[:], ssv[:, :, 0:1 + HEADS]).then_inc(s_l, 16)
                        sp.wait_ge(s_l, 16)

                    @block.vector
                    def _(v):
                        v.wait_ge(s_l, 16)
                        nc.vector.tensor_copy(key0[:], ka[:, 0:1, 0])
                self.order(None, ka[:, :, 0], s)
                with ExitStack() as cc:
                    s_v, s_o = self.sem(cc, "s_v"), self.sem(cc, "s_o")
                    block = cc.enter_context(nc.Block())

                    @block.vector
                    def _(v):
                        for k in range(HEADS):
                            nc.vector.tensor_tensor_scan(ka[:, :, 1 + k], s["contm"][:], ka[:, :, 1 + k], -BIG, ALU.min, ALU.max)
                        v.drain().then_inc(s_v, 1)

                    @block.sync
                    def _(sp):
                        sp.wait_ge(s_v, 1)
                        sp.dma_start(self.s_m[0:E_PAD].rearrange("(p t) w -> p t w", t=T), ka[:, :, 1:1 + HEADS]).then_inc(s_o, 16)
                        sp.wait_ge(s_o, 16)
                self.join(s, ka[:, T - 1, 1:1 + HEADS], HEADS, self.s_m, True)
            e_d = self.dram("e_d", (N_PAD, 2 * HEADS))
            with ExitStack() as c:
                mx = self.sb(c, "mx", [P, NJ, HEADS])
                self.fetch(self.s_m, last_s, mx)
                with ExitStack() as cc:
                    block = cc.enter_context(nc.Block())

                    @block.vector
                    def _(v):
                        nc.vector.tensor_tensor(mx[:], mx[:], ab[:, :, 0:HEADS], ALU.add)
                        v.drain()
                        nc.vector.scalar_tensor_tensor(ab[:, :, HEADS:], mx[:], 0.2, mx[:], ALU.mult, ALU.max)
                self.spread(self.z_e, first_s, ab, e_d)
            tail = self.sb(o_ctx, "tail", [P, W_V])
            self.attention_edges(s, tail, key0, e_d, ssv)
            self.join(s, tail, W_V, self.s_v, False)
            with ExitStack() as c:
                r = self.sb(c, "r", [P, NJ, W_V])
                self.fetch(self.s_v, last_s, r)
                self.attention_nodes(r)

    def attention_edges(self, s, tail, key0, e_d, ssv):
        nc = self.nc
        ze = self.z_e[0:E_PAD].rearrange("(p t) w -> p t w", t=T)
        sv = self.s_v[0:E_PAD].rearrange("(p t) w -> p t w", t=T)
        ROUNDS = T // (2 * TBA)
        HF = HEADS * F
        with ExitStack() as c:
            row = self.sb(c, "row", [P, 2, TBA, W_SS])
            ex = self.sb(c, "ex", [P, 2, TBA, 2 * HEADS])
            ecar = self.sb(c, "ecar", [P, 2 * HEADS])
            V = self.sb(c, "V", [P, 2, TBA, W_V])
            e = self.sb(c, "e", [P, 2, TBA, HEADS])
            p = self.sb(c, "p", [P, 2, TBA, HEADS])
            cb = self.sb(c, "cb", [P, 2, TBA])
            self.first_rows(e_d, key0[:, 0:1], ecar)
            s_ld = [self.sem(c, "s_ld") for _ in range(2)]
            s_st = [self.sem(c, "s_st") for _ in range(2)]
            s_vf = [self.sem(c, "s_vf") for _ in range(2)]
            names = ("s_e", "s_p", "s_x", "s_y", "s_m", "s_v", "tick")
            s_e, s_p, s_x, s_y, s_m, s_v, tick = (self.sem(c, n) for n in names)
            block = c.enter_context(nc.Block())

            def spot(i, h):
                return bass.ds((i * 2 + h) * TBA, TBA)

            @block.vector
            def _(v):
                def scores(i, h):
                    nc.vector.tensor_copy(cb[:, h, :], s["cont"][:, spot(i, h)])
                    hold(v, s_ld[h], (i + 1) * 32, tick)
                    v.drain()
                    for k in range(2 * HEADS):
                        nc.vector.tensor_tensor_scan(ex[:, h, :, k], cb[:, h, :], ex[:, h, :, k], ecar[:, k:k + 1], ALU.mult, ALU.add)
                    v.drain()
                    nc.vector.tensor_copy(ecar[:], ex[:, h, TBA - 1, :])
                    nc.vector.tensor_tensor(e[:, h], ex[:, h, :, 0:HEADS], row[:, h, :, 1:1 + HEADS], ALU.add)
                    v.drain()
                    nc.vector.scalar_tensor_tensor(e[:, h], e[:, h], 0.2, e[:, h], ALU.mult, ALU.max)
                    v.drain()
                    nc.vector.tensor_tensor(e[:, h], e[:, h], ex[:, h, :, HEADS:], ALU.subtract).then_inc(s_e, 1)

                def sums(i, h):
                    b = i * 2 + h
                    for k in range(POOL_HEADS, HEADS):
                        if k == POOL_HEADS:
                            hold(v, s_p, b + 1, tick)
                            hold(v, s_vf[h], i + 1, tick)
                        nc.vector.tensor_tensor(V[:, h, :, k * F:(k + 1) * F], row[:, h, :, 1 + HEADS:1 + W_XA],
                                                p[:, h, :, k:k + 1].to_broadcast([P, TBA, F]), ALU.mult)
                    v.drain().then_inc(s_y, 1)
                    hold(v, s_x, b + 1, tick)
                    hold(v, s_m, b + 1, tick)
                    for k in range(W_V):
                        nc.vector.tensor_tensor_scan(V[:, h, :, k], cb[:, h, :], V[:, h, :, k], tail[:, k:k + 1], ALU.mult, ALU.add)
                    v.drain()
                    nc.vector.tensor_copy(tail[:], V[:, h, TBA - 1, :]).then_inc(s_v, 1)

                nc.vector.memset(tail[:], 0.0)
                scores(0, 0)
                with v.Fori(0, ROUNDS - 1) as i:
                    scores(i, 1)
                    sums(i, 0)
                    scores(i + 1, 0)
                    sums(i, 1)
                    v.drain()
                scores(ROUNDS - 1, 1)
                sums(ROUNDS - 1, 0)
                sums(ROUNDS - 1, 1)

            @block.scalar
            def _(act):
                with act.Fori(0, ROUNDS) as i:
                    for h in range(2):
                        hold(act, s_e, i * 2 + h + 1, tick)
                        nc.scalar.activation(p[:, h], e[:, h], ACT.Exp).then_inc(s_p, 1)
                        hold(act, s_vf[h], i + 1, tick)
                        nc.scalar.copy(V[:, h, :, HF + HEADS:], row[:, h, :, 1 + W_XA:])
                        hold(act, s_p, i * 2 + h + 1, tick)
                        nc.scalar.copy(V[:, h, :, HF:HF + HEADS], p[:, h]).then_inc(s_x, 1)

            @block.gpsimd
            def _(pool):
                with pool.Fori(0, ROUNDS) as i:
                    for h in range(2):
                        hold(pool, s_p, i * 2 + h + 1, tick)
                        hold(pool, s_vf[h], i + 1, tick)
                        for k in range(POOL_HEADS):
                            m = nc.gpsimd.tensor_tensor(V[:, h, :, k * F:(k + 1) * F], row[:, h, :, 1 + HEADS:1 + W_XA],
                                                        p[:, h, :, k:k + 1].to_broadcast([P, TBA, F]), ALU.mult)
                        m.then_inc(s_m, 1)

            @block.sync
            def _(sp):
                def load(i, h):
                    sp.dma_start(row[:, h], ssv[:, spot(i, h), :]).then_inc(s_ld[h], 16)
                    sp.dma_start(ex[:, h], ze[:, spot(i, h), :]).then_inc(s_ld[h], 16)

                def taken(i, h):
                    hold(sp, s_x, i * 2 + h + 1, tick)
                    hold(sp, s_y, i * 2 + h + 1, tick)
                    hold(sp, s_m, i * 2 + h + 1, tick)

                def store(i, h):
                    hold(sp, s_v, i * 2 + h + 1, tick)
                    sp.dma_start(sv[:, spot(i, h), :], V[:, h]).then_inc(s_st[h], 16)
                for h in range(2):
                    sp.sem_inc(s_vf[h], 1)
                    load(0, h)
                with sp.Fori(0, ROUNDS - 1) as i:
                    for h in range(2):
                        taken(i, h)
                        load(i + 1, h)
                        store(i, h)
                        hold(sp, s_st[h], i * 16 + 16, s_vf[h])
                for h in range(2):
                    store(ROUNDS - 1, h)
                for h in range(2):
                    sp.wait_ge(s_st[h], 16 * ROUNDS)

    def attention_nodes(self, r):
        nc, a = self.nc, self.a
        HF = HEADS * F
        with ExitStack() as c:
            w = self.sb(c, "w0", [HF, F])
            y = self.sb(c, "y", [P, NJ, F])
            bias = self.row_of(c, a["L0_gnn_bias"], F)
            d0 = self.sb(c, "d0", [P, NJ, HEADS])
            with ExitStack() as cc:
                s_l = self.sem(cc, "s_l")
                block = cc.enter_context(nc.Block())

                @block.sync
                def _(sp):
                    sp.dma_start(w[:], a["L0_gnn_w"].rearrange("h f o -> (h f) o")).then_inc(s_l, 16)

                @block.vector
                def _(v):
                    den = r[:, :, HF:HF + HEADS]
                    nc.vector.tensor_copy(self.edge_sum[:], r[:, :, HF + HEADS:])
                    nc.vector.tensor_scalar(d0[:], den, 0.0, None, ALU.is_equal)
                    v.drain()
                    nc.vector.tensor_tensor(d0[:], d0[:], den, ALU.add)
                    v.drain()
                    nc.vector.tensor_scalar(d0[:], d0[:], float(HEADS), None, ALU.mult)
                    v.drain()
                    nc.vector.reciprocal(d0[:], d0[:])
                    v.drain()
                    for k in range(HEADS):
                        at = r[:, :, k * F:(k + 1) * F]
                        nc.vector.tensor_tensor(at, at, d0[:, :, k:k + 1].to_broadcast([P, NJ, F]), ALU.mult)
                    v.wait_ge(s_l, 16)

            def post(v, g, po):
                nc.vector.tensor_tensor(y[:, g, :], po[:], self.x[:, g, :], ALU.add)
                v.drain()
                nc.vector.tensor_tensor(y[:, g, :], y[:, g, :], bias[:, 0, :], ALU.add)
            self.dense(r[:, :, 0:HF], 1, HF, F, w[:], post)
            self.norm(y)

    def gather_sum(self, d, y_d, s_dram, tail):
        nc = self.nc
        sv = s_dram[0:E_PAD].rearrange("(p t) w -> p t w", t=T)
        with ExitStack() as c:
            buf = self.sb(c, "buf", [P, 2, TB, HID])
            idx = self.sb(c, "idx", [P, 2, TB], i32)
            cb = self.sb(c, "cb", [P, 2, TB])
            s_g = [self.sem(c, "s_g") for _ in range(2)]
            s_st = [self.sem(c, "s_st") for _ in range(2)]
            s_free = [self.sem(c, "s_free") for _ in range(2)]
            s_i, s_v, tick = (self.sem(c, n) for n in ("s_i", "s_v", "tick"))
            block = c.enter_context(nc.Block())

            @block.scalar
            def _(act):
                with act.Fori(0, NIT) as i:
                    for h in range(2):
                        hold(act, s_free[h], i + 1, tick)
                        nc.scalar.copy(idx[:, h, :], self.src_i[:, bass.ds((i * 2 + h) * TB, TB)]).then_inc(s_i, 1)

            @block.gpsimd
            def _(pool):
                with pool.Fori(0, NIT) as i:
                    for h in range(2):
                        hold(pool, s_i, i * 2 + h + 1, tick)
                        for t in range(TB):
                            nc.gpsimd.indirect_dma_start(buf[:, h, t, :], None, y_d[:, :],
                                                         bass.IndirectOffsetOnAxis(idx[:, h, t:t + 1], 0)).then_inc(s_g[h], 16)

            @block.vector
            def _(v):
                nc.vector.memset(tail[:], 0.0)
                with v.Fori(0, NIT) as i:
                    for h in range(2):
                        nc.vector.tensor_copy(cb[:, h, :], d["cont"][:, bass.ds((i * 2 + h) * TB, TB)])
                        v.drain()
                        hold(v, s_g[h], (i + 1) * (16 * TB), tick)
                        for k in range(HID):
                            nc.vector.tensor_tensor_scan(buf[:, h, :, k], cb[:, h, :], buf[:, h, :, k], tail[:, k:k + 1], ALU.mult, ALU.add)
                        v.drain()
                        nc.vector.tensor_copy(tail[:], buf[:, h, TB - 1, :])
                        v.drain().then_inc(s_v, 1)

            @block.sync
            def _(sp):
                for h in range(2):
                    sp.sem_inc(s_free[h], 1)
                with sp.Fori(0, NIT) as i:
                    for h in range(2):
                        hold(sp, s_v, i * 2 + h + 1, tick)
                        sp.dma_start(sv[:, bass.ds((i * 2 + h) * TB, TB), :], buf[:, h]).then_inc(s_st[h], 16)
                        hold(sp, s_st[h], i * 16 + 16, s_free[h])

    def gin(self, d, last_d):
        nc, a = self.nc, self.a
        with ExitStack() as c:
            y = self.sb(c, "y", [P, NJ, HID])
            h = self.sb(c, "h", [P, NJ, HID])
            r = self.sb(c, "r", [P, NJ, F])
            tail = self.sb(c, "tail", [P, HID])
            w1 = self.block_diagonal(c, a["L1_gnn_W1"], F, HID)
            w2 = self.block_diagonal(c, a["L1_gnn_W2"], HID, F)
            w3 = self.block_diagonal(c, a["L1_gnn_W3"], F, HID)
            w4 = self.block_diagonal(c, a["L1_gnn_W4"], HID, F)
            b1 = self.row_of(c, a["L1_gnn_b1"], HID)
            b2 = self.row_of(c, a["L1_gnn_b2"], F, 4)
            b3 = self.row_of(c, a["L1_gnn_b3"], HID)
            b4 = self.row_of(c, a["L1_gnn_b4"], F, 4)

            def conv(x, w_in, b_in, w_out, post, y_d, s_dram):
                def keep(v, g, po):
                    nc.vector.tensor_copy(y[:, 4 * g:4 * g + 4, :], po[:].rearrange("p (j m) -> p j m", j=4))
                self.dense(x, 4, F, HID, w_in, keep)
                self.spread(None, None, y, y_d)
                self.gather_sum(d, y_d, s_dram, tail)
                self.join(d, tail, HID, s_dram, False)
                self.fetch(s_dram, last_d, h)
                with ExitStack() as cc:
                    block = cc.enter_context(nc.Block())

                    @block.vector
                    def _(v):
                        nc.vector.tensor_tensor(h[:], h[:], y[:], ALU.add)
                        v.drain()
                        nc.vector.tensor_tensor(h[:], h[:], b_in[:].to_broadcast([P, NJ, HID]), ALU.add)
                        v.drain()
                        nc.vector.tensor_scalar(h[:], h[:], 0.0, None, ALU.max)
                self.dense(h, 4, HID, F, w_out, post)

            def post_a(v, g, po):
                at = r[:, 4 * g:4 * g + 4, :]
                nc.vector.tensor_tensor(at, po[:].rearrange("p (j m) -> p j m", j=4), b2[:], ALU.add)
                v.drain()
                nc.vector.tensor_scalar(at, at, 0.0, None, ALU.max)

            def post_b(v, g, po):
                at = r[:, 4 * g:4 * g + 4, :]
                nc.vector.tensor_tensor(at, po[:].rearrange("p (j m) -> p j m", j=4), b4[:], ALU.add)
                v.drain()
                nc.vector.tensor_tensor(at, at, self.x[:, 4 * g:4 * g + 4, :], ALU.add)
            conv(self.x, w1, b1, w2, post_a, self.dram("y1", (N_PAD, HID)), self.s_1)
            conv(r, w3, b3, w4, post_b, self.dram("y2", (N_PAD, HID)), self.s_1b)
            self.norm(r)

    def edge_mlp(self, d, first_d, last_d):
        nc, a = self.nc, self.a
        D = 2 * F + ATTR
        with ExitStack() as top:
            x_d = self.dram("x_d", (N_PAD, F))
            self.spread(self.z_2, first_d, self.x, x_d)
            tail = self.sb(top, "tail", [P, F])
            z = self.z_2[0:E_PAD].rearrange("(p t) w -> p t w", t=T)
            dsv = self.ds.rearrange("(p t) w -> p t w", t=T)
            sv = self.s_2[0:E_PAD].rearrange("(p t) w -> p t w", t=T)
            with ExitStack() as c:
                w1 = self.sb(c, "w1", [D, MID + 1])
                b1 = self.sb(c, "b1", [64, 1])
                w2 = self.sb(c, "w2", [MID + 1, F])
                car = self.sb(c, "car", [P, F])
                et = self.sb(c, "et", [P, 2, TB, D])
                V = self.sb(c, "V", [P, 2, TB, F])
                idx = self.sb(c, "idx", [P, 2, TB], i32)
                cb = self.sb(c, "cb", [P, 2, 2, TB])
                eT = self.sb(c, "eT", [D, 2, 4 * P])
                zT = self.sb(c, "zT", [MID + 1, 2, 4 * P])
                hT = self.sb(c, "hT", [MID + 1, 2, 4 * P])
                pT = [self.ps(c, "pT", [D, 4 * P]) for _ in range(2)]
                p1 = [self.ps(c, "p1", [MID + 1, 4 * P]) for _ in range(2)]
                p2 = self.ps(c, "p2", [P, TB, F])
                self.first_rows(x_d, self.key0_i[:, 0:1], car)
                with ExitStack() as cc:
                    s_m, s_l = self.sem(cc, "s_m"), self.sem(cc, "s_l")
                    block = cc.enter_context(nc.Block())

                    @block.vector
                    def _(v):
                        nc.vector.memset(w1[:], 0.0)
                        nc.vector.memset(b1[:], 1.0)
                        nc.vector.memset(tail[:], -BIG)
                        v.drain().then_inc(s_m, 1)

                    @block.sync
                    def _(sp):
                        sp.wait_ge(s_m, 1)
                        sp.dma_start(w1[:, 0:MID], a["L2_gnn_W1"]).then_inc(s_l, 16)
                        with nc.allow_non_contiguous_dma(reason="one value per partition"):
                            sp.dma_start(b1[0:MID, :], a["L2_gnn_b1"].rearrange("(n o) -> n o", o=1)).then_inc(s_l, 16)
                        sp.dma_start(w2[0:MID, :], a["L2_gnn_W2"]).then_inc(s_l, 16)
                        sp.dma_start(w2[MID:MID + 1, :], a["L2_gnn_b2"].rearrange("(o n) -> o n", o=1)).then_inc(s_l, 16)
                        sp.wait_ge(s_l, 64)
                s_g = [self.sem(c, "s_g") for _ in range(2)]
                s_ld = [self.sem(c, "s_ld") for _ in range(2)]
                s_st = [self.sem(c, "s_st") for _ in range(2)]
                names = ("s_i", "s_f", "s_T", "s_c", "s_1", "s_h", "s_2", "s_y", "s_v", "s_free", "s_z", "tick")
                s_i, s_f, s_T, s_c, s_1, s_h, s_2, s_y, s_v, s_free, s_z, tick = (self.sem(c, n) for n in names)
                block = c.enter_context(nc.Block())
                NQ = TB // 4

                @block.sync
                def _(sp):
                    def load(i, h):
                        at = bass.ds((i * 2 + h) * TB, TB)
                        sp.dma_start(et[:, h, :, F:2 * F], z[:, at, :]).then_inc(s_ld[h], 16)
                        sp.dma_start(et[:, h, :, 2 * F:D], dsv[:, at, 2:2 + ATTR]).then_inc(s_ld[h], 16)

                    def store(i, h):
                        sp.dma_start(sv[:, bass.ds((i * 2 + h) * TB, TB), :], V[:, h]).then_inc(s_st[h], 16)
                    sp.sem_inc(s_free, 1)
                    load(0, 0)
                    sp.sem_inc(s_free, 1)
                    load(0, 1)
                    with sp.Fori(0, NIT - 1) as i:
                        for h in range(2):
                            hold(sp, s_v, i * 2 + h + 1, tick)
                            store(i, h)
                            hold(sp, s_st[h], i * 16 + 16, s_free)
                            load(i + 1, h)
                    for h in range(2):
                        sp.wait_ge(s_v, 2 * (NIT - 1) + h + 1)
                        store(NIT - 1, h)
                    for h in range(2):
                        sp.wait_ge(s_st[h], 16 * NIT)

                @block.gpsimd
                def _(pool):
                    with pool.Fori(0, NIT) as i:
                        for h in range(2):
                            hold(pool, s_i, i * 2 + h + 1, tick)
                            for t in range(TB):
                                nc.gpsimd.indirect_dma_start(et[:, h, t, 0:F], None, x_d[:, :],
                                                             bass.IndirectOffsetOnAxis(idx[:, h, t:t + 1], 0)).then_inc(s_g[h], 16)

                @block.vector
                def _(v):
                    def carry_on(i, h):
                        nc.vector.tensor_copy(cb[:, h, 0, :], d["cont"][:, bass.ds((i * 2 + h) * TB, TB)])
                        nc.vector.tensor_copy(cb[:, h, 1, :], d["contm"][:, bass.ds((i * 2 + h) * TB, TB)])
                        v.drain()
                        for k in range(F):
                            nc.vector.tensor_tensor_scan(et[:, h, :, F + k], cb[:, h, 0, :], et[:, h, :, F + k], car[:, k:k + 1], ALU.mult, ALU.add)
                        v.drain()
                        nc.vector.tensor_copy(car[:], et[:, h, TB - 1, F:2 * F])
                        v.drain().then_inc(s_f, 1)

                    with v.Fori(0, NIT) as i:
                        for h in range(2):
                            hold(v, s_free, i * 2 + h + 1, tick)
                            nc.vector.tensor_copy(idx[:, h, :], self.src_i[:, bass.ds((i * 2 + h) * TB, TB)])
                            v.drain().then_inc(s_i, 1)
                        for h in range(2):
                            hold(v, s_ld[h], (i + 1) * 32, tick)
                            carry_on(i, h)
                        for h in range(2):
                            for q in range(NQ):
                                hold(v, s_z, (i * 2 + h) * NQ + q + 1, tick)
                                nc.vector.scalar_tensor_tensor(hT[:, q % 2, :], zT[:, q % 2, :], 0.01, zT[:, q % 2, :],
                                                               ALU.mult, ALU.max).then_inc(s_h, 1)
                            hold(v, s_y, i * 2 + h + 1, tick)
                            nc.vector.scalar_tensor_tensor(V[:, h], V[:, h], 0.01, V[:, h], ALU.mult, ALU.max)
                            v.drain()
                            for k in range(F):
                                nc.vector.tensor_tensor_scan(V[:, h, :, k], cb[:, h, 1, :], V[:, h, :, k], tail[:, k:k + 1], ALU.min, ALU.max)
                            v.drain()
                            nc.vector.tensor_copy(tail[:], V[:, h, TB - 1, :])
                            v.drain().then_inc(s_v, 1)

                @block.tensor
                def _(pe):
                    with pe.Fori(0, NIT) as i:
                        for h in range(2):
                            hold(pe, s_g[h], (i + 1) * (16 * TB), tick)
                            hold(pe, s_f, i * 2 + h + 1, tick)
                            for q in range(NQ + 2):
                                n = (i * 2 + h) * NQ
                                if q < NQ:
                                    for k in range(4):
                                        mm = nc.tensor.transpose(pT[q % 2][:, k * P:(k + 1) * P], et[:, h, 4 * q + k, :], self.ident[:])
                                    mm.then_inc(s_T, 1)
                                if 1 <= q <= NQ:
                                    hold(pe, s_c, n + q, tick)
                                    nc.tensor.matmul(p1[(q - 1) % 2][:], w1[:], eT[:, (q - 1) % 2, :], start=True, stop=True).then_inc(s_1, 1)
                                if q >= 2:
                                    hold(pe, s_h, n + q - 1, tick)
                                    if q == 2:
                                        hold(pe, s_free, i * 2 + h + 1, tick)
                                    for k in range(4):
                                        mm = nc.tensor.matmul(p2[:, 4 * (q - 2) + k, :], hT[:, (q - 2) % 2, k * P:(k + 1) * P], w2[:],
                                                              start=True, stop=True)
                            mm.then_inc(s_2, 1)
                            hold(pe, s_y, i * 2 + h + 1, tick)

                @block.scalar
                def _(act):
                    with act.Fori(0, NIT) as i:
                        for h in range(2):
                            n = (i * 2 + h) * NQ
                            for q in range(NQ + 1):
                                if q < NQ:
                                    hold(act, s_T, n + q + 1, tick)
                                    nc.scalar.copy(eT[:, q % 2, :], pT[q % 2][:]).then_inc(s_c, 1)
                                if q >= 1:
                                    hold(act, s_1, n + q, tick)
                                    nc.scalar.activation(zT[:, (q - 1) % 2, :], p1[(q - 1) % 2][:], ACT.Identity,
                                                         bias=b1[0:MID + 1, 0:1]).then_inc(s_z, 1)
                            hold(act, s_2, i * 2 + h + 1, tick)
                            for k in range(2):
                                o = slice(k * TB // 2, (k + 1) * TB // 2)
                                last = nc.scalar.copy(V[:, h, o, :], p2[:, o, :])
                            last.then_inc(s_y, 1)
            self.join(d, tail, F, self.s_2, True)
            with ExitStack() as c:
                y = self.sb(c, "y", [P, NJ, F])
                self.fetch(self.s_2, last_d, y)
                with ExitStack() as cc:
                    block = cc.enter_context(nc.Block())

                    @block.vector
                    def _(v):
                        nc.vector.tensor_tensor(y[:], y[:], self.x[:], ALU.max)
                        v.drain()
                        nc.vector.tensor_tensor(y[:], y[:], self.x[:], ALU.add)
                self.norm(y)

    def finish(self):
        nc = self.nc
        with ExitStack() as c:
            y = self.sb(c, "y", [P, NJ, F])
            with ExitStack() as cc:
                block = cc.enter_context(nc.Block())

                @block.vector
                def _(v):
                    nc.vector.tensor_tensor(y[:], self.x[:], self.edge_sum[:], ALU.add)
            self.norm(y)
            s_o = self.sem(c, "s_o")
            block = c.enter_context(nc.Block())

            @block.sync
            def _(sp):
                for lo, hi in SPLITS:
                    sp.dma_start(self.out.rearrange("(p j) f -> p j f", j=NJ)[lo:hi], self.x[lo:hi]).then_inc(s_o, 16)
                sp.wait_ge(s_o, 32)

    def program(self):
        with ExitStack() as top:
            self.top = top
            self.setup(top)
            self.edge_sum = self.sb(top, "edge_sum", [P, NJ, F])
            first_d, last_d = self.sb(top, "first_d", [P, NJ], i32), self.sb(top, "last_d", [P, NJ], i32)
            self.sort_by_dst(first_d, last_d)
            d = self.dst_order(top)
            self.attention(d, first_d)
            self.gin(d, last_d)
            self.edge_mlp(d, first_d, last_d)
            self.finish()


_INS = ["x", "src", "dst", "edge_attr_16", "edge_attr_32", "L0_gnn_w", "L0_gnn_fc_w", "L0_gnn_fc_b", "L0_gnn_bias",
        "L1_gnn_W1", "L1_gnn_b1", "L1_gnn_W2", "L1_gnn_b2", "L1_gnn_W3", "L1_gnn_b3", "L1_gnn_W4", "L1_gnn_b4",
        "L2_gnn_W1", "L2_gnn_b1", "L2_gnn_W2", "L2_gnn_b2"]


def kernel(**inputs):
    import numpy as _np
    import concourse.bacc as _bacc
    from concourse.bass_utils import run_bass_kernel_spmd as _run

    nc = _bacc.Bacc("TRN2", target_bir_lowering=False, num_devices=1)
    arrays, args = {}, {}
    for name in _INS:
        a = _np.ascontiguousarray(inputs[name])
        arrays[f"in_{name}_dram"] = a
        args[name] = nc.dram_tensor(f"in_{name}_dram", a.shape, mybir.dt.from_np(a.dtype), kind="ExternalInput").ap()
    out = nc.dram_tensor("out_0_dram", (N, F), f32, kind="ExternalOutput").ap()
    Build(nc, args, out).program()
    r = _run(nc, [arrays], core_ids=[0])
    return r.results[0]["out_0_dram"]
```

```python
import concourse.bass as bass
from concourse import mybir
from contextlib import ExitStack

f32 = mybir.dt.float32
bf16 = mybir.dt.bfloat16
i32 = mybir.dt.int32
ALU = mybir.AluOpType
ACT = mybir.ActivationFunctionType
AX = mybir.AxisListType

P = 128
N, E, F, HEADS, HID = 12500, 200000, 32, 4, 16
ATTR, MID = 16, 56
NJ = 100
NP_REAL = N // NJ
T = 1600
EP_REAL = E // T
N_PAD, E_PAD = P * NJ, P * T
TB = 32
NIT = T // (2 * TB)
LAST = NIT - 1
CH = 8
STEPS = TB // CH
BIG = 3.4e38
MAGIC = 12582912.0
W_DS = 2 + ATTR + F
W_XA = HEADS + F
W_SS = 1 + W_XA + F
W_V = HEADS * F + HEADS + F
BY_ACT = 3
POOL_HEADS = 2
SUMS = 4
TBA = 32
SPLITS = ((0, 112), (112, 125))


def hold(eng, sem, value, tick):
    eng.wait_ge(sem, value)
    if not isinstance(value, int):
        eng.sem_inc(tick, 1)


class SpreadFill:

    def __init__(self, b, c, d, z, table):
        self.b, self.d, self.z = b, d, z
        self.part = W_XA // STEPS
        self.zt = b.sb(c, "zt", [P, 2, TB, W_XA])
        self.zf = b.sb(c, "zf", [P, 2, W_XA, TB])
        self.goes_on = b.sb(c, "goes_on", [P, 2, self.part, TB])
        self.cont0 = b.sb(c, "cont0", [P, 2])
        self.carry = b.sb(c, "carry", [P, W_XA])
        b.first_rows(table, b.key0_i[:, 0:1], self.carry)
        self.s_z = [b.sem(c, "s_zl") for _ in range(2)]
        self.s_u, self.s_f, self.s_d, self.s_0, self.tick = (b.sem(c, n) for n in ("s_u", "s_f", "s_d", "s_0", "tick"))

    def load(self, sp, i, h):
        sp.dma_start(self.zt[:, h], self.z[:, bass.ds((i * 2 + h) * TB, TB), :]).then_inc(self.s_z[h], 16)

    def free(self, sp, i, h):
        hold(sp, self.s_u, i * 2 + h + 1, self.tick)

    def turn(self, act, i, h):
        nc, at = self.b.nc, (i * 2 + h) * TB
        hold(act, self.s_z[h], (i + 1) * 16, self.tick)
        nc.scalar.copy(self.goes_on[:, h, :, 1:TB], self.d["cont"][:, bass.ds(at + 1, TB - 1)].unsqueeze(1).to_broadcast([P, self.part, TB - 1]))
        nc.scalar.copy(self.cont0[:, h:h + 1], self.d["cont"][:, bass.ds(at, 1)])
        nc.scalar.copy(self.zf[:, h], self.zt[:, h].rearrange("p t f -> p f t")).then_inc(self.s_u, 1)

    def begin(self, act):
        act.wait_ge(self.s_0, 1)
        for h in range(2):
            self.turn(act, 0, h)

    def columns(self, v, i, h, lo, hi):
        nc = self.b.nc
        if lo == 0:
            hold(v, self.s_u, i * 2 + h + 1, self.tick)
            v.drain()
            nc.vector.scalar_tensor_tensor(self.zf[:, h, :, 0], self.carry[:], self.cont0[:, h:h + 1], self.zf[:, h, :, 0], ALU.mult, ALU.add)
            v.drain()
        for f in range(lo, hi, self.part):
            at = self.zf[:, h, f:f + self.part, :].rearrange("p f t -> p (f t)")
            nc.vector.tensor_tensor_scan(at, self.goes_on[:, h].rearrange("p f t -> p (f t)"), at, 0.0, ALU.mult, ALU.add)
        if hi == W_XA:
            v.drain()
            nc.vector.tensor_copy(self.carry[:], self.zf[:, h, :, TB - 1]).then_inc(self.s_f, 1)

    def first(self, v):
        self.b.nc.vector.memset(self.goes_on[:], 0.0)
        v.drain().then_inc(self.s_0, 1)
        self.columns(v, 0, 0, 0, W_XA)

    def scan(self, v, i, s):
        n = self.part
        h, k = s // STEPS, s % STEPS
        if h == 0:
            self.columns(v, i, 1, k * n, (k + 1) * n)
        else:
            self.columns(v, i + 1, 0, k * n, (k + 1) * n)

    def deliver(self, act, i, h, pay):
        hold(act, self.s_f, i * 2 + h + 1, self.tick)
        self.b.nc.scalar.copy(pay[:, h, :, 1:1 + W_XA], self.zf[:, h].rearrange("p f t -> p t f")).then_inc(self.s_d, 1)

    def next(self, act, i, h):
        hold(act, self.s_d, i * 2 + h + 1, self.tick)
        self.turn(act, i + 1, h)


class Build:
    def __init__(self, nc, a, out):
        self.nc, self.a, self.out, self.n, self.owned = nc, a, out, 0, {}

    def sb(self, ctx, name, shape, dt=f32):
        self.n += 1
        return ctx.enter_context(self.nc.sbuf_tensor(f"{name}_{self.n}", shape, dt))

    def ps(self, ctx, name, shape, dt=f32):
        self.n += 1
        return ctx.enter_context(self.nc.psum_tensor(f"{name}_{self.n}", shape, dt))

    def sem(self, ctx, name):
        self.n += 1
        s = self.nc.alloc_semaphore(f"{name}_{self.n}")
        if id(ctx) not in self.owned:
            self.owned[id(ctx)] = []
            ctx.callback(self.release, id(ctx))
        self.owned[id(ctx)].append(s)
        return s

    def release(self, key):
        self.nc.clear_and_free_semaphores(self.owned.pop(key))
        self.nc.all_engine_barrier()

    def dram(self, name, shape, dt=f32):
        return self.nc.dram_tensor(name, shape, dt, kind="Internal").ap()

    def setup(self, ctx):
        nc, a = self.nc, self.a
        sb = lambda name, shape, dt=f32: self.sb(ctx, name, shape, dt)
        self.irow = sb("irow", [P, P])
        self.ipart = sb("ipart", [P, 1])
        self.inode = sb("inode", [P, NJ])
        self.irow_b = sb("irow_b", [P, P], bf16)
        self.ident = sb("ident", [P, P])
        self.ident_b = sb("ident_b", [P, P], bf16)
        self.tri = sb("tri", [P, P])
        self.tri_b = sb("tri_b", [P, P], bf16)
        self.ones = sb("ones", [P, P])
        self.x = sb("x", [P, NJ, F])
        self.zero = sb("zero", [P, T // 2])
        self.edge = sb("edge", [P, T + 2 * CH, 2])
        self.z_x = self.dram("z_x", (E_PAD + N_PAD, W_XA))
        self.z_e = self.dram("z_e", (E_PAD + N_PAD, 2 * HEADS))
        self.z_2 = self.dram("z_2", (E_PAD + N_PAD, F))
        self.s_v = self.dram("s_v", (E_PAD + 1, W_V))
        self.s_m = self.dram("s_m", (E_PAD + 1, HEADS))
        self.s_1 = self.dram("s_1", (E_PAD + 1, HID))
        self.s_1b = self.dram("s_1b", (E_PAD + 1, HID))
        self.s_2 = self.dram("s_2", (E_PAD + 1, F))
        with ExitStack() as c:
            ki = self.sb(c, "ki", [P, 2, T], i32)
            s_in, s_io, s_ms = (self.sem(c, n) for n in ("s_in", "s_io", "s_ms"))
            self.s_zx, self.s_z = self.sem(ctx, "s_zx"), self.sem(ctx, "s_z")
            block = c.enter_context(nc.Block())

            @block.gpsimd
            def _(pool):
                nc.gpsimd.iota(self.irow[:], [[1, P]], base=0, channel_multiplier=0,
                               allow_small_or_imprecise_dtypes=True)
                nc.gpsimd.iota(self.ipart[:], [[1, 1]], base=0, channel_multiplier=1,
                               allow_small_or_imprecise_dtypes=True)
                nc.gpsimd.iota(self.inode[:], [[1, NJ]], base=0, channel_multiplier=NJ,
                               allow_small_or_imprecise_dtypes=True)
                pool.drain().then_inc(s_io, 1)

            @block.vector
            def _(v):
                nc.vector.memset(self.zero[:], 0.0)
                nc.vector.memset(self.x[:], 0.0)
                nc.vector.memset(self.ones[:], 1.0)
                nc.vector.memset(ki[:], N)
                nc.vector.memset(self.edge[:], float(N))
                v.drain().then_inc(s_ms, 1)
                v.wait_ge(s_io, 1)
                nc.vector.tensor_scalar(self.ident[:], self.irow[:], self.ipart[:, 0:1], None, ALU.is_equal)
                nc.vector.tensor_scalar(self.tri[:], self.irow[:], self.ipart[:, 0:1], None, ALU.is_gt)
                nc.vector.tensor_scalar(self.ident_b[:], self.irow[:], self.ipart[:, 0:1], None, ALU.is_equal)
                nc.vector.tensor_scalar(self.tri_b[:], self.irow[:], self.ipart[:, 0:1], None, ALU.is_gt)
                nc.vector.tensor_copy(self.irow_b[:], self.irow[:])
                v.wait_ge(s_in, 16 * 6)
                nc.vector.tensor_copy(self.edge[:, 0:T, 0], ki[:, 0, :])
                nc.vector.tensor_copy(self.edge[:, 0:T, 1], ki[:, 1, :])

            @block.sync
            def _(sp):
                sp.wait_ge(s_ms, 1)
                for lo, hi in SPLITS:
                    sp.dma_start(self.x[lo:hi], a["x"].rearrange("(p j) f -> p j f", j=NJ)[lo:hi]).then_inc(s_in, 16)
                    for k, name in ((0, "dst"), (1, "src")):
                        sp.dma_start(ki[lo:hi, k, :], a[name].rearrange("(p t) -> p t", t=T)[lo:hi]).then_inc(s_in, 16)

    def csr(self, ctx, digits, which, C, first, last, by_pool, scatter=None, on_sync=None):
        nc = self.nc
        kp, kj = digits
        with ExitStack() as c:
            H = self.sb(c, "H", [P, CH, NJ])
            cnt, incl, start, full, t1, t2 = (self.sb(c, n, [P, NJ]) for n in ("cnt", "incl", "start", "full", "t1", "t2"))
            kbp = self.sb(c, "kbp", [P, 2 * TB])
            kbj = self.sb(c, "kbj", [P, 2 * TB])
            kbv = self.sb(c, "kbv", [P, 2 * TB])
            nkb = self.sb(c, "nkb", [P, 2 * TB])
            sq = self.sb(c, "sq", [P, BY_ACT, P])
            ohp = self.sb(c, "ohp", [P, 2, CH, P], bf16)
            ohj = self.sb(c, "ohj", [P, 2, CH, P], bf16)
            Hp = self.ps(c, "Hp", [P, 2, CH, P])
            pre = self.ps(c, "pre", [P, 1])
            names = ("s_dig", "s_kp", "s_oa", "s_oj", "s_op", "s_mm", "s_add", "s_rs", "s_pre", "tick")
            s_dig, s_kp, s_oa, s_oj, s_op, s_mm, s_add, s_rs, s_pre, tick = (self.sem(c, n) for n in names)
            if scatter:
                each = NJ // (2 * NIT)
                srow = self.sb(c, "srow", [P, 2, each, W_XA])
                sidx = self.sb(c, "sidx", [P, 2, each], i32)
                s_st = self.sem(c, "s_st")
                s_sc = [self.sem(c, "s_sc") for _ in range(2)]
            block = c.enter_context(nc.Block())
            NS = 2 * STEPS
            GS = NS // 2

            @block.vector
            def _(v):
                key = self.edge[:, :, which]
                nc.vector.memset(H[:], 0.0)
                nc.vector.memset(Hp[:, 1], 0.0)
                nc.vector.tensor_scalar(kp[:], key, 1.0 / NJ, -0.495, ALU.mult, ALU.add)
                v.drain()
                nc.vector.tensor_scalar(kp[:], kp[:], MAGIC, MAGIC, ALU.add, ALU.subtract)
                v.drain().then_inc(s_dig, 1)
                nc.vector.scalar_tensor_tensor(kj[:], kp[:], -float(NJ), key, ALU.mult, ALU.add)
                v.drain()
                with v.Fori(0, NIT) as i:
                    nc.vector.tensor_copy(kbj[:], kj[:, bass.ds(i * 2 * TB, 2 * TB)])
                    nc.vector.tensor_copy(kbv[:], kp[:, bass.ds(i * 2 * TB, 2 * TB)])
                    v.drain()
                    for s in range(NS):
                        hold(v, s_mm, i * NS + s + 1, tick)
                        for k in range(CH):
                            oh = nc.vector.tensor_scalar(ohj[:, s % 2, k, 0:NJ], self.irow_b[:, 0:NJ],
                                                         kbj[:, s * CH + k:s * CH + k + 1], None, ALU.is_equal)
                        for k in range(by_pool + BY_ACT, CH):
                            oh = nc.vector.tensor_scalar(ohp[:, s % 2, k, :], self.irow_b[:], kbv[:, s * CH + k:s * CH + k + 1], None, ALU.is_equal)
                        oh.then_inc(s_oj, 1)
                        if s % GS == 1:
                            nc.vector.tensor_tensor(H[:], H[:], Hp[:, (s // GS + 1) % 2, :, 0:NJ], ALU.add)
                            v.drain().then_inc(s_add, 1)
                    v.drain()
                v.wait_ge(s_mm, NIT * NS + 2)
                nc.vector.tensor_tensor(H[:], H[:], Hp[:, 1, :, 0:NJ], ALU.add)
                v.drain()
                nc.vector.tensor_tensor(cnt[:], H[:, 0, :], H[:, 1, :], ALU.add)
                for k in range(2, CH):
                    v.drain()
                    nc.vector.tensor_tensor(cnt[:], cnt[:], H[:, k, :], ALU.add)
                v.drain()
                nc.vector.tensor_tensor_scan(incl[:], self.ones[:, 0:NJ], cnt[:], 0.0, ALU.mult, ALU.add)
                v.drain().then_inc(s_rs, 1)
                v.wait_ge(s_pre, 1)
                nc.vector.tensor_tensor(start[:], incl[:], cnt[:], ALU.subtract)
                v.drain()
                nc.vector.tensor_scalar(start[:], start[:], pre[:, 0:1], None, ALU.add)
                nc.vector.tensor_scalar(full[:], cnt[:], 0.0, None, ALU.is_gt)
                v.drain()
                nc.vector.tensor_copy(C[:, 0, :], start[:])
                for k in range(1, CH):
                    v.drain()
                    nc.vector.tensor_tensor(C[:, k, :], C[:, k - 1, :], H[:, k - 1, :], ALU.add)
                nc.vector.tensor_scalar(t1[:], self.inode[:], float(E_PAD), None, ALU.add)
                nc.vector.scalar_tensor_tensor(t2[:], start[:], -1.0 - E_PAD, cnt[:], ALU.add, ALU.add)
                v.drain()
                nc.vector.tensor_tensor(start[:], start[:], t1[:], ALU.subtract)
                nc.vector.tensor_tensor(t2[:], t2[:], full[:], ALU.mult)
                v.drain()
                nc.vector.tensor_tensor(start[:], start[:], full[:], ALU.mult)
                nc.vector.tensor_scalar(last[:], t2[:], float(E_PAD), None, ALU.add)
                v.drain()
                nc.vector.tensor_tensor(first[:], start[:], t1[:], ALU.add)

            @block.gpsimd
            def _(pool):
                def stage(i, h):
                    idx, rows = scatter
                    at = bass.ds((i * 2 + h) * each, each)
                    nc.gpsimd.tensor_copy(sidx[:, h], idx[:, at])
                    nc.gpsimd.tensor_copy(srow[:, h], rows[:, at, :]).then_inc(s_st, 1)

                if scatter:
                    pool.wait_ge(self.s_zx, self.zeroed_x)
                    for h in range(2):
                        stage(0, h)
                pool.wait_ge(s_dig, 1)

                def round_(i, last=False):
                    hold(pool, s_mm, i * NS + 2, tick)
                    nc.gpsimd.tensor_copy(kbp[:], kp[:, bass.ds(i * 2 * TB, 2 * TB)]).then_inc(s_kp, 1)
                    hold(pool, s_kp, i + 1, tick)
                    for s in range(NS):
                        hold(pool, s_mm, i * NS + s + 1, tick)
                        for k in range(by_pool):
                            oh = nc.gpsimd.tensor_scalar(ohp[:, s % 2, k, :], self.irow_b[:], kbp[:, s * CH + k:s * CH + k + 1], None, ALU.is_equal)
                        oh.then_inc(s_op, 1)
                        if scatter:
                            h, k = s // STEPS, s % STEPS
                            if k < each:
                                hold(pool, s_st, i * 2 + h + 1, tick)
                                nc.gpsimd.indirect_dma_start(self.z_x[:, :], bass.IndirectOffsetOnAxis(sidx[:, h, k:k + 1], 0),
                                                             srow[:, h, k, :], None).then_inc(s_sc[h], 16)
                            if k == STEPS - 1 and not last:
                                hold(pool, s_sc[h], (i + 1) * (16 * each), tick)
                                stage(i + 1, h)
                with pool.Fori(0, LAST) as i:
                    round_(i)
                round_(LAST, True)
                if scatter:
                    for h in range(2):
                        pool.wait_ge(s_sc[h], NIT * 16 * each)

            @block.scalar
            def _(act):
                act.wait_ge(s_dig, 1)
                with act.Fori(0, NIT) as i:
                    nc.scalar.activation(nkb[:], kp[:, bass.ds(i * 2 * TB, 2 * TB)], ACT.Copy, scale=-1.0)
                    for s in range(NS):
                        act.drain()
                        for k in range(BY_ACT):
                            t = s * CH + by_pool + k
                            nc.scalar.activation(sq[:, k, :], self.irow[:], ACT.Square, bias=nkb[:, t:t + 1])
                        act.drain()
                        hold(act, s_mm, i * NS + s + 1, tick)
                        nc.scalar.activation(ohp[:, s % 2, by_pool:by_pool + BY_ACT, :], sq[:], ACT.Relu, bias=1.0, scale=-1.0).then_inc(s_oa, 1)
                    act.drain()

            if on_sync:
                @block.sync
                def _(sp):
                    on_sync(sp)

            @block.tensor
            def _(pe):
                pe.sem_inc(s_mm, 1)
                pe.sem_inc(s_mm, 1)
                pe.sem_inc(s_add, 1)
                with pe.Fori(0, NIT) as i:
                    for s in range(NS):
                        hold(pe, s_oj, i * NS + s + 1, tick)
                        hold(pe, s_op, i * NS + s + 1, tick)
                        hold(pe, s_oa, i * NS + s + 1, tick)
                        if s % GS == 0:
                            hold(pe, s_add, i * 2 + s // GS + 1, tick)
                        for k in range(CH):
                            mm = nc.tensor.matmul(Hp[:, s // GS, k, 0:NJ], ohp[:, s % 2, k, :], ohj[:, s % 2, k, 0:NJ],
                                                  start=(s % GS == 0 and k % 4 == 0), stop=(s % GS == GS - 1),
                                                  skip_group_check=True)
                        mm.then_inc(s_mm, 1)
                pe.wait_ge(s_rs, 1)
                nc.tensor.matmul(pre[:], self.tri[:], incl[:, NJ - 1:NJ], start=True, stop=True).then_inc(s_pre, 1)

    def sort(self, digits, C, W, rows, prepare, loads):
        nc = self.nc
        kp, kj = digits
        with ExitStack() as c:
            pay = self.sb(c, "pay", [P, 2, TB, W])
            pos = self.sb(c, "pos", [P, 2, TB], i32)
            kb = self.sb(c, "kb", [P, 2, 2 * TB + 2 * CH])
            ohp = self.sb(c, "ohp", [P, 4, CH, P], bf16)
            ohj = self.sb(c, "ohj", [P, 4, CH, P], bf16)
            ohT = self.sb(c, "ohT", [P, 2, CH, P])
            ohTb = self.sb(c, "ohTb", [P, 2, CH, P], bf16)
            Lm = self.sb(c, "Lm", [P, CH, P], bf16)
            g = self.sb(c, "g", [P, 2, CH, NJ])
            posf = self.sb(c, "posf", [P, CH])
            pT = self.ps(c, "pT", [P, CH, P], bf16)
            pS = self.ps(c, "pS", [P, CH, P])
            pD = self.ps(c, "pD", [P, CH, P])
            pG = self.ps(c, "pG", [P, CH, P])
            names = ("s_oh", "s_T", "s_cp", "s_S", "s_L", "s_G", "s_C", "s_D", "s_pos", "tick", "s_pre")
            s_oh, s_T, s_cp, s_S, s_L, s_G, s_C, s_D, s_pos, tick, s_prep = (self.sem(c, n) for n in names)
            s_ld = [self.sem(c, "s_ld") for _ in range(2)]
            s_sc = [self.sem(c, "s_sc") for _ in range(2)]
            s_free = [self.sem(c, "s_free") for _ in range(2)]
            s_pay = self.sem(c, "s_pay")
            fill = prepare(c)
            nload = loads(None, None, None, None)
            nkey = 1 if fill else 2
            block = c.enter_context(nc.Block())
            NS = 2 * STEPS
            target = rows

            @block.vector
            def _(v):
                def onehots(s, buf):
                    for k in range(CH):
                        t = s * CH + k
                        nc.vector.tensor_scalar(ohp[:, buf, k, :], self.irow_b[:], kb[:, 0, t:t + 1], None, ALU.is_equal)
                        nc.vector.tensor_scalar(ohj[:, buf, k, 0:NJ], self.irow_b[:, 0:NJ], kb[:, 1, t:t + 1], None, ALU.is_equal)
                    v.drain().then_inc(s_oh, 1)

                def place(i, s):
                    h, o = s // STEPS, (s % STEPS) * CH
                    if s % STEPS == 0:
                        hold(v, s_ld[h], (i + 1) * (16 * nload), tick)
                    v.drain()
                    nc.vector.tensor_reduce(posf[:], g[:, s % 2], AX.X, ALU.add)
                    v.drain()
                    nc.vector.tensor_copy(pos[:, h, o:o + CH], posf[:]).then_inc(s_pos, 1)

                nc.vector.memset(pay[:], 0.0)
                nc.vector.tensor_copy(kb[:, 0, 0:2 * CH], kp[:, 0:2 * CH])
                nc.vector.tensor_copy(kb[:, 1, 0:2 * CH], kj[:, 0:2 * CH])
                v.drain().then_inc(s_prep, 1)
                onehots(0, 0)
                onehots(1, 1)
                v.drain()
                if fill:
                    fill.first(v)
                def round_(i):
                    nc.vector.tensor_copy(kb[:, 0, :], kp[:, bass.ds(i * 2 * TB, 2 * TB + 2 * CH)])
                    nc.vector.tensor_copy(kb[:, 1, :], kj[:, bass.ds(i * 2 * TB, 2 * TB + 2 * CH)])
                    for s in range(NS):
                        h = s // STEPS
                        hold(v, s_S, i * NS + s + 1, tick)
                        nc.vector.tensor_tensor(Lm[:], pS[:], self.tri_b[:].unsqueeze(1).to_broadcast([P, CH, P]), ALU.mult).then_inc(s_L, 1)
                        if s > 0:
                            place(i, s - 1)
                        else:
                            v.drain()
                        onehots(s + 2, (s + 2) % 4)
                        if fill and not (isinstance(i, int) and s >= STEPS):
                            fill.scan(v, i, s)
                        hold(v, s_G, i * NS + s + 1, tick)
                        hold(v, s_D, i * NS + s + 1, tick)
                        nc.vector.tensor_tensor(C[:], C[:], pD[:, :, 0:NJ], ALU.add).then_inc(s_C, 1)
                        nc.vector.tensor_tensor(g[:, s % 2], pG[:, :, 0:NJ], ohj[:, s % 4, :, 0:NJ], ALU.mult)
                    v.drain()
                    place(i, NS - 1)
                    v.drain()

                with v.Fori(0, LAST) as i:
                    round_(i)
                round_(LAST)

            @block.scalar
            def _(act):
                def copies(buf):
                    nc.scalar.copy(ohTb[:, buf], pT[:])
                    nc.scalar.copy(ohT[:, buf], pT[:]).then_inc(s_cp, 1)
                if fill:
                    fill.begin(act)
                for n in range(2):
                    act.wait_ge(s_T, n + 1)
                    copies(n)

                def round_(i, last=False):
                    for s in range(NS):
                        h = s // STEPS
                        if s % STEPS == 0:
                            hold(act, s_ld[h], (i + 1) * (16 * nload), tick)
                            at = bass.ds((i * 2 + h) * TB, TB)
                            if fill:
                                fill.deliver(act, i, h, pay)
                            nc.scalar.copy(pay[:, h, :, 0:nkey], self.edge[:, at, 2 - nkey:2]).then_inc(s_pay, 1)
                        hold(act, s_T, i * NS + s + 3, tick)
                        copies(s % 2)
                        if fill and s % STEPS == 0 and not last:
                            fill.next(act, i, h)
                with act.Fori(0, LAST) as i:
                    round_(i)
                round_(LAST, True)

            @block.tensor
            def _(pe):
                def turn(buf):
                    for k in range(CH):
                        mm = nc.tensor.transpose(pT[:, k, :], ohp[:, buf, k, :], self.ident_b[:])
                    mm.then_inc(s_T, 1)

                def pairs(buf):
                    for k in range(CH):
                        mm = nc.tensor.matmul(pS[:, k, :], ohTb[:, buf, k, :], ohTb[:, buf, k, :], start=True, stop=True)
                    mm.then_inc(s_S, 1)

                def counts(buf):
                    for k in range(CH):
                        mm = nc.tensor.matmul(pD[:, k, 0:NJ], ohp[:, buf, k, :], ohj[:, buf, k, 0:NJ], start=True, stop=True)
                    mm.then_inc(s_D, 1)

                pe.wait_ge(s_oh, 1)
                turn(0)
                pe.wait_ge(s_cp, 1)
                pairs(0)
                counts(0)
                pe.wait_ge(s_oh, 2)
                turn(1)
                with pe.Fori(0, NIT) as i:
                    for s in range(NS):
                        hold(pe, s_L, i * NS + s + 1, tick)
                        for k in range(CH):
                            nc.tensor.matmul(pG[:, k, 0:NJ], ohT[:, s % 2, k, :], C[:, k, :], start=True, stop=False)
                            mm = nc.tensor.matmul(pG[:, k, 0:NJ], Lm[:, k, :], ohj[:, s % 4, k, 0:NJ], start=False, stop=True)
                        mm.then_inc(s_G, 1)
                        hold(pe, s_cp, i * NS + s + 2, tick)
                        pairs((s + 1) % 2)
                        hold(pe, s_C, i * NS + s + 1, tick)
                        counts((s + 1) % 4)
                        hold(pe, s_oh, i * NS + s + 3, tick)
                        turn((s + 2) % 4)

            @block.gpsimd
            def _(pool):
                with pool.Fori(0, NIT) as i:
                    for s in range(NS):
                        h = s // STEPS
                        if s % STEPS == 0:
                            hold(pool, s_pay, i * 2 + h + 1, tick)
                        hold(pool, s_pos, i * NS + s + 1, tick)
                        for k in range(CH):
                            t = (s % STEPS) * CH + k
                            nc.gpsimd.indirect_dma_start(target[:, :], bass.IndirectOffsetOnAxis(pos[:, h, t:t + 1], 0),
                                                         pay[:, h, t, :], None).then_inc(s_sc[h], 16)
                for h in range(2):
                    pool.wait_ge(s_sc[h], NIT * TB * 16)

            @block.sync
            def _(sp):
                sp.wait_ge(s_prep, 1)
                for h in range(2):
                    loads(sp, 0, h, (pay, s_ld[h]))
                    if fill:
                        fill.load(sp, 0, h)
                with sp.Fori(0, NIT - 1) as i:
                    for h in range(2):
                        if fill:
                            fill.free(sp, i, h)
                            fill.load(sp, i + 1, h)
                        hold(sp, s_sc[h], (i + 1) * (TB * 16), tick)
                        loads(sp, i + 1, h, (pay, s_ld[h]))

    def sort_by_dst(self, first_d, last_d):
        nc, a = self.nc, self.a
        self.ds = self.dram("ds", (E_PAD, W_DS))
        a16 = a["edge_attr_16"].rearrange("(p t) f -> p t f", t=T)
        a32 = a["edge_attr_32"].rearrange("(p t) f -> p t f", t=T)
        dsv = self.ds.rearrange("(p t) w -> p t w", t=T)
        with ExitStack() as c:
            digits = [self.sb(c, n, [P, T + 2 * CH]) for n in ("kp", "kj")]
            C = self.sb(c, "C", [P, CH, NJ])
            falls = self.sb(c, "falls", [P, 1], i32)
            self.lay_down(falls, dsv, a16, a32)
            self.csr(c, digits, 0, C, first_d, last_d, 3, on_sync=self.clear_x)

            def loads(sp, i, h, to):
                if sp is not None:
                    pay, done = to
                    at = bass.ds((i * 2 + h) * TB, TB)
                    for lo, hi in SPLITS:
                        sp.dma_start(pay[lo:hi, h, :, 2:2 + ATTR], a16[lo:hi, at, :]).then_inc(done, 16)
                        sp.dma_start(pay[lo:hi, h, :, 2 + ATTR:W_DS], a32[lo:hi, at, :]).then_inc(done, 16)
                return 4

            self.laid_down()
            unsorted = nc.values_load(falls[0:1, 0:1], min_val=0, max_val=E_PAD)
            with nc.If(unsorted > 0):
                self.sort(digits, C, W_DS, self.ds, lambda c: None, loads)
                self.reload_keys()

    def reload_keys(self):
        nc = self.nc
        with ExitStack() as c:
            s_l = self.sem(c, "s_l")
            block = c.enter_context(nc.Block())

            @block.sync
            def _(sp):
                with nc.allow_non_contiguous_dma(reason="key columns of the sorted rows"):
                    sp.dma_start(self.edge[:, 0:T, :], self.ds.rearrange("(p t) w -> p t w", t=T)[:, :, 0:2]).then_inc(s_l, 16)
                sp.wait_ge(s_l, 16)

    def lay_down(self, falls, dsv, a16, a32):
        nc = self.nc
        self.s_lay = self.sem(self.top, "s_lay")
        with ExitStack() as c:
            prev, last, n = (self.sb(c, k, [P, 1]) for k in ("prev", "lastk", "n"))
            lt = self.sb(c, "lt", [P, T])
            pn = self.ps(c, "pn", [P, 1])
            s_a, s_b, s_n, s_m = (self.sem(c, k) for k in ("s_a", "s_b", "s_n", "s_m"))
            block = c.enter_context(nc.Block())

            @block.vector
            def _(v):
                key = self.edge[:, 0:T, 0]
                nc.vector.memset(prev[:], -1.0)
                nc.vector.tensor_copy(last[:], key[:, T - 1:T])
                v.drain().then_inc(s_a, 1)
                nc.vector.tensor_tensor(lt[:, 1:T], key[:, 1:T], key[:, 0:T - 1], ALU.is_lt)
                v.wait_ge(s_b, 16)
                nc.vector.tensor_tensor(lt[:, 0:1], key[:, 0:1], prev[:], ALU.is_lt)
                v.drain()
                nc.vector.reduce_sum(n[:], lt[:], AX.X)
                v.drain().then_inc(s_n, 1)
                v.wait_ge(s_m, 1)
                nc.vector.tensor_copy(falls[:], pn[:])

            @block.tensor
            def _(pe):
                pe.wait_ge(s_n, 1)
                nc.tensor.matmul(pn[:], self.ones[:], n[:], start=True, stop=True).then_inc(s_m, 1)

            @block.sync
            def _(sp):
                sp.wait_ge(s_a, 1)
                sp.dma_start(prev[1:P, :], last[0:P - 1, :]).then_inc(s_b, 16)
                sp.wait_ge(s_b, 16)

            @block.scalar
            def _(act):
                act.wait_ge(s_b, 16)
                pads = self.ds[E:E_PAD].rearrange("a w -> (a w)").rearrange("(p c) -> p c", p=P)
                piece = pads.shape[1] // 3
                for k in range(3):
                    act.dma_start(pads[:, k * piece:(k + 1) * piece], self.zero[:, 0:piece]).then_inc(self.s_lay, 16)
                act.wait_ge(self.s_lay, 48)
                with nc.allow_non_contiguous_dma(reason="key columns"):
                    act.dma_start(dsv[:, :, 0:2], self.edge[:, 0:T, :]).then_inc(self.s_lay, 16)
                for lo, hi in SPLITS:
                    act.dma_start(dsv[lo:hi, :, 2:2 + ATTR], a16[lo:hi]).then_inc(self.s_lay, 16)
                    act.dma_start(dsv[lo:hi, :, 2 + ATTR:W_DS], a32[lo:hi]).then_inc(self.s_lay, 16)

    def clear(self, sp, z, done, before=None):
        w = z.shape[1]
        rows = z[0:E_PAD].rearrange("(p t) w -> p (t w)", p=P)
        for k in range(2 * w):
            sp.dma_start(rows[:, k * T // 2:(k + 1) * T // 2], self.zero[:]).then_inc(done, 16)
            if before is not None:
                sp.wait_ge(done, before + 16 * (k + 1))
        return 16 * 2 * w

    def clear_x(self, sp):
        self.zeroed_x = self.clear(sp, self.z_x, self.s_zx)

    def clear_rest(self, sp):
        self.zeroed = self.clear(sp, self.z_e, self.s_z, 0)
        self.zeroed += self.clear(sp, self.z_2, self.s_z, self.zeroed)
        for s in (self.s_v, self.s_m, self.s_1, self.s_1b, self.s_2):
            sp.dma_start(s[E_PAD:E_PAD + 1, :], self.zero[0:1, 0:s.shape[1]]).then_inc(self.s_z, 16)
            self.zeroed += 16

    def laid_down(self):
        with self.nc.Block() as block:
            @block.sync
            def _(sp):
                sp.wait_ge(self.s_lay, 16 * 8)

    def cleared(self):
        with self.nc.Block() as block:
            @block.sync
            def _(sp):
                sp.wait_ge(self.s_z, self.zeroed)

    def order_tiles(self, ctx):
        return {
            "cont": self.sb(ctx, "cont", [P, T]),
            "contm": self.sb(ctx, "contm", [P, T]),
            "fix": self.sb(ctx, "fix", [P, 1], i32),
            "w": self.sb(ctx, "w", [P, P]),
            "wm": self.sb(ctx, "wm", [P, P]),
        }

    def order(self, ctx, key, o=None):
        nc = self.nc
        o = o or self.order_tiles(ctx)
        with ExitStack() as c:
            prev = self.sb(c, "prev", [P, 1])
            last = self.sb(c, "lastk", [P, 1])
            n, whole = self.sb(c, "n", [P, 1]), self.sb(c, "whole", [P, 1])
            eq = self.sb(c, "eq", [P, T])
            wb = self.sb(c, "wb", [P, P])
            pw = self.ps(c, "pw", [P, P])
            s_a, s_b, s_w, s_m = (self.sem(c, n_) for n_ in ("s_a", "s_b", "s_w", "s_m"))
            block = c.enter_context(nc.Block())

            @block.sync
            def _(sp):
                sp.wait_ge(s_a, 1)
                sp.dma_start(prev[1:P, :], last[0:P - 1, :]).then_inc(s_b, 16)
                sp.wait_ge(s_b, 16)

            @block.tensor
            def _(pe):
                pe.wait_ge(s_w, 1)
                nc.tensor.matmul(pw[:], wb[:], self.ident[:], start=True, stop=True).then_inc(s_m, 1)

            @block.vector
            def _(v):
                nc.vector.memset(prev[:], -1.0)
                nc.vector.tensor_copy(last[:], key[:, T - 1:T])
                v.drain().then_inc(s_a, 1)
                nc.vector.tensor_copy(eq[:], key)
                v.drain()
                nc.vector.tensor_tensor(o["cont"][:, 1:T], eq[:, 1:T], eq[:, 0:T - 1], ALU.is_equal)
                v.wait_ge(s_b, 16)
                nc.vector.tensor_tensor(o["cont"][:, 0:1], eq[:, 0:1], prev[:], ALU.is_equal)
                v.drain()
                nc.vector.tensor_scalar(o["contm"][:], o["cont"][:], 2.0, -1.0, ALU.mult, ALU.add)
                nc.vector.tensor_scalar(wb[:, 0:1], eq[:, 0:1], 1.0, None, ALU.mult)
                v.drain()
                nc.vector.tensor_scalar(o["contm"][:], o["contm"][:], BIG, None, ALU.mult)
                nc.vector.tensor_scalar(eq[:], eq[:], wb[:, 0:1], None, ALU.is_equal)
                v.drain()
                nc.vector.reduce_sum(n[:], eq[:], AX.X)
                v.drain()
                nc.vector.tensor_scalar(whole[:], n[:], float(T), None, ALU.is_equal)
                nc.vector.scalar_tensor_tensor(n[:], self.ipart[:], float(T), n[:], ALU.mult, ALU.add)
                v.drain()
                nc.vector.tensor_scalar(o["fix"][:], n[:], 1.0, None, ALU.subtract)
                nc.vector.tensor_tensor(whole[:], whole[:], o["cont"][:, 0:1], ALU.mult)
                v.drain()
                nc.vector.tensor_scalar(wb[:], self.ones[:], whole[:, 0:1], None, ALU.mult)
                v.drain().then_inc(s_w, 1)
                v.wait_ge(s_m, 1)
                nc.vector.tensor_copy(o["w"][:], pw[:])
                v.drain()
                nc.vector.tensor_scalar(o["wm"][:], o["w"][:], 2.0, -1.0, ALU.mult, ALU.add)
                v.drain()
                nc.vector.tensor_scalar(o["wm"][:], o["wm"][:], BIG, None, ALU.mult)
        return o

    def join(self, o, tail, W, s, is_max):
        nc = self.nc
        neutral = -BIG if is_max else 0.0
        ops = (ALU.min, ALU.max) if is_max else (ALU.mult, ALU.add)
        groups = [(lo, min(lo + P, W)) for lo in range(0, W, P)]
        with ExitStack() as c:
            tT = self.sb(c, "tT", [P, P])
            sT = self.sb(c, "sT", [P, P + 1])
            carry = self.sb(c, "carry", [P, W])
            row = self.sb(c, "row", [P, W])
            pt = self.ps(c, "pt", [P, P])
            pb = self.ps(c, "pb", [P, P])
            s_t, s_s, s_b, s_g, s_r, s_o, s_d = (self.sem(c, n) for n in ("s_t", "s_s", "s_b", "s_g", "s_r", "s_o", "s_d"))
            block = c.enter_context(nc.Block())

            @block.tensor
            def _(pe):
                for k, (lo, hi) in enumerate(groups):
                    if k:
                        pe.wait_ge(s_d, k)
                    nc.tensor.transpose(pt[0:hi - lo, :], tail[:, lo:hi], self.ident[:]).then_inc(s_t, 1)
                    pe.wait_ge(s_s, k + 1)
                    nc.tensor.transpose(pb[:, 0:hi - lo], sT[0:hi - lo, 0:P], self.ident[0:hi - lo, 0:hi - lo]).then_inc(s_b, 1)

            @block.vector
            def _(v):
                nc.vector.memset(sT[:], neutral)
                v.drain()
                for k, (lo, hi) in enumerate(groups):
                    n = hi - lo
                    v.wait_ge(s_t, k + 1)
                    nc.vector.tensor_copy(tT[0:n, :], pt[0:n, :])
                    v.drain()
                    nc.vector.tensor_tensor_scan(sT[0:n, 1:P + 1], o["wm" if is_max else "w"][0:n, :], tT[0:n, :], neutral, *ops)
                    v.drain().then_inc(s_s, 1)
                    v.wait_ge(s_b, k + 1)
                    nc.vector.tensor_scalar(carry[:, lo:hi], pb[:, 0:n], o["contm" if is_max else "cont"][:, 0:1], None, ops[0])
                    v.drain().then_inc(s_d, 1)
                v.wait_ge(s_g, 16)
                nc.vector.tensor_tensor(row[:], row[:], carry[:], ops[1])
                v.drain().then_inc(s_r, 1)

            @block.gpsimd
            def _(pool):
                nc.gpsimd.indirect_dma_start(row[:], None, s[:, :], bass.IndirectOffsetOnAxis(o["fix"][:, 0:1], 0)).then_inc(s_g, 16)
                pool.wait_ge(s_r, 1)
                nc.gpsimd.indirect_dma_start(s[:, :], bass.IndirectOffsetOnAxis(o["fix"][:, 0:1], 0), row[:], None).then_inc(s_o, 16)
                pool.wait_ge(s_o, 16)

    def fetch(self, s, idx, out):
        nc = self.nc
        with ExitStack() as c:
            s_g = self.sem(c, "s_g")
            block = c.enter_context(nc.Block())

            @block.gpsimd
            def _(pool):
                for j in range(NJ):
                    nc.gpsimd.indirect_dma_start(out[:, j, :], None, s[:, :], bass.IndirectOffsetOnAxis(idx[:, j:j + 1], 0)).then_inc(s_g, 16)
                pool.wait_ge(s_g, 16 * NJ)

    def spread(self, z, idx, rows, table=None):
        nc = self.nc
        with ExitStack() as c:
            s_g, s_t = self.sem(c, "s_g"), self.sem(c, "s_t")
            block = c.enter_context(nc.Block())

            @block.gpsimd
            def _(pool):
                for j in range(NJ if z is not None else 0):
                    nc.gpsimd.indirect_dma_start(z[:, :], bass.IndirectOffsetOnAxis(idx[:, j:j + 1], 0), rows[:, j, :], None).then_inc(s_g, 16)
                if z is not None:
                    pool.wait_ge(s_g, 16 * NJ)

            @block.sync
            def _(sp):
                if table is not None:
                    sp.dma_start(table.rearrange("(p j) f -> p j f", j=NJ), rows[:]).then_inc(s_t, 16)
                    sp.wait_ge(s_t, 16)

    def first_rows(self, table, idx, out):
        nc = self.nc
        with ExitStack() as c:
            s_g = self.sem(c, "s_g")
            block = c.enter_context(nc.Block())

            @block.gpsimd
            def _(pool):
                nc.gpsimd.indirect_dma_start(out[:], None, table[:, :], bass.IndirectOffsetOnAxis(idx, 0)).then_inc(s_g, 16)
                pool.wait_ge(s_g, 16)

    def dense(self, src, J, K, M, weights, post, idx=None, s=None, prepare=None):
        nc = self.nc
        G, SUB = NJ // 4, 4 // J
        PIECE = 5
        with ExitStack() as c:
            xT = self.sb(c, "xT", [P, 2, SUB * P])
            pt = [self.ps(c, "pt", [P, SUB * P]) for _ in range(2)]
            po = [self.ps(c, "po", [P, 4, M]) for _ in range(2)]
            s_t, s_c, s_m, s_p, s_r = (self.sem(c, n) for n in ("s_t", "s_c", "s_m", "s_p", "s_r"))
            s_g = [self.sem(c, "s_g") for _ in range(G // PIECE)] if s is not None else []
            block = c.enter_context(nc.Block())

            @block.gpsimd
            def _(pool):
                for n, got in enumerate(s_g):
                    for j in range(n * 4 * PIECE, (n + 1) * 4 * PIECE):
                        nc.gpsimd.indirect_dma_start(src[:, j, :], None, s[:, :], bass.IndirectOffsetOnAxis(idx[:, j:j + 1], 0)).then_inc(got, 16)

            @block.tensor
            def _(pe):
                for g in range(G + 1):
                    if g < G:
                        if s_g and g % PIECE == 0:
                            pe.wait_ge(s_r, g // PIECE + 1)
                        if g >= 2:
                            pe.wait_ge(s_c, g - 1)
                        for k in range(SUB):
                            at = src[:, g * 4 + k * J:g * 4 + (k + 1) * J, 0:K].rearrange("p j k -> p (j k)") if J > 1 else src[:, g * 4 + k, 0:K]
                            mm = nc.tensor.transpose(pt[g % 2][0:J * K, k * P:(k + 1) * P], at, self.ident[:])
                        mm.then_inc(s_t, 1)
                    if g >= 1:
                        pe.wait_ge(s_c, g)
                        if g >= 3:
                            pe.wait_ge(s_p, g - 2)
                        for k in range(SUB):
                            mm = nc.tensor.matmul(po[(g - 1) % 2][:, k * J:(k + 1) * J, :].rearrange("p j m -> p (j m)"),
                                                  xT[0:J * K, (g - 1) % 2, k * P:(k + 1) * P], weights, start=True, stop=True)
                        mm.then_inc(s_m, 1)

            @block.scalar
            def _(act):
                for g in range(G):
                    act.wait_ge(s_t, g + 1)
                    if g >= 2:
                        act.wait_ge(s_m, g - 1)
                    nc.scalar.copy(xT[0:J * K, g % 2, :], pt[g % 2][0:J * K, :]).then_inc(s_c, 1)

            @block.vector
            def _(v):
                def piece(n):
                    v.wait_ge(s_g[n], 16 * 4 * PIECE)
                    prepare(v, slice(n * 4 * PIECE, (n + 1) * 4 * PIECE))
                    v.drain().then_inc(s_r, 1)
                if s_g:
                    piece(0)
                for g in range(G):
                    if s_g and g % PIECE == 0 and g + PIECE < G:
                        piece(g // PIECE + 1)
                    v.wait_ge(s_m, g + 1)
                    post(v, g, po[g % 2])
                    v.drain().then_inc(s_p, 1)

    def block_diagonal(self, ctx, w, K, M, J=4, transform=None):
        nc = self.nc
        wd = self.sb(ctx, "wd", [P, J * M])
        with ExitStack() as c:
            s_z, s_l = self.sem(c, "s_z"), self.sem(c, "s_l")
            block = c.enter_context(nc.Block())

            @block.vector
            def _(v):
                nc.vector.memset(wd[:], 0.0)
                v.drain().then_inc(s_z, 1)

            @block.sync
            def _(sp):
                sp.wait_ge(s_z, 1)
                for j in range(J):
                    sp.dma_start(wd[j * K:(j + 1) * K, j * M:(j + 1) * M], w).then_inc(s_l, 16)
                sp.wait_ge(s_l, 16 * J)
        return wd[0:J * K, :]

    def row_of(self, ctx, b, n, J=1):
        nc = self.nc
        t = self.sb(ctx, "bias", [P, J, n])
        with ExitStack() as c:
            s_l = self.sem(c, "s_l")
            block = c.enter_context(nc.Block())

            @block.sync
            def _(sp):
                for j in range(J):
                    sp.dma_start(t[:, j, :], b.rearrange("(o n) -> o n", o=1).to_broadcast([P, n])).then_inc(s_l, 16)
                sp.wait_ge(s_l, 16 * J)
        return t

    def norm(self, y):
        nc = self.nc
        with ExitStack() as c:
            m, q = self.sb(c, "m", [P, NJ]), self.sb(c, "q", [P, NJ])
            sq = self.sb(c, "sq", [P, NJ, F])
            s_v, s_q = self.sem(c, "s_v"), self.sem(c, "s_q")
            block = c.enter_context(nc.Block())
            wide = lambda t: t[:].unsqueeze(2).to_broadcast([P, NJ, F])

            @block.vector
            def _(v):
                nc.vector.reduce_sum(m[:], y[:], AX.X)
                v.drain()
                nc.vector.tensor_scalar(m[:], m[:], 1.0 / F, None, ALU.mult)
                v.drain()
                nc.vector.tensor_tensor(y[:], y[:], wide(m), ALU.subtract)
                v.drain()
                nc.vector.tensor_tensor(sq[:], y[:], y[:], ALU.mult)
                v.drain()
                nc.vector.reduce_sum(q[:], sq[:], AX.X)
                v.drain()
                nc.vector.tensor_scalar(q[:], q[:], 1.0 / F, 1e-5, ALU.mult, ALU.add)
                v.drain().then_inc(s_v, 1)
                v.wait_ge(s_q, 1)
                nc.vector.reciprocal(q[:], q[:])
                v.drain()
                nc.vector.tensor_tensor(self.x[:], y[:], wide(q), ALU.mult)

            @block.scalar
            def _(act):
                act.wait_ge(s_v, 1)
                nc.scalar.activation(q[:], q[:], ACT.Sqrt).then_inc(s_q, 1)

    def dst_order(self, ctx):
        nc = self.nc
        self.src_i = self.sb(ctx, "src_i", [P, T + 2 * TB], i32)
        self.key0_i = self.sb(ctx, "key0_i", [P, 1], i32)
        with nc.Block() as block:
            @block.vector
            def _(v):
                nc.vector.memset(self.src_i[:, T:], 0)
                nc.vector.tensor_copy(self.src_i[:, 0:T], self.edge[:, 0:T, 1])
                nc.vector.tensor_copy(self.key0_i[:], self.edge[:, 0:1, 0])
        return self.order(ctx, self.edge[:, 0:T, 0])

    def attention(self, d, first_d):
        nc, a = self.nc, self.a
        with ExitStack() as top:
            ab = self.sb(top, "ab", [P, NJ, 2 * HEADS])
            first_s, last_s = (self.sb(top, n, [P, NJ], i32) for n in ("first_s", "last_s"))
            sorting = top.enter_context(ExitStack())
            digits = [self.sb(sorting, n, [P, T + 2 * CH]) for n in ("kp", "kj")]
            C = self.sb(sorting, "C", [P, CH, NJ])
            self.ss = self.dram("ss", (E_PAD, W_SS))
            xa_d = self.dram("xa_d", (N_PAD, W_XA))
            with ExitStack() as c:
                xa = self.sb(c, "xa", [P, NJ, W_XA])
                w_s = self.sb(c, "w_s", [F, HEADS, F])
                fc = self.sb(c, "fc", [F, 2 * F])
                fcb = self.sb(c, "fcb", [P, 1])
                pr = self.sb(c, "pr", [F, 2, HEADS, F])
                u = self.sb(c, "u", [F, 2 * HEADS])
                ud = self.sb(c, "ud", [P, 4 * 2 * HEADS])
                with ExitStack() as cc:
                    s_l, s_u, s_d = (self.sem(cc, n) for n in ("s_l", "s_u", "s_d"))
                    block = cc.enter_context(nc.Block())

                    @block.sync
                    def _(sp):
                        sp.dma_start(w_s[:], a["L0_gnn_w"].rearrange("h f o -> f h o")).then_inc(s_l, 16)
                        sp.dma_start(fc[:], a["L0_gnn_fc_w"].to_broadcast([F, 2 * F])).then_inc(s_l, 16)
                        sp.dma_start(fcb[:], a["L0_gnn_fc_b"].rearrange("(o n) -> o n", o=1).to_broadcast([P, 1])).then_inc(s_l, 16)
                        sp.wait_ge(s_u, 1)
                        for j in range(4):
                            sp.dma_start(ud[j * F:(j + 1) * F, j * 8:(j + 1) * 8], u[:]).then_inc(s_d, 16)
                        sp.wait_ge(s_d, 64)

                    @block.vector
                    def _(v):
                        nc.vector.memset(ud[:], 0.0)
                        v.wait_ge(s_l, 48)
                        for k in range(2):
                            nc.vector.tensor_tensor(pr[:, k], w_s[:], fc[:, k * F:(k + 1) * F].unsqueeze(1).to_broadcast([F, HEADS, F]), ALU.mult)
                            v.drain()
                            nc.vector.reduce_sum(u[:, k * HEADS:(k + 1) * HEADS], pr[:, k], AX.X)
                        nc.vector.tensor_copy(xa[:, :, HEADS:W_XA], self.x[:])
                        v.drain().then_inc(s_u, 1)

                def post(v, g, po):
                    o = po
                    nc.vector.tensor_scalar(ab[:, 4 * g:4 * g + 4, 0:HEADS], o[:, :, 0:HEADS], fcb[:, 0:1], None, ALU.add)
                    nc.vector.tensor_copy(xa[:, 4 * g:4 * g + 4, 0:HEADS], o[:, :, HEADS:2 * HEADS])
                self.dense(self.x, 4, F, 2 * HEADS, ud[:], post)
                self.spread(None, None, xa, xa_d)
                self.csr(sorting, digits, 1, C, first_s, last_s, 2, (first_d, xa), self.clear_rest)
            self.cleared()

            z = self.z_x[0:E_PAD].rearrange("(p t) w -> p t w", t=T)
            dsv = self.ds.rearrange("(p t) w -> p t w", t=T)

            def loads(sp, i, h, to):
                if sp is not None:
                    pay, done = to
                    at = bass.ds((i * 2 + h) * TB, TB)
                    sp.dma_start(pay[:, h, :, 1 + W_XA:W_SS], dsv[:, at, 2 + ATTR:W_DS]).then_inc(done, 16)
                return 1
            self.sort(digits, C, W_SS, self.ss, lambda c: SpreadFill(self, c, d, z, xa_d), loads)
            sorting.close()

            o_ctx = top.enter_context(ExitStack())
            ssv = self.ss.rearrange("(p t) w -> p t w", t=T)
            key0 = self.sb(o_ctx, "key0", [P, 1], i32)
            s = self.order_tiles(o_ctx)
            with ExitStack() as c:
                ka = self.sb(c, "ka", [P, T, 1 + HEADS])
                mo = self.sb(c, "mo", [P, T, HEADS])
                s_l = self.sem(c, "s_l")
                with ExitStack() as cc:
                    block = cc.enter_context(nc.Block())

                    @block.sync
                    def _(sp):
                        sp.dma_start(ka[:], ssv[:, :, 0:1 + HEADS]).then_inc(s_l, 16)
                        sp.wait_ge(s_l, 16)

                    @block.vector
                    def _(v):
                        v.wait_ge(s_l, 16)
                        nc.vector.tensor_copy(key0[:], ka[:, 0:1, 0])
                self.order(None, ka[:, :, 0], s)
                with ExitStack() as cc:
                    s_v, s_o = self.sem(cc, "s_v"), self.sem(cc, "s_o")
                    block = cc.enter_context(nc.Block())

                    @block.vector
                    def _(v):
                        for k in range(HEADS):
                            nc.vector.tensor_tensor_scan(mo[:, :, k], s["contm"][:], ka[:, :, 1 + k], -BIG, ALU.min, ALU.max)
                        v.drain().then_inc(s_v, 1)

                    @block.sync
                    def _(sp):
                        sp.wait_ge(s_v, 1)
                        sp.dma_start(self.s_m[0:E_PAD].rearrange("(p t) w -> p t w", t=T), mo[:]).then_inc(s_o, 16)
                        sp.wait_ge(s_o, 16)
                self.join(s, mo[:, T - 1, :], HEADS, self.s_m, True)
            e_d = self.dram("e_d", (N_PAD, 2 * HEADS))
            with ExitStack() as c:
                mx = self.sb(c, "mx", [P, NJ, HEADS])
                self.fetch(self.s_m, last_s, mx)
                with ExitStack() as cc:
                    block = cc.enter_context(nc.Block())

                    @block.vector
                    def _(v):
                        nc.vector.tensor_tensor(mx[:], mx[:], ab[:, :, 0:HEADS], ALU.add)
                        v.drain()
                        nc.vector.scalar_tensor_tensor(ab[:, :, HEADS:], mx[:], 0.2, mx[:], ALU.mult, ALU.max)
                self.spread(self.z_e, first_s, ab, e_d)
            tail = self.sb(o_ctx, "tail", [P, W_V])
            self.attention_edges(s, tail, key0, e_d, ssv)
            self.join(s, tail, W_V, self.s_v, False)
            with ExitStack() as c:
                r = self.sb(c, "r", [P, NJ, W_V])
                self.attention_nodes(r, last_s)

    def attention_edges(self, s, tail, key0, e_d, ssv):
        nc = self.nc
        ze = self.z_e[0:E_PAD].rearrange("(p t) w -> p t w", t=T)
        sv = self.s_v[0:E_PAD].rearrange("(p t) w -> p t w", t=T)
        ROUNDS = T // (2 * TBA)
        HF = HEADS * F
        with ExitStack() as c:
            row = self.sb(c, "row", [P, 2, TBA, W_SS])
            ex = self.sb(c, "ex", [P, 2, TBA, 2 * HEADS])
            ecar = self.sb(c, "ecar", [P, 2 * HEADS])
            V = self.sb(c, "V", [P, 2, W_V, TBA])
            Vt = self.sb(c, "Vt", [P, 2, TBA, W_V])
            part = W_V // SUMS
            goes_on = self.sb(c, "goes_on", [P, 2, part, TBA])
            e = self.sb(c, "e", [P, 2, TBA, HEADS])
            p = self.sb(c, "p", [P, 2, TBA, HEADS])
            cb = self.sb(c, "cb", [P, 2, TBA])
            self.first_rows(e_d, key0[:, 0:1], ecar)
            s_ld = [self.sem(c, "s_ld") for _ in range(2)]
            s_st = [self.sem(c, "s_st") for _ in range(2)]
            names = ("s_e", "s_p", "s_x", "s_y", "s_w", "s_m", "s_v", "s_0", "tick")
            s_e, s_p, s_x, s_y, s_w, s_m, s_v, s_0, tick = (self.sem(c, n) for n in names)
            block = c.enter_context(nc.Block())

            def spot(i, h):
                return bass.ds((i * 2 + h) * TBA, TBA)

            def product(eng, h, k):
                x = row[:, h, :, 1 + HEADS:1 + W_XA].rearrange("p t f -> p f t")
                by = p[:, h, :, k:k + 1].rearrange("p t o -> p o t").to_broadcast([P, F, TBA])
                return eng.tensor_tensor(V[:, h, k * F:(k + 1) * F, :], x, by, ALU.mult)

            @block.vector
            def _(v):
                def scores(i, h):
                    nc.vector.tensor_copy(cb[:, h, :], s["cont"][:, spot(i, h)])
                    hold(v, s_ld[h], (i + 1) * 32, tick)
                    v.drain()
                    for k in range(2 * HEADS):
                        nc.vector.tensor_tensor_scan(ex[:, h, :, k], cb[:, h, :], ex[:, h, :, k], ecar[:, k:k + 1], ALU.mult, ALU.add)
                    v.drain()
                    nc.vector.tensor_copy(ecar[:], ex[:, h, TBA - 1, :])
                    nc.vector.tensor_tensor(e[:, h], ex[:, h, :, 0:HEADS], row[:, h, :, 1:1 + HEADS], ALU.add)
                    v.drain()
                    nc.vector.scalar_tensor_tensor(e[:, h], e[:, h], 0.2, e[:, h], ALU.mult, ALU.max)
                    v.drain()
                    nc.vector.tensor_tensor(e[:, h], e[:, h], ex[:, h, :, HEADS:], ALU.subtract).then_inc(s_e, 1)

                def sums(i, h):
                    b = i * 2 + h
                    hold(v, s_p, b + 1, tick)
                    hold(v, s_w, b + 1, tick)
                    for k in range(POOL_HEADS, HEADS):
                        product(nc.vector, h, k)
                    v.drain().then_inc(s_y, 1)
                    hold(v, s_x, b + 1, tick)
                    hold(v, s_m, b + 1, tick)
                    v.drain()
                    nc.vector.scalar_tensor_tensor(V[:, h, :, 0], tail[:], cb[:, h, 0:1], V[:, h, :, 0], ALU.mult, ALU.add)
                    v.drain()
                    for k in range(SUMS):
                        at = V[:, h, k * part:(k + 1) * part, :].rearrange("p f t -> p (f t)")
                        nc.vector.tensor_tensor_scan(at, goes_on[:, h].rearrange("p f t -> p (f t)"), at, 0.0, ALU.mult, ALU.add)
                    v.drain()
                    nc.vector.tensor_copy(tail[:], V[:, h, :, TBA - 1]).then_inc(s_v, 1)

                nc.vector.memset(tail[:], 0.0)
                nc.vector.memset(goes_on[:], 0.0)
                v.drain().then_inc(s_0, 1)
                scores(0, 0)
                with v.Fori(0, ROUNDS - 1) as i:
                    scores(i, 1)
                    sums(i, 0)
                    scores(i + 1, 0)
                    sums(i, 1)
                    v.drain()
                scores(ROUNDS - 1, 1)
                sums(ROUNDS - 1, 0)
                sums(ROUNDS - 1, 1)

            @block.scalar
            def _(act):
                def prepare(i, h):
                    b = i * 2 + h
                    hold(act, s_e, b + 1, tick)
                    nc.scalar.activation(p[:, h], e[:, h], ACT.Exp).then_inc(s_p, 1)
                    nc.scalar.copy(goes_on[:, h, :, 1:TBA], cb[:, h, 1:TBA].unsqueeze(1).to_broadcast([P, part, TBA - 1]))
                    hold(act, s_w, b + 1, tick)
                    nc.scalar.copy(V[:, h, HF + HEADS:, :], row[:, h, :, 1 + W_XA:].rearrange("p t f -> p f t"))
                    hold(act, s_p, b + 1, tick)
                    nc.scalar.copy(V[:, h, HF:HF + HEADS, :], p[:, h].rearrange("p t k -> p k t")).then_inc(s_x, 1)

                def turn(i, h):
                    hold(act, s_v, i * 2 + h + 1, tick)
                    hold(act, s_st[h], i * 16 + 1, tick)
                    nc.scalar.copy(Vt[:, h], V[:, h].rearrange("p w t -> p t w")).then_inc(s_w, 1)

                act.sem_inc(s_w, 1)
                act.sem_inc(s_w, 1)
                act.wait_ge(s_0, 1)
                prepare(0, 0)
                with act.Fori(0, ROUNDS - 1) as i:
                    prepare(i, 1)
                    turn(i, 0)
                    prepare(i + 1, 0)
                    turn(i, 1)
                prepare(ROUNDS - 1, 1)
                turn(ROUNDS - 1, 0)
                turn(ROUNDS - 1, 1)

            @block.gpsimd
            def _(pool):
                with pool.Fori(0, ROUNDS) as i:
                    for h in range(2):
                        hold(pool, s_p, i * 2 + h + 1, tick)
                        hold(pool, s_w, i * 2 + h + 1, tick)
                        for k in range(POOL_HEADS):
                            m = product(nc.gpsimd, h, k)
                        m.then_inc(s_m, 1)

            @block.sync
            def _(sp):
                def load(i, h):
                    sp.dma_start(row[:, h], ssv[:, spot(i, h), :]).then_inc(s_ld[h], 16)
                    sp.dma_start(ex[:, h], ze[:, spot(i, h), :]).then_inc(s_ld[h], 16)

                def taken(i, h):
                    hold(sp, s_x, i * 2 + h + 1, tick)
                    hold(sp, s_y, i * 2 + h + 1, tick)
                    hold(sp, s_m, i * 2 + h + 1, tick)

                def store(i, h):
                    hold(sp, s_w, i * 2 + h + 3, tick)
                    sp.dma_start(sv[:, spot(i, h), :], Vt[:, h]).then_inc(s_st[h], 16)
                for h in range(2):
                    sp.sem_inc(s_st[h], 1)
                    load(0, h)

                def round_(i, first=False):
                    taken(i, 0)
                    load(i + 1, 0)
                    if not first:
                        store(i - 1, 1)
                    taken(i, 1)
                    load(i + 1, 1)
                    store(i, 0)
                round_(0, first=True)
                with sp.Fori(1, ROUNDS - 1) as i:
                    round_(i)
                store(ROUNDS - 2, 1)
                for h in range(2):
                    store(ROUNDS - 1, h)
                for h in range(2):
                    sp.wait_ge(s_st[h], 16 * ROUNDS + 1)

    def attention_nodes(self, r, last_s):
        nc, a = self.nc, self.a
        HF = HEADS * F
        with ExitStack() as c:
            w = self.sb(c, "w0", [HF, F])
            y = self.sb(c, "y", [P, NJ, F])
            bias = self.row_of(c, a["L0_gnn_bias"], F, 4)
            d0 = self.sb(c, "d0", [P, NJ, HEADS])
            with ExitStack() as cc:
                s_l = self.sem(cc, "s_l")
                block = cc.enter_context(nc.Block())

                @block.sync
                def _(sp):
                    sp.dma_start(w[:], a["L0_gnn_w"].rearrange("h f o -> (h f) o")).then_inc(s_l, 16)
                    sp.wait_ge(s_l, 16)

            def prepare(v, j):
                n = j.stop - j.start
                den = r[:, j, HF:HF + HEADS]
                nc.vector.tensor_copy(self.edge_sum[:, j], r[:, j, HF + HEADS:])
                nc.vector.tensor_scalar(d0[:, j], den, 0.0, None, ALU.is_equal)
                v.drain()
                nc.vector.tensor_tensor(d0[:, j], d0[:, j], den, ALU.add)
                v.drain()
                nc.vector.tensor_scalar(d0[:, j], d0[:, j], float(HEADS), None, ALU.mult)
                v.drain()
                nc.vector.reciprocal(d0[:, j], d0[:, j])
                v.drain()
                for k in range(HEADS):
                    at = r[:, j, k * F:(k + 1) * F]
                    nc.vector.tensor_tensor(at, at, d0[:, j, k:k + 1].to_broadcast([P, n, F]), ALU.mult)

            def post(v, g, po):
                at = y[:, 4 * g:4 * g + 4, :]
                nc.vector.tensor_tensor(at, po[:], self.x[:, 4 * g:4 * g + 4, :], ALU.add)
                v.drain()
                nc.vector.tensor_tensor(at, at, bias[:], ALU.add)
            self.dense(r, 1, HF, F, w[:], post, last_s, self.s_v, prepare)
            self.norm(y)

    def gather_sum(self, d, y_d, s_dram, tail):
        nc = self.nc
        sv = s_dram[0:E_PAD].rearrange("(p t) w -> p t w", t=T)
        with ExitStack() as c:
            buf = self.sb(c, "buf", [P, 2, TB, HID])
            idx = self.sb(c, "idx", [P, 2, TB], i32)
            cb = self.sb(c, "cb", [P, 2, TB])
            s_g = [self.sem(c, "s_g") for _ in range(2)]
            s_st = [self.sem(c, "s_st") for _ in range(2)]
            s_free = [self.sem(c, "s_free") for _ in range(2)]
            s_i, s_v, tick = (self.sem(c, n) for n in ("s_i", "s_v", "tick"))
            block = c.enter_context(nc.Block())

            @block.scalar
            def _(act):
                with act.Fori(0, NIT) as i:
                    for h in range(2):
                        hold(act, s_free[h], i + 1, tick)
                        nc.scalar.copy(idx[:, h, :], self.src_i[:, bass.ds((i * 2 + h) * TB, TB)]).then_inc(s_i, 1)

            @block.gpsimd
            def _(pool):
                with pool.Fori(0, NIT) as i:
                    for h in range(2):
                        hold(pool, s_i, i * 2 + h + 1, tick)
                        for t in range(TB):
                            nc.gpsimd.indirect_dma_start(buf[:, h, t, :], None, y_d[:, :],
                                                         bass.IndirectOffsetOnAxis(idx[:, h, t:t + 1], 0)).then_inc(s_g[h], 16)

            @block.vector
            def _(v):
                nc.vector.memset(tail[:], 0.0)
                with v.Fori(0, NIT) as i:
                    for h in range(2):
                        nc.vector.tensor_copy(cb[:, h, :], d["cont"][:, bass.ds((i * 2 + h) * TB, TB)])
                        v.drain()
                        hold(v, s_g[h], (i + 1) * (16 * TB), tick)
                        for k in range(HID):
                            nc.vector.tensor_tensor_scan(buf[:, h, :, k], cb[:, h, :], buf[:, h, :, k], tail[:, k:k + 1], ALU.mult, ALU.add)
                        v.drain()
                        nc.vector.tensor_copy(tail[:], buf[:, h, TB - 1, :])
                        v.drain().then_inc(s_v, 1)

            @block.sync
            def _(sp):
                for h in range(2):
                    sp.sem_inc(s_free[h], 1)
                with sp.Fori(0, NIT) as i:
                    for h in range(2):
                        hold(sp, s_v, i * 2 + h + 1, tick)
                        sp.dma_start(sv[:, bass.ds((i * 2 + h) * TB, TB), :], buf[:, h]).then_inc(s_st[h], 16)
                        hold(sp, s_st[h], i * 16 + 16, s_free[h])

    def gin(self, d, last_d):
        nc, a = self.nc, self.a
        with ExitStack() as c:
            y = self.sb(c, "y", [P, NJ, HID])
            h = self.sb(c, "h", [P, NJ, HID])
            r = self.sb(c, "r", [P, NJ, F])
            tail = self.sb(c, "tail", [P, HID])
            w1 = self.block_diagonal(c, a["L1_gnn_W1"], F, HID)
            w2 = self.block_diagonal(c, a["L1_gnn_W2"], HID, F)
            w3 = self.block_diagonal(c, a["L1_gnn_W3"], F, HID)
            w4 = self.block_diagonal(c, a["L1_gnn_W4"], HID, F)
            b1 = self.row_of(c, a["L1_gnn_b1"], HID)
            b2 = self.row_of(c, a["L1_gnn_b2"], F, 4)
            b3 = self.row_of(c, a["L1_gnn_b3"], HID)
            b4 = self.row_of(c, a["L1_gnn_b4"], F, 4)

            def conv(x, w_in, b_in, w_out, post, y_d, s_dram):
                def keep(v, g, po):
                    nc.vector.tensor_copy(y[:, 4 * g:4 * g + 4, :], po[:])
                self.dense(x, 4, F, HID, w_in, keep)
                self.spread(None, None, y, y_d)
                self.gather_sum(d, y_d, s_dram, tail)
                self.join(d, tail, HID, s_dram, False)

                def relu(v, j):
                    nc.vector.tensor_tensor(h[:, j], h[:, j], y[:, j], ALU.add)
                    v.drain()
                    nc.vector.tensor_tensor(h[:, j], h[:, j], b_in[:].to_broadcast([P, 20, HID]), ALU.add)
                    v.drain()
                    nc.vector.tensor_scalar(h[:, j], h[:, j], 0.0, None, ALU.max)
                self.dense(h, 4, HID, F, w_out, post, last_d, s_dram, relu)

            def post_a(v, g, po):
                at = r[:, 4 * g:4 * g + 4, :]
                nc.vector.tensor_tensor(at, po[:], b2[:], ALU.add)
                v.drain()
                nc.vector.tensor_scalar(at, at, 0.0, None, ALU.max)

            def post_b(v, g, po):
                at = r[:, 4 * g:4 * g + 4, :]
                nc.vector.tensor_tensor(at, po[:], b4[:], ALU.add)
                v.drain()
                nc.vector.tensor_tensor(at, at, self.x[:, 4 * g:4 * g + 4, :], ALU.add)
            conv(self.x, w1, b1, w2, post_a, self.dram("y1", (N_PAD, HID)), self.s_1)
            conv(r, w3, b3, w4, post_b, self.dram("y2", (N_PAD, HID)), self.s_1b)
            self.norm(r)

    def edge_mlp(self, d, first_d, last_d):
        nc, a = self.nc, self.a
        D = 2 * F + ATTR
        with ExitStack() as top:
            x_d = self.dram("x_d", (N_PAD, F))
            self.spread(self.z_2, first_d, self.x, x_d)
            tail = self.sb(top, "tail", [P, F])
            z = self.z_2[0:E_PAD].rearrange("(p t) w -> p t w", t=T)
            dsv = self.ds.rearrange("(p t) w -> p t w", t=T)
            sv = self.s_2[0:E_PAD].rearrange("(p t) w -> p t w", t=T)
            with ExitStack() as c:
                w1 = self.sb(c, "w1", [D, MID + 1])
                b1 = self.sb(c, "b1", [64, 1])
                w2 = self.sb(c, "w2", [MID + 1, F])
                car = self.sb(c, "car", [P, F])
                et = self.sb(c, "et", [P, 2, TB, D])
                V = self.sb(c, "V", [P, 2, TB, F])
                idx = self.sb(c, "idx", [P, 2, TB], i32)
                cb = self.sb(c, "cb", [P, TB])
                cbm = self.sb(c, "cbm", [P, TB])
                eT = self.sb(c, "eT", [D, 2, 4 * P])
                zT = self.sb(c, "zT", [MID + 1, 4, 4 * P])
                hT = self.sb(c, "hT", [MID + 1, 4, 4 * P])
                pT = [self.ps(c, "pT", [D, 4 * P]) for _ in range(2)]
                p1 = [self.ps(c, "p1", [MID + 1, 4 * P]) for _ in range(2)]
                p2 = self.ps(c, "p2", [P, TB, F])
                self.first_rows(x_d, self.key0_i[:, 0:1], car)
                with ExitStack() as cc:
                    s_m, s_l = self.sem(cc, "s_m"), self.sem(cc, "s_l")
                    block = cc.enter_context(nc.Block())

                    @block.vector
                    def _(v):
                        nc.vector.memset(w1[:], 0.0)
                        nc.vector.memset(b1[:], 1.0)
                        nc.vector.memset(tail[:], -BIG)
                        v.drain().then_inc(s_m, 1)

                    @block.sync
                    def _(sp):
                        sp.wait_ge(s_m, 1)
                        sp.dma_start(w1[:, 0:MID], a["L2_gnn_W1"]).then_inc(s_l, 16)
                        with nc.allow_non_contiguous_dma(reason="one value per partition"):
                            sp.dma_start(b1[0:MID, :], a["L2_gnn_b1"].rearrange("(n o) -> n o", o=1)).then_inc(s_l, 16)
                        sp.dma_start(w2[0:MID, :], a["L2_gnn_W2"]).then_inc(s_l, 16)
                        sp.dma_start(w2[MID:MID + 1, :], a["L2_gnn_b2"].rearrange("(o n) -> o n", o=1)).then_inc(s_l, 16)
                        sp.wait_ge(s_l, 64)
                s_g = [self.sem(c, "s_g") for _ in range(2)]
                s_ld = [self.sem(c, "s_ld") for _ in range(2)]
                s_st = [self.sem(c, "s_st") for _ in range(2)]
                names = ("s_i", "s_f", "s_T", "s_c", "s_1", "s_h", "s_2", "s_y", "s_v", "s_free", "s_z", "tick")
                s_i, s_f, s_T, s_c, s_1, s_h, s_2, s_y, s_v, s_free, s_z, tick = (self.sem(c, n) for n in names)
                block = c.enter_context(nc.Block())
                NQ = TB // 4

                @block.sync
                def _(sp):
                    def load(i, h):
                        at = bass.ds((i * 2 + h) * TB, TB)
                        sp.dma_start(et[:, h, :, F:2 * F], z[:, at, :]).then_inc(s_ld[h], 16)
                        sp.dma_start(et[:, h, :, 2 * F:D], dsv[:, at, 2:2 + ATTR]).then_inc(s_ld[h], 16)

                    def store(i, h):
                        hold(sp, s_v, i * 2 + h + 1, tick)
                        sp.dma_start(sv[:, bass.ds((i * 2 + h) * TB, TB), :], V[:, h]).then_inc(s_st[h], 16)
                    for h in range(2):
                        sp.sem_inc(s_free, 1)
                        load(0, h)
                    with sp.Fori(0, LAST) as i:
                        for h in range(2):
                            hold(sp, s_T, (i * 2 + h) * NQ + NQ, tick)
                            load(i + 1, h)
                            store(i, h)
                            hold(sp, s_st[h], i * 16 + 16, s_free)
                    for h in range(2):
                        store(LAST, h)
                    for h in range(2):
                        sp.wait_ge(s_st[h], 16 * NIT)

                @block.gpsimd
                def _(pool):
                    with pool.Fori(0, NIT) as i:
                        for h in range(2):
                            hold(pool, s_i, i * 2 + h + 1, tick)
                            for t in range(TB):
                                nc.gpsimd.indirect_dma_start(et[:, h, t, 0:F], None, x_d[:, :],
                                                             bass.IndirectOffsetOnAxis(idx[:, h, t:t + 1], 0)).then_inc(s_g[h], 16)

                @block.vector
                def _(v):
                    PART = F // NQ

                    def carry_on(i, h, q):
                        if q == 0:
                            nc.vector.tensor_copy(cb[:], d["cont"][:, bass.ds((i * 2 + h) * TB, TB)])
                            hold(v, s_ld[h], (i + 1) * 32, tick)
                            v.drain()
                        for k in range(q * PART, (q + 1) * PART):
                            nc.vector.tensor_tensor_scan(et[:, h, :, F + k], cb[:], et[:, h, :, F + k], car[:, k:k + 1], ALU.mult, ALU.add)
                        if q == NQ - 1:
                            v.drain()
                            nc.vector.tensor_copy(car[:], et[:, h, TB - 1, F:2 * F]).then_inc(s_f, 1)

                    def maxima(i, h, q):
                        if q == 0:
                            nc.vector.tensor_copy(cbm[:], d["contm"][:, bass.ds((i * 2 + h) * TB, TB)])
                            hold(v, s_y, i * 2 + h + 1, tick)
                            nc.vector.scalar_tensor_tensor(V[:, h], V[:, h], 0.01, V[:, h], ALU.mult, ALU.max)
                            v.drain()
                        for k in range(q * PART, (q + 1) * PART):
                            nc.vector.tensor_tensor_scan(V[:, h, :, k], cbm[:], V[:, h, :, k], tail[:, k:k + 1], ALU.min, ALU.max)
                        if q == NQ - 1:
                            v.drain()
                            nc.vector.tensor_copy(tail[:], V[:, h, TB - 1, :]).then_inc(s_v, 1)
                            v.drain()

                    def hidden(i, h, q):
                        hold(v, s_z, (i * 2 + h) * NQ + q + 1, tick)
                        nc.vector.scalar_tensor_tensor(hT[:, q % 4, :], zT[:, q % 4, :], 0.01, zT[:, q % 4, :],
                                                       ALU.mult, ALU.max).then_inc(s_h, 1)

                    def round_(i, first=False, last=False):
                        for q in range(NQ):
                            hidden(i, 0, q)
                            carry_on(i, 1, q)
                            if not first:
                                maxima(i - 1, 1, q)
                        for q in range(NQ):
                            hidden(i, 1, q)
                            if not last:
                                carry_on(i + 1, 0, q)
                            maxima(i, 0, q)

                    for q in range(NQ):
                        carry_on(0, 0, q)
                    round_(0, first=True)
                    with v.Fori(1, LAST) as i:
                        round_(i)
                    round_(LAST, last=True)
                    for q in range(NQ):
                        maxima(LAST, 1, q)

                @block.tensor
                def _(pe):
                    with pe.Fori(0, NIT) as i:
                        for h in range(2):
                            hold(pe, s_f, i * 2 + h + 1, tick)
                            hold(pe, s_g[h], (i + 1) * (16 * TB), tick)
                            n = (i * 2 + h) * NQ
                            for q in range(NQ + 3):
                                if q < NQ:
                                    for k in range(4):
                                        mm = nc.tensor.transpose(pT[q % 2][:, k * P:(k + 1) * P], et[:, h, 4 * q + k, :], self.ident[:])
                                    mm.then_inc(s_T, 1)
                                if 1 <= q <= NQ:
                                    hold(pe, s_c, n + q, tick)
                                    if q >= 3:
                                        hold(pe, s_z, n + q - 2, tick)
                                    nc.tensor.matmul(p1[(q - 1) % 2][:], w1[:], eT[:, (q - 1) % 2, :], start=True, stop=True).then_inc(s_1, 1)
                                if q >= 3:
                                    hold(pe, s_h, n + q - 2, tick)
                                    for k in range(4):
                                        mm = nc.tensor.matmul(p2[:, 4 * (q - 3) + k, :], hT[:, (q - 3) % 4, k * P:(k + 1) * P], w2[:],
                                                              start=True, stop=True)
                            mm.then_inc(s_2, 1)
                            hold(pe, s_y, i * 2 + h + 1, tick)

                @block.scalar
                def _(act):
                    def indices(i, h):
                        nc.scalar.copy(idx[:, h, :], self.src_i[:, bass.ds((i * 2 + h) * TB, TB)]).then_inc(s_i, 1)
                    for h in range(2):
                        indices(0, h)
                    with act.Fori(0, NIT) as i:
                        for h in range(2):
                            n = (i * 2 + h) * NQ
                            for q in range(NQ + 1):
                                if q < NQ:
                                    hold(act, s_T, n + q + 1, tick)
                                    nc.scalar.copy(eT[:, q % 2, :], pT[q % 2][:]).then_inc(s_c, 1)
                                if q == NQ - 1:
                                    indices(i + 1, h)
                                if q >= 1:
                                    hold(act, s_1, n + q, tick)
                                    nc.scalar.activation(zT[:, (q - 1) % 4, :], p1[(q - 1) % 2][:], ACT.Identity,
                                                         bias=b1[0:MID + 1, 0:1]).then_inc(s_z, 1)
                            hold(act, s_2, i * 2 + h + 1, tick)
                            hold(act, s_free, i * 2 + h + 1, tick)
                            for k in range(2):
                                o = slice(k * TB // 2, (k + 1) * TB // 2)
                                last = nc.scalar.copy(V[:, h, o, :], p2[:, o, :])
                            last.then_inc(s_y, 1)
            self.join(d, tail, F, self.s_2, True)
            with ExitStack() as c:
                y = self.sb(c, "y", [P, NJ, F])
                self.fetch(self.s_2, last_d, y)
                with ExitStack() as cc:
                    block = cc.enter_context(nc.Block())

                    @block.vector
                    def _(v):
                        nc.vector.tensor_tensor(y[:], y[:], self.x[:], ALU.max)
                        v.drain()
                        nc.vector.tensor_tensor(y[:], y[:], self.x[:], ALU.add)
                self.norm(y)

    def finish(self):
        nc = self.nc
        with ExitStack() as c:
            y = self.sb(c, "y", [P, NJ, F])
            with ExitStack() as cc:
                block = cc.enter_context(nc.Block())

                @block.vector
                def _(v):
                    nc.vector.tensor_tensor(y[:], self.x[:], self.edge_sum[:], ALU.add)
            self.norm(y)
            s_o = self.sem(c, "s_o")
            block = c.enter_context(nc.Block())

            @block.sync
            def _(sp):
                for lo, hi in SPLITS:
                    sp.dma_start(self.out.rearrange("(p j) f -> p j f", j=NJ)[lo:hi], self.x[lo:hi]).then_inc(s_o, 16)
                sp.wait_ge(s_o, 32)

    def program(self):
        with ExitStack() as top:
            self.top = top
            self.setup(top)
            self.edge_sum = self.sb(top, "edge_sum", [P, NJ, F])
            first_d, last_d = self.sb(top, "first_d", [P, NJ], i32), self.sb(top, "last_d", [P, NJ], i32)
            self.sort_by_dst(first_d, last_d)
            d = self.dst_order(top)
            self.attention(d, first_d)
            self.gin(d, last_d)
            self.edge_mlp(d, first_d, last_d)
            self.finish()


_INS = ["x", "src", "dst", "edge_attr_16", "edge_attr_32", "L0_gnn_w", "L0_gnn_fc_w", "L0_gnn_fc_b", "L0_gnn_bias",
        "L1_gnn_W1", "L1_gnn_b1", "L1_gnn_W2", "L1_gnn_b2", "L1_gnn_W3", "L1_gnn_b3", "L1_gnn_W4", "L1_gnn_b4",
        "L2_gnn_W1", "L2_gnn_b1", "L2_gnn_W2", "L2_gnn_b2"]


def kernel(**inputs):
    import numpy as _np
    import concourse.bacc as _bacc
    from concourse.bass_utils import run_bass_kernel_spmd as _run

    nc = _bacc.Bacc("TRN2", target_bir_lowering=False, num_devices=1)
    arrays, args = {}, {}
    for name in _INS:
        a = _np.ascontiguousarray(inputs[name])
        arrays[f"in_{name}_dram"] = a
        args[name] = nc.dram_tensor(f"in_{name}_dram", a.shape, mybir.dt.from_np(a.dtype), kind="ExternalInput").ap()
    out = nc.dram_tensor("out_0_dram", (N, F), f32, kind="ExternalOutput").ap()
    Build(nc, args, out).program()
    r = _run(nc, [arrays], core_ids=[0])
    return r.results[0]["out_0_dram"]
```
